# Optimizing a Trainium2 kernel written in Bass

```python
import numpy as np
import jax
import jax.numpy as jnp

def _softmax(x, axis=-1):
    return jax.nn.softmax(x, axis=axis)

def _gelu(x):
    return jax.nn.gelu(x, approximate=True)

def _silu(x):
    return jax.nn.silu(x)

def _sigmoid(x):
    return jax.nn.sigmoid(x)

def _layernorm(x, axis=-1, eps=1e-05):
    m = jnp.mean(x, axis=axis, keepdims=True)
    v = jnp.var(x, axis=axis, keepdims=True)
    return (x - m) / jnp.sqrt(v + eps)

def _scatter_add(tgt, idx, src, axis=0):
    return tgt.at[idx].add(src)

def _segment_sum(src, seg, n):
    return jax.ops.segment_sum(src, seg, n)
kernel_name = 'mk_vit_tower_d2_tok_img768_r4_bca52f'

def setup_inputs(seed: int=0):
    np.random.seed(seed)
    _w = jnp.asarray

    def _rec_inputs():
        import jax
        import jax.numpy as jnp
        _rk = jax.random.key(seed)
        x = -0.000356955 + 1 * jax.random.normal(jax.random.fold_in(_rk, 1), (64, 3, 96, 96), jnp.float32)
        return x
    x = _rec_inputs()

    def _L0_tok_setup():
        import jax, jax.numpy as jnp
        import numpy as np
        PATCH = 16
        POS_GRID = (14, 14)
        EMBED = 192
        C_IN = 3

        def _nearest_resize(x, out_h, out_w):
            _, _, h, w = x.shape
            ih = jnp.arange(out_h) * h // out_h
            iw = jnp.arange(out_w) * w // out_w
            return x[:, :, ih][:, :, :, iw]
        key = jax.random.key(seed)
        k1, k2, k3, k4, k5 = jax.random.split(key, 5)
        im = jax.random.normal(k1, (128, C_IN, 224, 224), dtype=jnp.float32)
        W = jax.random.normal(k2, (C_IN * PATCH * PATCH, EMBED), dtype=jnp.float32) * 0.02
        b = jax.random.normal(k3, (EMBED,), dtype=jnp.float32) * 0.02
        positions = jax.random.normal(k4, (1, EMBED, POS_GRID[0], POS_GRID[1]), dtype=jnp.float32)
        cls_embedding = jax.random.normal(k5, (1, 1, EMBED), dtype=jnp.float32)
        return {'im': im, 'W': W, 'b': b, 'positions': positions, 'cls_embedding': cls_embedding}
    _L0_tok_all = _L0_tok_setup()
    _L0_tok_in = {k: v for k, v in _L0_tok_all.items() if k in ('W', 'b', 'positions', 'cls_embedding')}
    del _L0_tok_all

    def _L0_attn_setup():
        import jax, jax.numpy as jnp
        import numpy as np
        import math
        D_MODEL, N_HEADS, D_HEAD, SEQ, BATCH = (192, 12, 64, 256, 8)
        INIT_RANGE = 0.02
        key = jax.random.key(seed)
        ks = jax.random.split(key, 6)
        x = jax.random.normal(ks[0], (BATCH, SEQ, D_MODEL), dtype=jnp.float32)
        W_Q = jax.random.normal(ks[1], (N_HEADS, D_MODEL, D_HEAD), dtype=jnp.float32) * INIT_RANGE
        W_K = jax.random.normal(ks[2], (N_HEADS, D_MODEL, D_HEAD), dtype=jnp.float32) * INIT_RANGE
        W_V = jax.random.normal(ks[3], (N_HEADS, D_MODEL, D_HEAD), dtype=jnp.float32) * INIT_RANGE
        W_O = jax.random.normal(ks[4], (N_HEADS, D_HEAD, D_MODEL), dtype=jnp.float32) * INIT_RANGE
        b_Q = jnp.zeros((N_HEADS, D_HEAD), dtype=jnp.float32)
        b_K = jnp.zeros((N_HEADS, D_HEAD), dtype=jnp.float32)
        b_V = jnp.zeros((N_HEADS, D_HEAD), dtype=jnp.float32)
        b_O = jnp.zeros((D_MODEL,), dtype=jnp.float32)
        return {'normalized_resid_pre': x, 'W_Q': W_Q, 'b_Q': b_Q, 'W_K': W_K, 'b_K': b_K, 'W_V': W_V, 'b_V': b_V, 'W_O': W_O, 'b_O': b_O}
    _L0_attn_all = _L0_attn_setup()
    _L0_attn_in = {k: v for k, v in _L0_attn_all.items() if k in ('W_Q', 'b_Q', 'W_K', 'b_K', 'W_V', 'b_V', 'W_O', 'b_O')}
    del _L0_attn_all

    def _L0_ffn_setup():
        import jax, jax.numpy as jnp
        import numpy as np
        EPS_NORM = 1e-06
        EPS_Q = 1e-05

        def rmsnorm(x, g):
            return x * jax.lax.rsqrt(jnp.mean(x * x, axis=-1, keepdims=True) + EPS_NORM) * g

        def activation_quant(x):
            scale = 127.0 / jnp.maximum(jnp.max(jnp.abs(x), axis=-1, keepdims=True), EPS_Q)
            return jnp.clip(jnp.round(x * scale), -128, 127) / scale

        def weight_quant(w):
            scale = 1.0 / jnp.maximum(jnp.mean(jnp.abs(w)), EPS_Q)
            return jnp.clip(jnp.round(w * scale), -1, 1) / scale

        def bitlinear(x, w, g):
            x_norm = rmsnorm(x, g)
            x_q = x_norm + jax.lax.stop_gradient(activation_quant(x_norm) - x_norm)
            w_q = w + jax.lax.stop_gradient(weight_quant(w) - w)
            return jnp.einsum('bsd,od->bso', x_q, w_q)
        key = jax.random.key(seed)
        k1, k2, k3 = jax.random.split(key, 3)
        B, S, D, H = (8, 1024, 192, 512)
        x = jax.random.normal(k1, (B, S, D), dtype=jnp.float32)
        w_in = jax.random.normal(k2, (2 * H, D), dtype=jnp.float32) * 0.002
        w_out = jax.random.normal(k3, (D, H), dtype=jnp.float32) * 0.002
        g_in = jnp.ones((D,), dtype=jnp.float32)
        g_out = jnp.ones((H,), dtype=jnp.float32)
        return {'x': x, 'w_in': w_in, 'g_in': g_in, 'w_out': w_out, 'g_out': g_out}
    _L0_ffn_all = _L0_ffn_setup()
    _L0_ffn_in = {k: v for k, v in _L0_ffn_all.items() if k in ('w_in', 'g_in', 'w_out', 'g_out')}
    del _L0_ffn_all

    def _L1_attn_setup():
        import math
        import jax, jax.numpy as jnp
        import numpy as np
        D_MODEL = 192
        N_HEAD = 12
        HEAD_DIM = D_MODEL // N_HEAD
        ROPE_BASE = 10000.0
        EPS = 1e-06

        def rotary_cache(seq_len, head_dim, base=ROPE_BASE):
            half = head_dim // 2
            freq = 1.0 / base ** (jnp.arange(half, dtype=jnp.float32) / half)
            freqs = jnp.arange(seq_len, dtype=jnp.float32)[:, None] * freq[None, :]
            return (jnp.cos(freqs), jnp.sin(freqs))

        def apply_rope(x, cos, sin):
            cos = cos.astype(x.dtype)
            sin = sin.astype(x.dtype)
            x1 = x[..., ::2]
            x2 = x[..., 1::2]
            out = jnp.stack((x1 * cos - x2 * sin, x1 * sin + x2 * cos), axis=-1)
            return out.reshape(x.shape)
        key = jax.random.key(seed)
        kx, kq, kk, kv, kp = jax.random.split(key, 5)
        B, S, D = (2, 512, D_MODEL)
        x = jax.random.normal(kx, (B, S, D), dtype=jnp.float32)
        scale = 0.02
        Wq = jax.random.normal(kq, (D, D), dtype=jnp.float32) * scale
        Wk = jax.random.normal(kk, (D, D), dtype=jnp.float32) * scale
        Wv = jax.random.normal(kv, (D, D), dtype=jnp.float32) * scale
        Wproj = jax.random.normal(kp, (D, D), dtype=jnp.float32) * scale
        return {'x': x, 'Wq': Wq, 'Wk': Wk, 'Wv': Wv, 'Wproj': Wproj}
    _L1_attn_all = _L1_attn_setup()
    _L1_attn_in = {k: v for k, v in _L1_attn_all.items() if k in ('Wq', 'Wk', 'Wv', 'Wproj')}
    del _L1_attn_all

    def _L1_ffn_setup():
        import jax, jax.numpy as jnp
        import numpy as np
        DIM = 192
        FF = 768
        E = 8
        K = 2
        H = 12
        HD = DIM // H
        LN_EPS = 1e-05

        def _layernorm(x, g, b):
            m = jnp.mean(x, axis=-1, keepdims=True)
            v = jnp.var(x, axis=-1, keepdims=True)
            return (x - m) * jax.lax.rsqrt(v + LN_EPS) * g + b

        def _attention(x, Wqkv, Wproj):
            B, T, D = x.shape
            qkv = (x @ Wqkv).reshape(B, T, 3, H, HD)
            q, k, v = (qkv[:, :, 0], qkv[:, :, 1], qkv[:, :, 2])
            scores = jnp.einsum('bqhd,bkhd->bhqk', q, k) * jnp.float32(HD) ** (-0.5)
            attn = jax.nn.softmax(scores, axis=-1)
            out = jnp.einsum('bhqk,bkhd->bqhd', attn, v).reshape(B, T, D)
            return out @ Wproj

        def _moe(x, Wrouter, W1, W2):
            B, T, D = x.shape
            xf = x.reshape(-1, D)
            N = xf.shape[0]
            logits = xf @ Wrouter
            topk_w, topk_idx = jax.lax.top_k(logits, K)
            topk_w = jax.nn.softmax(topk_w.astype(jnp.float32), axis=-1).astype(x.dtype)
            we = jnp.zeros((N, E), x.dtype).at[jnp.arange(N)[:, None], topk_idx].add(topk_w)

            def body(acc, expert):
                W1e, W2e, we_e = expert
                h = jax.nn.gelu(xf @ W1e, approximate=False)
                return (acc + we_e[:, None] * (h @ W2e), None)
            out, _ = jax.lax.scan(body, jnp.zeros_like(xf), (W1, W2, we.T))
            return out.reshape(B, T, D)
        key = jax.random.key(seed)
        ks = jax.random.split(key, 7)
        B, T = (4, 256)
        init = lambda k, shape, fan: jax.random.normal(k, shape, jnp.float32) * fan ** (-0.5)
        return {'x': jax.random.normal(ks[0], (B, T, DIM), jnp.float32), 'Wqkv': init(ks[1], (DIM, 3 * DIM), DIM), 'Wproj': init(ks[2], (DIM, DIM), DIM), 'Wrouter': init(ks[3], (DIM, E), DIM), 'W1': init(ks[4], (E, DIM, FF), DIM), 'W2': init(ks[5], (E, FF, DIM), FF), 'ln1_g': jnp.ones((DIM,), jnp.float32), 'ln1_b': jnp.zeros((DIM,), jnp.float32), 'ln2_g': jnp.ones((DIM,), jnp.float32), 'ln2_b': jnp.zeros((DIM,), jnp.float32)}
    _L1_ffn_all = _L1_ffn_setup()
    _L1_ffn_in = {k: v for k, v in _L1_ffn_all.items() if k in ('Wqkv', 'Wproj', 'Wrouter', 'W1', 'W2', 'ln1_g', 'ln1_b', 'ln2_g', 'ln2_b')}
    del _L1_ffn_all
    return {'x': x, 'L0_tok_W': _L0_tok_in['W'], 'L0_tok_b': _L0_tok_in['b'], 'L0_tok_positions': _L0_tok_in['positions'], 'L0_tok_cls_embedding': _L0_tok_in['cls_embedding'], 'L0_attn_W_Q': _L0_attn_in['W_Q'], 'L0_attn_b_Q': _L0_attn_in['b_Q'], 'L0_attn_W_K': _L0_attn_in['W_K'], 'L0_attn_b_K': _L0_attn_in['b_K'], 'L0_attn_W_V': _L0_attn_in['W_V'], 'L0_attn_b_V': _L0_attn_in['b_V'], 'L0_attn_W_O': _L0_attn_in['W_O'], 'L0_attn_b_O': _L0_attn_in['b_O'], 'L0_ffn_w_in': _L0_ffn_in['w_in'], 'L0_ffn_g_in': _L0_ffn_in['g_in'], 'L0_ffn_w_out': _L0_ffn_in['w_out'], 'L0_ffn_g_out': _L0_ffn_in['g_out'], 'L1_attn_Wq': _L1_attn_in['Wq'], 'L1_attn_Wk': _L1_attn_in['Wk'], 'L1_attn_Wv': _L1_attn_in['Wv'], 'L1_attn_Wproj': _L1_attn_in['Wproj'], 'L1_ffn_Wqkv': _L1_ffn_in['Wqkv'], 'L1_ffn_Wproj': _L1_ffn_in['Wproj'], 'L1_ffn_Wrouter': _L1_ffn_in['Wrouter'], 'L1_ffn_W1': _L1_ffn_in['W1'], 'L1_ffn_W2': _L1_ffn_in['W2'], 'L1_ffn_ln1_g': _L1_ffn_in['ln1_g'], 'L1_ffn_ln1_b': _L1_ffn_in['ln1_b'], 'L1_ffn_ln2_g': _L1_ffn_in['ln2_g'], 'L1_ffn_ln2_b': _L1_ffn_in['ln2_b']}

def reference(x, L0_tok_W, L0_tok_b, L0_tok_positions, L0_tok_cls_embedding, L0_attn_W_Q, L0_attn_b_Q, L0_attn_W_K, L0_attn_b_K, L0_attn_W_V, L0_attn_b_V, L0_attn_W_O, L0_attn_b_O, L0_ffn_w_in, L0_ffn_g_in, L0_ffn_w_out, L0_ffn_g_out, L1_attn_Wq, L1_attn_Wk, L1_attn_Wv, L1_attn_Wproj, L1_ffn_Wqkv, L1_ffn_Wproj, L1_ffn_Wrouter, L1_ffn_W1, L1_ffn_W2, L1_ffn_ln1_g, L1_ffn_ln1_b, L1_ffn_ln2_g, L1_ffn_ln2_b):
    import jax
    import jax.numpy as jnp

    def _L0_tok_ref(im, W, b, positions, cls_embedding):
        import jax, jax.numpy as jnp
        import numpy as np
        PATCH = 16
        POS_GRID = (14, 14)
        EMBED = 192
        C_IN = 3

        def _nearest_resize(x, out_h, out_w):
            _, _, h, w = x.shape
            ih = jnp.arange(out_h) * h // out_h
            iw = jnp.arange(out_w) * w // out_w
            return x[:, :, ih][:, :, :, iw]
        B, C, H, Wd = im.shape
        ph, pw = (PATCH, PATCH)
        gh, gw = (H // ph, Wd // pw)
        patches = im.reshape(B, C, gh, ph, gw, pw)
        patches = patches.transpose(0, 2, 4, 1, 3, 5).reshape(B, gh * gw, C * ph * pw)
        pos = _nearest_resize(positions, gh, gw)
        pos = pos.reshape(1, EMBED, gh * gw).transpose(0, 2, 1)
        embeds = jnp.einsum('bsp,pd->bsd', patches, W) + b + pos
        cls_tok = jnp.broadcast_to(cls_embedding, (B, 1, EMBED))
        return jnp.concatenate((cls_tok, embeds), axis=1)

    def _L0_attn_ref(normalized_resid_pre, W_Q, b_Q, W_K, b_K, W_V, b_V, W_O, b_O):
        import jax, jax.numpy as jnp
        import numpy as np
        import math
        D_MODEL, N_HEADS, D_HEAD, SEQ, BATCH = (192, 12, 64, 256, 8)
        INIT_RANGE = 0.02
        x = normalized_resid_pre
        q = jnp.einsum('bsd,hde->bshe', x, W_Q) + b_Q
        k = jnp.einsum('bsd,hde->bshe', x, W_K) + b_K
        v = jnp.einsum('bsd,hde->bshe', x, W_V) + b_V
        scores = jnp.einsum('bqhe,bkhe->bhqk', q, k) / math.sqrt(D_HEAD)
        s = x.shape[1]
        causal = jnp.tril(jnp.ones((s, s), dtype=bool))
        scores = jnp.where(causal[None, None], scores, -jnp.inf)
        pattern = jax.nn.softmax(scores, axis=-1)
        pattern = jnp.where(jnp.isnan(pattern), 0.0, pattern)
        z = jnp.einsum('bhqk,bkhe->bqhe', pattern, v)
        attn_out = jnp.einsum('bqhe,hed->bqd', z, W_O) + b_O
        return attn_out

    def _L0_ffn_ref(x, w_in, g_in, w_out, g_out):
        import jax, jax.numpy as jnp
        import numpy as np
        EPS_NORM = 1e-06
        EPS_Q = 1e-05

        def rmsnorm(x, g):
            return x * jax.lax.rsqrt(jnp.mean(x * x, axis=-1, keepdims=True) + EPS_NORM) * g

        def activation_quant(x):
            scale = 127.0 / jnp.maximum(jnp.max(jnp.abs(x), axis=-1, keepdims=True), EPS_Q)
            return jnp.clip(jnp.round(x * scale), -128, 127) / scale

        def weight_quant(w):
            scale = 1.0 / jnp.maximum(jnp.mean(jnp.abs(w)), EPS_Q)
            return jnp.clip(jnp.round(w * scale), -1, 1) / scale

        def bitlinear(x, w, g):
            x_norm = rmsnorm(x, g)
            x_q = x_norm + jax.lax.stop_gradient(activation_quant(x_norm) - x_norm)
            w_q = w + jax.lax.stop_gradient(weight_quant(w) - w)
            return jnp.einsum('bsd,od->bso', x_q, w_q)
        h = bitlinear(x, w_in, g_in)
        up, gate = jnp.split(h, 2, axis=-1)
        y = jax.nn.silu(gate) * up
        return bitlinear(y, w_out, g_out)

    def _L1_attn_ref(x, Wq, Wk, Wv, Wproj):
        import math
        import jax, jax.numpy as jnp
        import numpy as np
        D_MODEL = 192
        N_HEAD = 12
        HEAD_DIM = D_MODEL // N_HEAD
        ROPE_BASE = 10000.0
        EPS = 1e-06

        def rotary_cache(seq_len, head_dim, base=ROPE_BASE):
            half = head_dim // 2
            freq = 1.0 / base ** (jnp.arange(half, dtype=jnp.float32) / half)
            freqs = jnp.arange(seq_len, dtype=jnp.float32)[:, None] * freq[None, :]
            return (jnp.cos(freqs), jnp.sin(freqs))

        def apply_rope(x, cos, sin):
            cos = cos.astype(x.dtype)
            sin = sin.astype(x.dtype)
            x1 = x[..., ::2]
            x2 = x[..., 1::2]
            out = jnp.stack((x1 * cos - x2 * sin, x1 * sin + x2 * cos), axis=-1)
            return out.reshape(x.shape)
        B, S, D = x.shape
        H, hd = (N_HEAD, HEAD_DIM)

        def heads(W):
            return (x @ W.T).reshape(B, S, H, hd).transpose(0, 2, 1, 3)
        q, k, v = (heads(Wq), heads(Wk), heads(Wv))
        cos, sin = rotary_cache(S, hd)
        cos = cos[None, None]
        sin = sin[None, None]
        q = apply_rope(q, cos, sin)
        k = apply_rope(k, cos, sin)
        scores = jnp.einsum('bhsd,bhtd->bhst', q.astype(jnp.float32), k.astype(jnp.float32))
        scores = scores / math.sqrt(hd)
        weights = jax.lax.erf(scores) + 1.0
        mask = jnp.tril(jnp.ones((S, S), dtype=bool))[None, None]
        weights = jnp.where(mask, weights, 0.0)
        denom = jnp.maximum(weights.sum(axis=-1, keepdims=True), EPS)
        y = jnp.einsum('bhst,bhtd->bhsd', weights, v.astype(jnp.float32)) / denom
        y = y.astype(v.dtype)
        y = y.transpose(0, 2, 1, 3).reshape(B, S, D)
        return y @ Wproj.T

    def _L1_ffn_ref(x, Wqkv, Wproj, Wrouter, W1, W2, ln1_g, ln1_b, ln2_g, ln2_b):
        import jax, jax.numpy as jnp
        import numpy as np
        DIM = 192
        FF = 768
        E = 8
        K = 2
        H = 12
        HD = DIM // H
        LN_EPS = 1e-05

        def _layernorm(x, g, b):
            m = jnp.mean(x, axis=-1, keepdims=True)
            v = jnp.var(x, axis=-1, keepdims=True)
            return (x - m) * jax.lax.rsqrt(v + LN_EPS) * g + b

        def _attention(x, Wqkv, Wproj):
            B, T, D = x.shape
            qkv = (x @ Wqkv).reshape(B, T, 3, H, HD)
            q, k, v = (qkv[:, :, 0], qkv[:, :, 1], qkv[:, :, 2])
            scores = jnp.einsum('bqhd,bkhd->bhqk', q, k) * jnp.float32(HD) ** (-0.5)
            attn = jax.nn.softmax(scores, axis=-1)
            out = jnp.einsum('bhqk,bkhd->bqhd', attn, v).reshape(B, T, D)
            return out @ Wproj

        def _moe(x, Wrouter, W1, W2):
            B, T, D = x.shape
            xf = x.reshape(-1, D)
            N = xf.shape[0]
            logits = xf @ Wrouter
            topk_w, topk_idx = jax.lax.top_k(logits, K)
            topk_w = jax.nn.softmax(topk_w.astype(jnp.float32), axis=-1).astype(x.dtype)
            we = jnp.zeros((N, E), x.dtype).at[jnp.arange(N)[:, None], topk_idx].add(topk_w)

            def body(acc, expert):
                W1e, W2e, we_e = expert
                h = jax.nn.gelu(xf @ W1e, approximate=False)
                return (acc + we_e[:, None] * (h @ W2e), None)
            out, _ = jax.lax.scan(body, jnp.zeros_like(xf), (W1, W2, we.T))
            return out.reshape(B, T, D)
        x = x + _attention(_layernorm(x, ln1_g, ln1_b), Wqkv, Wproj)
        x = x + _moe(_layernorm(x, ln2_g, ln2_b), Wrouter, W1, W2)
        return x
    h = _L0_tok_ref(x, L0_tok_W, L0_tok_b, L0_tok_positions, L0_tok_cls_embedding)
    h = h + _L0_attn_ref(_layernorm(h, axis=-1), L0_attn_W_Q, L0_attn_b_Q, L0_attn_W_K, L0_attn_b_K, L0_attn_W_V, L0_attn_b_V, L0_attn_W_O, L0_attn_b_O)
    h = h + _L0_ffn_ref(_layernorm(h, axis=-1), L0_ffn_w_in, L0_ffn_g_in, L0_ffn_w_out, L0_ffn_g_out)
    h = h + _L1_attn_ref(_layernorm(h, axis=-1), L1_attn_Wq, L1_attn_Wk, L1_attn_Wv, L1_attn_Wproj)
    h = h + _L1_ffn_ref(_layernorm(h, axis=-1), L1_ffn_Wqkv, L1_ffn_Wproj, L1_ffn_Wrouter, L1_ffn_W1, L1_ffn_W2, L1_ffn_ln1_g, L1_ffn_ln1_b, L1_ffn_ln2_g, L1_ffn_ln2_b)
    return h

_drawn_inputs = setup_inputs


def setup_inputs(seed=0):
    import zlib

    import numpy as np

    out = dict(_drawn_inputs(seed))
    spreads = {'L0_attn_b_Q': (0.0, 0.8),
     'L0_attn_b_K': (0.0, 0.8),
     'L0_attn_b_V': (0.0, 0.1),
     'L0_attn_b_O': (0.0, 0.1),
     'L0_ffn_g_in': (1.0, 0.6),
     'L0_ffn_g_out': (1.0, 0.6),
     'L1_ffn_ln1_g': (1.0, 0.2),
     'L1_ffn_ln1_b': (0.0, 0.1),
     'L1_ffn_ln2_g': (1.0, 0.2),
     'L1_ffn_ln2_b': (0.0, 0.1)}
    factors = {'L0_attn_W_Q': 8.0,
     'L0_attn_W_K': 7.341,
     'L0_ffn_w_in': 4.375,
     'L0_ffn_w_out': 4.652,
     'L1_attn_Wq': 8.0,
     'L1_attn_Wk': 8.0}
    for name, (base, spread) in spreads.items():
        noise = np.random.default_rng([zlib.crc32(name.encode()), seed]).standard_normal(out[name].shape)
        drawn = base * np.exp(spread * noise) if base else spread * noise
        out[name] = jnp.asarray(drawn.astype(out[name].dtype))
    for name, factor in factors.items():
        out[name] = (out[name] * factor).astype(out[name].dtype)
    return out
```

```python
import numpy as np
import concourse.bass as bass
from concourse import mybir
from contextlib import ExitStack

F32 = mybir.dt.float32
F32R = mybir.dt.float32r
BF16 = mybir.dt.bfloat16
U32 = mybir.dt.uint32
ALU = mybir.AluOpType
ACT = mybir.ActivationFunctionType
AX = mybir.AxisListType
RADD = bass.bass_isa.ReduceOp.add

B, C_IN, IMG, PATCH = 64, 3, 96, 16
GRID = IMG // PATCH
S = GRID * GRID + 1
D = 192
K0 = 128
IPT = 3
R = IPT * S
TILES = 22
TILES_ALL = 24
PAIRS = TILES // 2
R2 = 2 * R
GI = 18
GROUPS = 4
GT = GI // IPT
GROWS = GI * GRID
NK = C_IN * 2
PW = PATCH * IMG
NH = 12
HD = 64
HE = 16
HF = 512
E, FF = 8, 768
FM = FF // 128
NQ = NH * S
BIG = -1.0e30
TINY = 1.0e-20
MAGIC = 12582912.0
MK = 72
M_CAUSAL = 32
M_IMAGE = M_CAUSAL + S
W34 = 3 * 128 + 6 * 128 + D
W4 = 3 * 128 + 3 * 128 + D
WCOLS = W34 + W4
WSTEP = 210
WPAD = PAIRS * WSTEP
E_CHUNK = 4


def build_program(nc, t):
    ctx = ExitStack()
    with ctx:
        def sem(name):
            return ctx.enter_context(nc.semaphore(name))

        cursor = [16512]

        def put(name, shape, dt, at=None):
            where = cursor if at is None else at
            size = 4 if dt in (F32, F32R, U32) else 2
            n = size
            for d in shape[1:]:
                n *= d
            got = nc.alloc_sbuf_tensor_at(name, shape, dt, offset=where[0])
            where[0] += (n + 31) // 32 * 32
            assert where[0] <= 229344, (name, where[0])
            return got

        ps = ctx.enter_context(nc.psum_tensor("ps", [128, 8, 512], F32))

        h = put("h", [R, TILES_ALL, D], F32)
        ident = put("ident", [128, 128], F32)
        identb = put("identb", [128, 128], BF16)
        halfneg = put("halfneg", [R, 2], F32)
        eps_ln = put("eps_ln", [R, 2], F32)
        eps_rms = put("eps_rms", [R, 2], F32)
        after_stats = put("after_stats", [1, 1], F32)
        key_rows = put("key_rows", [MK, R], F32R)
        query_rows = put("query_rows", [MK, 2, R], F32R)
        key_cols = put("key_cols", [MK, 4 * R], F32R)
        shift = [put(f"shift{s}", [MK, NH * R], F32R) for s in range(2)]
        sel12 = put("sel12", [NH, NH * R], F32)
        posb = put("posb", [R, D], F32)
        bo_t = put("bo_t", [R, D], F32)
        bqk = put("bqk", [128, 12], F32)
        bv_t = put("bv_t", [R, NH * HD], F32)
        stats = put("stats", [R, 2, 6], F32)
        mv = put("mv", [R, 2, 2], F32)
        vare = put("vare", [R, 2], F32)
        rstd = put("rstd", [R, 2], F32)
        yn = put("yn", [R, 2, D], F32)
        yn2 = put("yn2", [R, 2, D], F32)
        xs = put("xs", [R, 2, 2 * D], F32R)
        nmx = put("nmx", [R, 2, NH], F32)
        nmT = put("nmT", [NH, 2, R], F32)
        rden = put("rden", [R, 2, NH], F32)
        xT = put("xT", [128, 3, R2], F32R)
        wq_in = put("wq_in", [128, 2, 2 * HF], BF16)
        wq_out = put("wq_out", [128, 4, D], BF16)
        g_in = put("g_in", [R, D], F32)
        g_out = put("g_out", [R, HF], F32)
        wsum = put("wsum", [128, 2], F32)
        wall = put("wall", [128, 2], F32)
        wmean = put("wmean", [128, 2], F32)
        wmean2 = put("wmean2", [128, 2], F32)
        wrec = put("wrec", [128, 2], F32)
        w127 = put("w127", [128, 2], F32)
        magic = put("magic", [R, 1], F32)
        ss, rq, rms, amax, amaxc, arec, qscale, dscale = (
            [put(f"{n}{k}", [R, 2], F32) for k in range(2)]
            for n in ("ss", "rq", "rms", "amax", "amaxc", "arec", "qscale", "dscale"))
        region_a = [cursor[0]]
        a0 = region_a[0]
        wh1 = put("wh1", [128, 2, 3 * NH * HD], F32R, region_a)
        wl1 = put("wl1", [128, 2, 3 * NH * HD], F32R, region_a)
        region_b = [region_a[0]]
        wh3 = put("wh3", [128, 2, WPAD], F32R, region_b)
        wl3 = put("wl3", [128, 2, WPAD], F32R, region_b)
        work0 = region_b[0]

        w = [work0]
        X = [put(f"X{p}", [128, C_IN * PW], F32, w) for p in range(2)]
        PT = [put(f"PT{p}", [128, NK, GI * S], F32, w) for p in range(2)]
        wtok = put("wtok", [128, NK, D], F32, w)
        w = [a0 + (region_b[0] - region_b[0])]
        w = [region_a[0]]
        stage1 = put("stage1", [128, 2, 2304], F32, w)
        mask_in = put("mask_in", [MK, R + 2 * R + 4 * R], F32, w)
        shift_in = put("shift_in", [MK, 2, R], F32, w)
        win_in = put("win_in", [128, 2, 2 * HF], F32, w)
        wout_in = put("wout_in", [128, 4, D], F32, w)
        assert w[0] <= work0, (w[0], work0)
        w = [work0]
        Qz = put("Qz", [128, 2, NH, R], F32, w)
        KT = put("KT", [128, 6, R2], F32, w)
        V = put("V", [R, 2, NH, HD + 1], F32, w)
        Pt = put("Pt", [R, 2, NH * R], F32, w)
        O = put("O", [R, 2, NH * HD], F32, w)
        OT = put("OT", [128, 2, 6, R], F32, w)
        wo1 = put("wo1", [128, 6, D], F32, w)
        wst3 = put("wst3", [128, 2, WPAD], F32, w)

        w = [work0]
        xn = put("xn", [R, 2, D], F32, w)
        t1 = put("t1", [R, 2, D], F32, w)
        q1 = put("q1", [R, 2, 2 * 128], BF16, w)
        q1T = put("q1T", [128, 2, 2, R + 1], BF16, w)
        sg = put("sg", [R, 2, HF], F32, w)
        z = put("z", [R, 2, HF], F32, w)
        zn = put("zn", [R, 2, HF], F32, w)
        t2 = put("t2", [R, 2, HF], F32, w)
        q2 = put("q2", [R, 2, HF], BF16, w)
        q2T = put("q2T", [128, 2, 4, R + 1], BF16, w)
        junk1 = put("junk1", [R, 2, D], F32, w)
        junk2 = put("junk2", [R, 2, HF], F32, w)
        psb = ps[:, :, :].bitcast(BF16)
        w = [a0]
        rope_q = put("rope_q", [128, 4, R], F32, w)
        rope_k = put("rope_k", [128, 2, R2], F32, w)
        causal = put("causal", [R, R], F32, w)
        image = put("image", [R, IPT], F32, w)
        quarter = put("quarter", [128, 4], F32, w)
        free_in = put("free_in", [MK, R], F32, w)
        proj = put("proj", [128, 2, 2, D], F32, w)
        gains = put("gains", [R, 4, D], F32, w)
        router_in = put("router_in", [128, 2, E], F32, w)
        router_h = put("router_h", [128, 2, E], F32R, w)
        router_l = put("router_l", [128, 2, E], F32R, w)
        lanes = put("lanes", [R, E], F32, w)
        logits = put("logits", [R, 2, E], F32, w)
        top8 = put("top8", [R, 2, 8], F32, w)
        at8 = put("at8", [R, 2, 8], U32, w)
        top = put("top", [R, 2, TILES], F32, w)
        top_at = put("top_at", [R, 2, TILES], F32, w)
        pr = put("pr", [R, 4, TILES], F32, w)
        share = put("share", [R, 2, E, TILES], F32, w)
        we = put("we", [R, E, TILES], F32, w)
        est1 = put("est1", [128, 2 * FF], F32, w)
        est2 = put("est2", [128, FM * D], F32, w)
        assert w[0] <= region_a[0]
        w = [work0]
        Qz1 = put("Qz1", [128, 2, NH, R], F32, w)
        KT1 = put("KT1", [128, 3, R2], F32, w)
        V1 = put("V1", [R, 2, NH, HE + 1], F32, w)
        Pt1 = put("Pt1", [R, 2, NH * R], F32, w)
        den = put("den", [R, 2, NH], F32, w)
        O1 = put("O1", [R, 2, 256], F32, w)
        OT1 = put("OT1", [128, 2, 2, R], F32, w)
        x1 = put("x1", [R, TILES_ALL, D], F32, list(w))
        kc = put("kc", [128, 3, R2], F32, w)
        ks = put("ks", [128, 3, R2], F32, w)
        own = put("own", [R, 2, NQ], F32, w)
        rown = put("rown", [R, 2, NQ], F32, w)
        gel = put("gel", [R, 2, NQ], F32, w)
        wt1 = put("wt1", [R, 2, NQ], F32, w)
        eh1, el1, eh2, el2 = [None] * 2, [None] * 2, [None] * 2, [None] * 2

        def expert_weights(q):
            eh1[q] = put(f"eh1{q}", [128, 2, FF], F32R, w)
            el1[q] = put(f"el1{q}", [128, 2, FF], F32R, w)
            eh2[q] = put(f"eh2{q}", [128, FM, D], F32R, w)
            el2[q] = put(f"el2{q}", [128, FM, D], F32R, w)

        expert_weights(0)
        w = [work0]
        expert_weights(1)
        graw = put("graw", [128, 2, 4 * R], F32, w)
        gh = put("gh", [128, FM, 4 * R], F32R, w)
        w2_ = [region_a[0]]
        xTm = put("xTm", [128, 3, TILES * R], F32R, w2_)
        gl_at = w2_
        gl = put("gl", [128, FM, 4 * R], F32R, w)

        x_in = [sem(f"x_in{p}") for p in range(2)]; ident_in = sem("ident_in"); wtok_in = sem("wtok_in"); const_in = sem("const_in"); w1_in = sem("w1_in")
        w3_in = sem("w3_in"); wo1_in = sem("wo1_in"); pos_in = sem("pos_in")
        cleared = sem("cleared")
        consts_ready = sem("consts_ready"); w1_hi = sem("w1_hi"); w1_ready = sem("w1_ready")
        w3_hi = sem("w3_hi")
        w3_ready = sem("w3_ready")
        pt_done = sem("pt_done"); pt_copied = sem("pt_copied"); tok_done = sem("tok_done"); tok_h = sem("tok_h")
        out_done = sem("out_done")

        def signals(stage, names):
            return {n: sem(f"{stage}_{n}") for n in names.split()}

        def counted(shared, before, own=None):
            got = {}
            for n, s in {**shared, **(own or {})}.items():
                got[n] = s
                got[n + " before"] = before.get(n, 0)
            return got

        ln = signals("ln", "stats mv vare rstd y scaled affine hi xs tr")
        STEPS = PAIRS + 1

        def norm_stage(norms, splits, affines):
            return counted(ln, {"stats": 2 * STEPS * norms, "mv": 2 * STEPS * norms, "vare": STEPS * norms,
                                "rstd": STEPS * norms, "y": 2 * STEPS * norms, "scaled": STEPS * affines,
                                "affine": STEPS * affines, "hi": STEPS * splits, "xs": STEPS * splits,
                                "tr": TILES * splits})

        L1, L2, L3, L4, L5 = (norm_stage(*n) for n in ((0, 0, 0), (1, 1, 0), (2, 1, 0), (3, 2, 0), (5, 3, 1)))
        tr_copied_dve = sem("tr_copied_dve"); tr_copied_act = sem("tr_copied_act")

        def split5(hi, lo, a, b):
            return ((1, hi[:, 0, a:b]), (0, hi[:, 0, a:b]), (1, lo[:, 0, a:b]), (2, hi[:, 1, a:b]), (2, lo[:, 1, a:b]))

        def ln_vector(dve, L, call, src=h, dst=None, count=None):
            n = call if count is None else count
            for s in range(2):
                nc.vector.bn_stats(stats[:, s, :], src[:, 2 * call + s, :]).then_inc(L["stats"], 1)
            dve.wait_ge(L["stats"], L["stats before"] + 2 * n + 2)
            nc.vector.memset(after_stats[0:1, :], 0.0)
            for s in range(2):
                nc.vector.bn_aggr(mv[:, s, :], stats[:, s, :]).then_inc(L["mv"], 1)
            dve.wait_ge(L["rstd"], L["rstd before"] + n + 1)
            for s in range(2):
                out = yn[:, s, :] if dst is None else dst[:, 2 * call + s, :]
                nc.vector.tensor_scalar(out, src[:, 2 * call + s, :], mv[:, s, 0:1], rstd[:, s:s + 1],
                                        ALU.subtract, ALU.mult).then_inc(L["y"], 1)

        def split_vector(dve, L, call, src):
            dve.wait_ge(L["tr"], L["tr before"] + 2 * call)
            nc.vector.tensor_copy(xs[:, :, K0:K0 + D], src[:, :, :]).then_inc(L["hi"], 1)
            dve.wait_ge(L["hi"], L["hi before"] + call + 1)
            nc.vector.tensor_tensor(xs[:, :, 0:K0], src[:, :, 0:K0], xs[:, :, K0:2 * K0].bitcast(F32),
                                    ALU.subtract)
            nc.vector.tensor_tensor(xs[:, :, K0 + D:2 * D], src[:, :, K0:D], xs[:, :, 2 * K0:K0 + D].bitcast(F32),
                                    ALU.subtract).then_inc(L["xs"], 1)

        def ln_pool(pool, L, call):
            pool.wait_ge(L["mv"], L["mv before"] + 2 * call + 2)
            nc.gpsimd.tensor_tensor(vare[:, :], mv[:, :, 1], eps_ln[:, :], ALU.add).then_inc(L["vare"], 1)
            pool.wait_ge(L["vare"], L["vare before"] + call + 1)
            nc.gpsimd.tensor_tensor(rstd[:, :], vare[:, :], halfneg[:, :], ALU.pow).then_inc(L["rstd"], 1)

        def affine_pool(pool, L, call, g, b, count=None):
            n = call if count is None else count
            pool.wait_ge(L["y"], L["y before"] + 2 * n + 2)
            pool.wait_ge(L["xs"], L["xs before"] + call)
            nc.gpsimd.tensor_tensor(yn2[:, :, :], yn[:, :, :], g.unsqueeze(1).to_broadcast([R, 2, D]),
                                    ALU.mult).then_inc(L["scaled"], 1)
            pool.wait_ge(L["scaled"], L["scaled before"] + call + 1)
            nc.gpsimd.tensor_tensor(yn2[:, :, :], yn2[:, :, :], b.unsqueeze(1).to_broadcast([R, 2, D]),
                                    ALU.add).then_inc(L["affine"], 1)

        def transposes(L, s, bank):
            x = xs[:, s, :].bitcast(F32)
            for c in range(3):
                tr = nc.tensor.transpose(ps[:, bank, c * R:(c + 1) * R], x[:, c * K0:(c + 1) * K0], ident[0:R, 0:R])
            tr.then_inc(L["tr"], 1)

        chain = sem("chain"); consts_copied = sem("consts_copied"); pos_ready = sem("pos_ready")
        bo_in = sem("bo_in"); qz_clear = sem("qz_clear"); hb_done = sem("hb_done")
        nmT_ready = sem("nmT_ready"); st_done = sem("st_done"); shift_ready = sem("shift_ready")
        o_ready = sem("o_ready"); ot_copied = sem("ot_copied"); q_copied = sem("q_copied"); k_copied = sem("k_copied")
        qk_done = sem("qk_done"); resid_done = sem("resid_done"); v_done = sem("v_done"); v_copied = sem("v_copied")
        s_done = sem("s_done"); nmx_ready = sem("nmx_ready"); mt_done = sem("mt_done"); p_ready = sem("p_ready")
        pv_done = sem("pv_done"); ot_done = sem("ot_done"); op_done = sem("op_done"); rden_ready = sem("rden_ready")
        Q = signals("quant", "in summed all step ready")
        F = signals("ffn0", "clear gain_in ssq1 rq1 rms1 xn amax1 amaxc1 arec1 small1 t1 q1 tr1 q1T up sg z ssq2 rq2 rms2 "
                    "zn amax2 amaxc2 arec2 small2 t2 q2 tr2 q2T down resid")
        both = signals("attn", "tr_dve tr_act q k qz v v_out pv rec o ot ot_out op resid")
        A1 = counted(both, {}, signals("attn1", "const_in clear ks kt s own rown gel wt pt den"))
        A2 = counted(both, {"tr_dve": PAIRS, "tr_act": PAIRS, "q": 3 * PAIRS, "k": 3 * PAIRS, "qz": 3 * PAIRS,
                            **{n: TILES for n in "v v_out pv rec o ot ot_out op resid".split()}},
                     signals("attn2", "copied kt s nmx mt nmT shift st p"))
        RT = signals("router", "streams hi split tr_dve tr_act xm1 xm2 logits raw top at kept k2 ex share")
        EX = signals("experts", "in1 in2 hi lo half gelu gh gl down acc")
        block = ctx.enter_context(nc.Block())

        @block.sync
        def _(sp):
            def load_group(g):
                n = min(GROWS, B * GRID - g * GROWS)
                sp.dma_start(X[g % 2][0:n, :], t["x"][g * GROWS:g * GROWS + n, :]).then_inc(x_in[g % 2], 16)

            load_group(0)
            sp.dma_start(ident[:, :], t["ident"]).then_inc(ident_in, 16)
            sp.dma_start(wtok[:, :, :], t["wtok"]).then_inc(wtok_in, 16)
            sp.dma_start(stage1[:, :, :], t["w1"]).then_inc(w1_in, 16)
            load_group(1)
            sp.dma_start(win_in[:, :, :], t["win"]).then_inc(Q["in"], 16)
            sp.dma_start(wout_in[:, :, :], t["wout"]).then_inc(Q["in"], 16)
            sp.dma_start(mask_in[:, :], t["masks"]).then_inc(const_in, 16)
            sp.dma_start(shift_in[:, :, :], t["shift"]).then_inc(const_in, 16)
            sp.dma_start(sel12[:, :], t["sel12"]).then_inc(const_in, 16)
            for g in range(2, GROUPS):
                sp.wait_ge(pt_done, 12 * (g - 1))
                load_group(g)
            sp.wait_ge(tok_done, GROUPS * GT)
            sp.wait_ge(pt_done, GROUPS * 12)
            sp.dma_start(wo1[:, :, :], t["wo1"]).then_inc(wo1_in, 16)
            sp.dma_start(wst3[:, :, :], t["w3"]).then_inc(w3_in, 16)
            sp.wait_ge(w3_in, 16)
            sp.wait_ge(resid_done, TILES)
            for name, dst in (("rope_q", rope_q), ("rope_k", rope_k), ("causal", causal), ("image", image),
                              ("quarter", quarter), ("free", free_in), ("proj", proj), ("gains", gains),
                              ("router", router_in), ("lanes", lanes)):
                if name == "gains":
                    sp.dma_start(dst[:, :, :], t[name].to_broadcast([R, 4, D])).then_inc(A1["const_in"], 16)
                else:
                    sp.dma_start(dst[tuple(slice(None) for _ in dst.shape)], t[name]).then_inc(A1["const_in"], 16)
            for e in range(E):
                if e:
                    sp.wait_ge(EX["lo"], 12 * e)
                sp.dma_start(est1[:, :], t["moe1"][e]).then_inc(EX["in1"], 16)
                sp.dma_start(est2[:, :], t["moe2"][e]).then_inc(EX["in2"], 16)
            rows = t["out"].rearrange("b s d -> (b s) d")
            for c in range(6):
                sp.wait_ge(EX["acc"], TILES * (E - 1) + min(4 * c + 4, TILES))
                t0, t1 = 4 * c, min(4 * c + 4, B // IPT)
                sp.dma_start(rows[t0 * R:t1 * R, :].rearrange("(t r) d -> r t d", r=R), h[:, t0:t1, :]
                             ).then_inc(out_done, 16)
            rest = B * S - (B // IPT) * R
            sp.dma_start(rows[B * S - rest:B * S, :], h[0:rest, TILES - 1, :]).then_inc(out_done, 16)
            sp.wait_ge(out_done, 16 * 7)

        @block.gpsimd
        def _(pool):
            nc.gpsimd.dma_start(posb[:, :], t["pos"]).then_inc(pos_in, 16)
            nc.gpsimd.memset(bo_t[:, :], 0.0).then_inc(cleared, 1)
            for p in range(2):
                cls = PT[p][:, :, :].rearrange("p k (b s) -> p k b s", s=S)[:, :, :, 0]
                nc.gpsimd.memset(cls, 0.0).then_inc(cleared, 1)
            nc.gpsimd.memset(halfneg[:, :], -0.5).then_inc(cleared, 1)
            nc.gpsimd.memset(eps_ln[:, :], 1e-5).then_inc(cleared, 1)
            nc.gpsimd.memset(eps_rms[:, :], 1e-6).then_inc(cleared, 1)
            pool.wait_ge(cleared, 1)
            for i in range(IPT):
                nc.gpsimd.dma_start(bo_t[i * S + 1:(i + 1) * S, :],
                                    t["tok_b"].to_broadcast([S - 1, D])).then_inc(pos_in, 16)
            nc.gpsimd.dma_start(bv_t[:, :], t["b_v"].to_broadcast([R, NH * HD])).then_inc(pos_in, 16)
            nc.gpsimd.dma_start(bqk[:, :], t["b_qk"]).then_inc(pos_in, 16)
            nc.gpsimd.dma_start(g_in[:, :], t["g_in"].to_broadcast([R, D])).then_inc(F["gain_in"], 16)
            nc.gpsimd.dma_start(g_out[:, :], t["g_out"].to_broadcast([R, HF])).then_inc(F["gain_in"], 16)
            nc.gpsimd.memset(magic[:, :], MAGIC).then_inc(F["clear"], 1)
            pool.wait_ge(Q["summed"], 2)
            nc.gpsimd.partition_all_reduce(wall[:, :], wsum[:, :], 128, RADD).then_inc(Q["all"], 1)
            pool.wait_ge(pos_ready, 1)
            nc.gpsimd.dma_start(bo_t[:, :], t["b_o"].to_broadcast([R, D])).then_inc(bo_in, 16)
            pool.wait_ge(tok_done, GROUPS * GT)
            nc.gpsimd.memset(Qz[:, :, :, :].rearrange("p s n r -> p (s n r)"), 0.0).then_inc(qz_clear, 1)
            nc.gpsimd.memset(V[:, :, :, HD:HD + 1], 1.0).then_inc(qz_clear, 1)
            ln_pool(pool, L1, 0)
            pool.wait_ge(bo_in, 16)
            with pool.Fori(0, PAIRS) as i:
                pool.wait_ge(L1["xs"], L1["xs before"] + i + 1)
                for s in range(2):
                    nc.gpsimd.tensor_tensor(h[:, 2 * i + s, :], h[:, 2 * i + s, :], bo_t[:, :],
                                            ALU.add).then_inc(hb_done, 1)
                for s in range(2):
                    pool.wait_ge(nmT_ready, 2 * i + s + 1)
                    pool.wait_ge(st_done, 6 * i)
                    nc.gpsimd.tensor_tensor(shift[s][0:NH, :].rearrange("p (n r) -> p n r", n=NH),
                                            nmT[:, s, :].unsqueeze(1).to_broadcast([NH, NH, R]),
                                            sel12[:, :].rearrange("p (n r) -> p n r", n=NH),
                                            ALU.mult).then_inc(shift_ready, 1)
                ln_pool(pool, L1, i + 1)
            pool.wait_ge(resid_done, TILES)
            nc.gpsimd.memset(q1[:, :, D:2 * 128], 0.0).then_inc(F["clear"], 1)

            def root(k, call):
                pool.wait_ge(F[f"ssq{k + 1}"], 2 * call + 2)
                nc.gpsimd.tensor_tensor(rq[k][:, :], ss[k][:, :], eps_rms[:, :], ALU.add).then_inc(F[f"rq{k + 1}"], 1)
                pool.wait_ge(F[f"rq{k + 1}"], call + 1)
                nc.gpsimd.tensor_tensor(rms[k][:, :], rq[k][:, :], halfneg[:, :], ALU.pow
                                        ).then_inc(F[f"rms{k + 1}"], 1)

            ln_pool(pool, L2, 0)
            root(0, 0)
            with pool.Fori(0, PAIRS) as i:
                ln_pool(pool, L2, i + 1)
                root(1, i)
                root(0, i + 1)

            pool.wait_ge(F["resid"], TILES)
            nc.gpsimd.memset(V1[:, :, :, HE:HE + 1], 1.0).then_inc(A1["clear"], 1)
            nc.gpsimd.memset(O1[:, :, D:256], 0.0).then_inc(A1["clear"], 1)
            pool.wait_ge(A1["const_in"], A1["const_in before"] + 160)
            ln_pool(pool, L3, 0)
            with pool.Fori(0, PAIRS) as i:
                pool.wait_ge(A1["ks"], A1["ks before"] + 6 * i + 6)
                pool.wait_ge(A1["s"], A1["s before"] + 6 * i)
                nc.gpsimd.tensor_tensor(KT1[:, :, :], kc[:, :, :], ks[:, :, :], ALU.add).then_inc(A1["kt"], 1)
                ln_pool(pool, L3, i + 1)
                for s in range(2):
                    pool.wait_ge(A1["wt"], A1["wt before"] + 2 * i + s + 1)
                    pool.wait_ge(A1["pv"], A1["pv before"] + 2 * i)
                    nc.gpsimd.tensor_tensor(
                        Pt1[:, s, :].rearrange("p (n i q) -> p n i q", n=NH, i=IPT),
                        wt1[:, s, :].rearrange("p (n q) -> p n q", n=NH).unsqueeze(2).to_broadcast([R, NH, IPT, S]),
                        causal[:, :].rearrange("p (i q) -> p i q", i=IPT).unsqueeze(1).to_broadcast([R, NH, IPT, S]),
                        ALU.mult).then_inc(A1["pt"], 1)
            pool.wait_ge(A1["resid"], A1["resid before"] + TILES)
            ln_pool(pool, L4, 0)
            ln_pool(pool, L4, 1)
            affine_pool(pool, L4, 0, gains[:, 0, :], gains[:, 1, :], count=1)
            pool.wait_ge(A2["copied"], A2["copied before"] + 2)
            with pool.Fori(0, PAIRS) as i:
                ln_pool(pool, L4, 2 * i + 2)
                ln_pool(pool, L4, 2 * i + 3)
                for s in range(2):
                    pool.wait_ge(A2["nmT"], A2["nmT before"] + 2 * i + s + 1)
                    pool.wait_ge(A2["st"], A2["st before"] + 6 * i)
                    nc.gpsimd.tensor_tensor(shift[s][0:NH, :].rearrange("p (n r) -> p n r", n=NH),
                                            nmT[:, s, :].unsqueeze(1).to_broadcast([NH, NH, R]),
                                            sel12[:, :].rearrange("p (n r) -> p n r", n=NH),
                                            ALU.mult).then_inc(A2["shift"], 1)
                affine_pool(pool, L4, i + 1, gains[:, 0, :], gains[:, 1, :], count=2 * i + 3)
            pool.wait_ge(A2["resid"], A2["resid before"] + TILES)
            ln_pool(pool, L5, 0)
            affine_pool(pool, L5, 0, gains[:, 2, :], gains[:, 3, :])
            with pool.Fori(0, PAIRS) as i:
                ln_pool(pool, L5, i + 1)
                affine_pool(pool, L5, i + 1, gains[:, 2, :], gains[:, 3, :])
                nc.gpsimd.tensor_tensor(h[:, bass.ds(2 * i, 2), :], h[:, bass.ds(2 * i, 2), :],
                                        x1[:, bass.ds(2 * i, 2), :], ALU.add).then_inc(RT["streams"], 1)

        @block.tensor
        def _(pe):
            pe.wait_ge(ident_in, 16)
            with pe.Fori(0, GROUPS // 2) as i:
                for p in range(2):
                    pe.wait_ge(x_in[p], 16 * i + 16)
                    src = X[p][:, :].rearrange("p (k g w) -> p k g w", k=NK, g=GRID)
                    for k in range(NK):
                        for half in range(2):
                            n = 12 * p + 2 * k + half
                            if n < 4:
                                pe.wait_ge(pt_copied, 24 * i)
                            else:
                                pe.wait_ge(pt_copied, 24 * i + n - 3)
                            for j in range(3):
                                gw = 3 * half + j
                                tr = nc.tensor.transpose(ps[:, n % 4, j * GROWS:(j + 1) * GROWS],
                                                         src[0:GROWS, k, gw, :],
                                                         ident[0:GROWS, 0:GROWS])
                            tr.then_inc(pt_done, 1)
                pe.wait_ge(wtok_in, 16)
                for p in range(2):
                    pe.wait_ge(pt_copied, 24 * i + 12 * p + 12)
                    for m in range(GT):
                        n = GT * p + m
                        if n < 4:
                            pe.wait_ge(tok_h, 12 * i)
                        else:
                            pe.wait_ge(tok_h, 12 * i + n - 3)
                        for k in range(NK):
                            mm = nc.tensor.matmul(ps[0:R, 4 + n % 4, 0:D], PT[p][:, k, m * R:(m + 1) * R],
                                                  wtok[:, k, :], start=(k == 0), stop=(k == NK - 1))
                        mm.then_inc(tok_done, 1)
            pe.wait_ge(tok_h, TILES_ALL)
            pe.wait_ge(w1_ready, 1)
            pe.wait_ge(consts_ready, 1)
            pe.wait_ge(const_in, 48)
            pe.wait_ge(qz_clear, 2)
            pe.wait_ge(wo1_in, 16)
            with pe.Fori(0, PAIRS) as i:
                pe.wait_ge(L1["xs"], L1["xs before"] + i + 1)
                pe.wait_ge(o_ready, 2 * i)
                transposes(L1, 0, 0)
                transposes(L1, 1, 1)
                pe.wait_ge(tr_copied_dve, i + 1)
                pe.wait_ge(tr_copied_act, i + 1)
                for g in range(3):
                    for side in range(2):
                        if g == 0:
                            pe.wait_ge(ot_copied, 4 * i)
                        elif side == 0:
                            pe.wait_ge(q_copied, 12 * i + 4 * g)
                        else:
                            pe.wait_ge(k_copied, 6 * i + 2 * g)
                        for j in range(2):
                            m = 6 * side + 2 * g + j
                            for n, (x, wt) in enumerate(split5(wh1, wl1, 128 * m, 128 * m + 128)):
                                mm = nc.tensor.matmul(ps[:, 2 + side, j * R2:(j + 1) * R2], wt, xT[:, x, :],
                                                      start=(n == 0), stop=(n == 4))
                        mm.then_inc(qk_done, 1)
                pe.wait_ge(resid_done, 2 * i)
                pe.wait_ge(ot_copied, 4 * i)
                for s in range(2):
                    for b in range(2):
                        c = 2 * NH * HD + 384 * b
                        for n, (x, wt) in enumerate(split5(wh1, wl1, c, c + 384)):
                            mm = nc.tensor.matmul(ps[0:R, 4 + 2 * s + b, 0:384], xT[:, x, s * R:(s + 1) * R], wt,
                                                  start=(n == 0), stop=(n == 4))
                        mm.then_inc(v_done, 1)
                pe.wait_ge(q_copied, 12 * i + 12)
                pe.wait_ge(k_copied, 6 * i + 6)
                for s in range(2):
                    if s == 1:
                        pe.wait_ge(v_copied, 4 * i + 2)
                    for b in range(3):
                        bank = 3 * s + b
                        nc.tensor.matmul(ps[0:R, bank, 0:4 * R], query_rows[:, 0, :], key_cols[:, :],
                                         start=True, stop=False)
                        for j in range(4):
                            n = 4 * b + j
                            mm = nc.tensor.matmul(ps[0:R, bank, j * R:(j + 1) * R], Qz[:, s, n, :],
                                                  KT[:, n // 2, s * R:(s + 1) * R], start=False, stop=(j == 3))
                    mm.then_inc(s_done, 1)
                for s in range(2):
                    pe.wait_ge(nmx_ready, 2 * i + s + 1)
                    if s == 0:
                        pe.wait_ge(v_copied, 4 * i + 4)
                    else:
                        pe.wait_ge(nmT_ready, 2 * i + 1)
                    nc.tensor.transpose(ps[0:NH, 6, 0:R], nmx[:, s, :], ident[0:R, 0:R]).then_inc(mt_done, 1)
                    pe.wait_ge(shift_ready, 2 * i + s + 1)
                    for b in range(3):
                        bank = 3 * s + b
                        nc.tensor.matmul(ps[0:R, bank, 0:4 * R], key_rows[:, :],
                                         shift[s][:, b * 4 * R:(b + 1) * 4 * R], start=True, stop=False)
                        for j in range(2):
                            n = 4 * b + 2 * j
                            mm = nc.tensor.matmul(ps[0:R, bank, j * R2:(j + 1) * R2], KT[:, n // 2, s * R:(s + 1) * R],
                                                  Qz[:, s, n:n + 2, :].rearrange("p n r -> p (n r)"),
                                                  start=False, stop=(j == 1))
                        mm.then_inc(st_done, 1)
                for s in range(2):
                    pe.wait_ge(p_ready, 6 * i + 3 * s + 3)
                    if s == 0:
                        pe.wait_ge(nmT_ready, 2 * i + 2)
                    for b in range(2):
                        bank = (6 if s == 0 else 0) + b
                        for j in range(6):
                            n = 6 * b + j
                            mm = nc.tensor.matmul(ps[0:R, bank, j * (HD + 1):(j + 1) * (HD + 1)],
                                                  Pt[:, s, n * R:(n + 1) * R], V[:, s, n, :], start=True, stop=True)
                        mm.then_inc(pv_done, 1)
                for s in range(2):
                    pe.wait_ge(o_ready, 2 * i + s + 1)
                    pe.wait_ge(p_ready, 6 * i + 6)
                    for b, (c0, c1) in enumerate(((0, 4), (4, 6))):
                        bank = (2 if s == 0 else 5) + b
                        for c in range(c0, c1):
                            mm = nc.tensor.transpose(ps[:, bank, (c - c0) * R:(c - c0 + 1) * R],
                                                     O[:, s, 128 * c:128 * c + 128], ident[0:R, 0:R])
                        mm.then_inc(ot_done, 1)
                    pe.wait_ge(ot_copied, 4 * i + 2 * s + 2)
                    for c in range(6):
                        mm = nc.tensor.matmul(ps[0:R, 4 + 3 * s, 0:D], OT[:, s, c, :], wo1[:, c, :],
                                              start=(c == 0), stop=(c == 5))
                    mm.then_inc(op_done, 1)

            pe.wait_ge(resid_done, TILES)
            pe.wait_ge(Q["ready"], 2)
            pe.wait_ge(consts_ready, 1)

            def rows_in(call):
                pe.wait_ge(F["q1"], call + 1)
                pe.wait_ge(F["resid"], 2 * call)
                for s in range(2):
                    for k in range(2):
                        tr = nc.tensor.transpose(psb[:, s, k * (R + 1):k * (R + 1) + R], q1[:, s, 128 * k:128 * k + 128],
                                                 identb[0:R, 0:R])
                    tr.then_inc(F["tr1"], 1)

            rows_in(0)
            with pe.Fori(0, PAIRS) as i:
                pe.wait_ge(F["q1T"], 2 * i + 2)
                pe.wait_ge(F["z"], 2 * i)
                for s in range(2):
                    for part in range(2):
                        for k in range(2):
                            mm = nc.tensor.matmul(ps[0:R, 2 + 2 * s + part, :], q1T[:, s, k, 0:R],
                                                  wq_in[:, k, part * HF:(part + 1) * HF], start=(k == 0), stop=(k == 1))
                    mm.then_inc(F["up"], 1)
                pe.wait_ge(F["q2"], i + 1)
                pe.wait_ge(F["q2T"], 2 * i)
                for s in range(2):
                    for k in range(4):
                        tr = nc.tensor.transpose(psb[:, 6 + s, k * (R + 1):k * (R + 1) + R],
                                                 q2[:, s, 128 * k:128 * k + 128], identb[0:R, 0:R])
                    tr.then_inc(F["tr2"], 1)
                pe.wait_ge(F["q1T"], 2 * i + 2)
                for s in range(2):
                    pe.wait_ge(F["q2T"], 2 * i + s + 1)
                    for k in range(4):
                        mm = nc.tensor.matmul(ps[0:R, s, 0:D], q2T[:, s, k, 0:R], wq_out[:, k, :],
                                              start=(k == 0), stop=(k == 3))
                    mm.then_inc(F["down"], 1)
                rows_in(i + 1)

            pe.wait_ge(F["resid"], TILES)
            pe.wait_ge(F["q1T"], 2 * (PAIRS + 1))
            pe.wait_ge(w3_ready, PAIRS)
            pe.wait_ge(A1["const_in"], A1["const_in before"] + 160)
            pe.wait_ge(A1["clear"], A1["clear before"] + 2)

            def project(x, c, bank, o, n_tokens=R2, done=None):
                for n, (k, wt) in enumerate(split5(wh3, wl3, c, c + 128)):
                    mm = nc.tensor.matmul(ps[:, bank, o:o + R2], wt, x[:, k, :], start=(n == 0), stop=(n == 4))
                return mm

            def values(A, c, bank, s):
                for n, (k, wt) in enumerate(split5(wh3, wl3, c, c + D)):
                    mm = nc.tensor.matmul(ps[0:R, bank, 0:D], xT[:, k, s * R:(s + 1) * R], wt,
                                          start=(n == 0), stop=(n == 4))
                mm.then_inc(A["v"], 1)

            def pv_products(A, i, s, bank):
                for n in range(NH):
                    mm = nc.tensor.matmul(ps[0:R, bank, n * (HE + 1):(n + 1) * (HE + 1)], Pt1[:, s, n * R:(n + 1) * R],
                                          V1[:, s, n, :], start=True, stop=True)
                mm.then_inc(A["pv"], 1)

            def project_out(A, i, s, layer):
                pe.wait_ge(A["o"], A["o before"] + 2 * i + s + 1)
                for c in range(2):
                    tr = nc.tensor.transpose(ps[:, 2 * s, c * R:(c + 1) * R], O1[:, s, 128 * c:128 * c + 128],
                                             ident[0:R, 0:R])
                tr.then_inc(A["ot"], 1)
                pe.wait_ge(A["ot_out"], A["ot_out before"] + 2 * i + s + 1)
                for c in range(2):
                    mm = nc.tensor.matmul(ps[0:R, 2 * s + 1, 0:D], OT1[:, s, c, :], proj[:, layer, c, :],
                                          start=(c == 0), stop=(c == 1))
                mm.then_inc(A["op"], 1)

            with pe.Fori(0, PAIRS) as i:
                pe.wait_ge(L3["xs"], L3["xs before"] + i + 1)
                pe.wait_ge(A1["ot_out"], A1["ot_out before"] + 2 * i)
                transposes(L3, 0, 0)
                pe.wait_ge(A1["resid"], A1["resid before"] + 2 * i)
                transposes(L3, 1, 1)
                pe.wait_ge(A1["tr_dve"], A1["tr_dve before"] + i + 1)
                pe.wait_ge(A1["tr_act"], A1["tr_act before"] + i + 1)
                for g in range(3):
                    if g:
                        pe.wait_ge(A1["qz"], A1["qz before"] + 3 * i + g)
                    project(xT, 128 * g, 2, 0).then_inc(A1["q"], 1)
                    if g:
                        pe.wait_ge(A1["ks"], A1["ks before"] + 6 * i + 2 * g)
                    project(xT, 384 + 128 * g, 3, 0)
                    project(xT, 768 + 128 * g, 3, R2).then_inc(A1["k"], 1)
                pe.wait_ge(A1["own"], A1["own before"] + 6 * i)
                for s in range(2):
                    values(A1, W34 - D, 4 + s, s)
                pe.wait_ge(A1["qz"], A1["qz before"] + 3 * i + 3)
                pe.wait_ge(A1["kt"], A1["kt before"] + i + 1)
                for s in range(2):
                    if s == 1:
                        pe.wait_ge(A1["v_out"], A1["v_out before"] + 2 * i + 2)
                    for b in range(3):
                        nc.tensor.matmul(ps[0:R, 3 * s + b, :].rearrange("p (n r) -> p n r", n=4)[:, :, 0:R],
                                         KT1[:, b, s * R:(s + 1) * R], Qz1[:, s, 4 * b:4 * b + 4, :],
                                         start=True, stop=True).then_inc(A1["s"], 1)
                for s in range(2):
                    pe.wait_ge(A1["pt"], A1["pt before"] + 2 * i + s + 1)
                    pe.wait_ge(A1["o"], A1["o before"] + 2 * i)
                    pv_products(A1, i, s, 6 + s)
                for s in range(2):
                    project_out(A1, i, s, 0)
            pe.wait_ge(A1["resid"], A1["resid before"] + TILES)
            pe.wait_ge(A2["copied"], A2["copied before"] + 2)
            with pe.Fori(0, PAIRS) as i:
                pe.wait_ge(L4["xs"], L4["xs before"] + i + 1)
                pe.wait_ge(A2["ot_out"], A2["ot_out before"] + 2 * i)
                transposes(L4, 0, 0)
                pe.wait_ge(A2["resid"], A2["resid before"] + 2 * i)
                transposes(L4, 1, 1)
                pe.wait_ge(A2["tr_dve"], A2["tr_dve before"] + i + 1)
                pe.wait_ge(A2["tr_act"], A2["tr_act before"] + i + 1)
                for g in range(3):
                    if g:
                        pe.wait_ge(A2["qz"], A2["qz before"] + 3 * i + g)
                    project(xT, W34 + 128 * g, 2, 0).then_inc(A2["q"], 1)
                    if g:
                        pe.wait_ge(A2["kt"], A2["kt before"] + 3 * i + g)
                    project(xT, W34 + 384 + 128 * g, 3, 0).then_inc(A2["k"], 1)
                pe.wait_ge(A2["p"], A2["p before"] + 6 * i)
                for s in range(2):
                    values(A2, WCOLS - D, 4 + s, s)
                pe.wait_ge(A2["qz"], A2["qz before"] + 3 * i + 3)
                pe.wait_ge(A2["kt"], A2["kt before"] + 3 * i + 3)
                for s in range(2):
                    if s == 1:
                        pe.wait_ge(A2["v_out"], A2["v_out before"] + 2 * i + 2)
                    for b in range(3):
                        nc.tensor.matmul(ps[0:R, 3 * s + b, 0:4 * R], query_rows[:, 1, :], key_cols[:, :],
                                         start=True, stop=False)
                        for j in range(4):
                            mm = nc.tensor.matmul(ps[0:R, 3 * s + b, j * R:(j + 1) * R], Qz1[:, s, 4 * b + j, :],
                                                  KT1[:, b, s * R:(s + 1) * R], start=False, stop=(j == 3))
                    mm.then_inc(A2["s"], 1)
                for s in range(2):
                    pe.wait_ge(A2["nmx"], A2["nmx before"] + 2 * i + s + 1)
                    if s == 0:
                        pe.wait_ge(A2["o"], A2["o before"] + 2 * i)
                    else:
                        pe.wait_ge(A2["nmT"], A2["nmT before"] + 2 * i + 1)
                    nc.tensor.transpose(ps[0:NH, 6, 0:R], nmx[:, s, :], ident[0:R, 0:R]).then_inc(A2["mt"], 1)
                    pe.wait_ge(A2["shift"], A2["shift before"] + 2 * i + s + 1)
                    for b in range(3):
                        nc.tensor.matmul(ps[0:R, 3 * s + b, 0:4 * R], key_rows[:, :],
                                         shift[s][:, b * 4 * R:(b + 1) * 4 * R], start=True, stop=False)
                        nc.tensor.matmul(ps[0:R, 3 * s + b, 0:4 * R], KT1[:, b, s * R:(s + 1) * R],
                                         Qz1[:, s, 4 * b:4 * b + 4, :].rearrange("p n r -> p (n r)"),
                                         start=False, stop=True).then_inc(A2["st"], 1)
                for s in range(2):
                    pe.wait_ge(A2["p"], A2["p before"] + 6 * i + 3 * s + 3)
                    if s == 0:
                        pe.wait_ge(A2["o"], A2["o before"] + 2 * i)
                    else:
                        pe.wait_ge(A2["nmT"], A2["nmT before"] + 2 * i + 2)
                    pv_products(A2, i, s, 7 - s)
                for s in range(2):
                    project_out(A2, i, s, 1)
            pe.wait_ge(A2["resid"], A2["resid before"] + TILES)
            pe.wait_ge(RT["split"], 1)
            with pe.Fori(0, PAIRS) as i:
                pe.wait_ge(L5["xs"], L5["xs before"] + i + 1)
                pe.wait_ge(RT["xm1"], i)
                pe.wait_ge(RT["xm2"], i)
                transposes(L5, 0, 0)
                transposes(L5, 1, 1)
                pe.wait_ge(RT["tr_dve"], i + 1)
                pe.wait_ge(RT["tr_act"], i + 1)
                pe.wait_ge(RT["raw"], 2 * i)
                for s in range(2):
                    for n, (k, wt) in enumerate(split5(router_h, router_l, 0, E)):
                        mm = nc.tensor.matmul(ps[0:R, 2 + s, 0:E], xT[:, k, s * R:(s + 1) * R], wt,
                                              start=(n == 0), stop=(n == 4))
                    mm.then_inc(RT["logits"], 1)
            pe.wait_ge(RT["raw"], TILES)
            pe.wait_ge(RT["xm1"], PAIRS)
            pe.wait_ge(RT["xm2"], PAIRS)

            def experts_tensor(e, q, c, tiles):
                base = 36 * e + 6 * c
                cols = tiles * R
                at = c * (E_CHUNK * R)
                pe.wait_ge(EX["lo"], 12 * e + 12)
                for step in range(FM + 2):
                    if step < FM:
                        m = step
                        if m < 4:
                            pe.wait_ge(EX["gelu"], base)
                        else:
                            pe.wait_ge(EX["gelu"], base + m - 3)
                        for n, (k, wt) in enumerate(split5(eh1[q], el1[q], 128 * m, 128 * m + 128)):
                            mm = nc.tensor.matmul(ps[:, m % 4, 0:cols], wt, xTm[:, k, bass.ds(at, cols)],
                                                  start=(n == 0), stop=(n == 4))
                        mm.then_inc(EX["half"], 1)
                    if step >= 2:
                        k = step - 2
                        pe.wait_ge(EX["gl"], base + k + 1)
                        if k == 0:
                            pe.wait_ge(EX["acc"], TILES * e + 4 * c)
                        for tt in range(tiles):
                            rows = slice(tt * R, (tt + 1) * R)
                            nc.tensor.matmul(ps[0:R, 4 + tt, 0:D], gh[:, k, rows], eh2[q][:, k, :],
                                             start=(k == 0), stop=False)
                            nc.tensor.matmul(ps[0:R, 4 + tt, 0:D], gh[:, k, rows], el2[q][:, k, :],
                                             start=False, stop=False)
                            mm = nc.tensor.matmul(ps[0:R, 4 + tt, 0:D], gl[:, k, rows], eh2[q][:, k, :],
                                                  start=False, stop=(k == FM - 1))
                            if k == FM - 1:
                                mm.then_inc(EX["down"], 1)

            with pe.Fori(0, E // 2) as pair:
                for q in range(2):
                    with pe.Fori(0, TILES // E_CHUNK) as c:
                        experts_tensor(2 * pair + q, q, c, E_CHUNK)
                    experts_tensor(2 * pair + q, q, TILES // E_CHUNK, TILES % E_CHUNK)

        @block.scalar
        def _(act):
            act.wait_ge(cleared, 3)
            with act.Fori(0, GROUPS // 2) as i:
                for p in range(2):
                    for k in range(NK):
                        for half in range(2):
                            n = 12 * p + 2 * k + half
                            act.wait_ge(pt_done, 24 * i + n + 1)
                            slots = PT[p][:, k, :].rearrange("p (b s) -> p b s", s=S)[:, :, 1:S]
                            slots = slots.rearrange("p b (g w) -> p w b g", w=GRID)
                            nc.scalar.copy(slots[:, 3 * half:3 * half + 3, :, :],
                                           ps[:, n % 4, 0:3 * GROWS].rearrange("p (w b g) -> p w b g", w=3, b=GI)
                                           ).then_inc(pt_copied, 1)
            act.wait_ge(pos_in, 16 * (IPT + 3))
            act.wait_ge(qz_clear, 1)
            with act.Fori(0, PAIRS) as i:
                act.wait_ge(L1["tr"], L1["tr before"] + 2 * i + 2)
                act.wait_ge(v_done, 4 * i)
                nc.scalar.copy(xT[:, :, R:R2], ps[:, 1, 0:3 * R].rearrange("p (c r) -> p c r", c=3)
                               ).then_inc(tr_copied_act, 1)
                for g in range(3):
                    act.wait_ge(qk_done, 6 * i + 2 * g + 1)
                    for j in range(2):
                        for hh in range(2):
                            n = 4 * g + 2 * j + hh
                            rows = slice(64 * hh, 64 * hh + 64)
                            nc.scalar.activation(Qz[rows, :, n, :],
                                                 ps[rows, 2, j * R2:(j + 1) * R2].rearrange("p (s r) -> p s r", s=2),
                                                 ACT.Identity, bias=bqk[rows, n // 2:n // 2 + 1]).then_inc(q_copied, 1)
                for s in range(2):
                    act.wait_ge(pv_done, 4 * i)
                    for b in range(3):
                        act.wait_ge(st_done, 6 * i + 3 * s + b + 1)
                        nc.scalar.activation(Pt[:, s, b * 4 * R:(b + 1) * 4 * R], ps[0:R, 3 * s + b, 0:4 * R],
                                             ACT.Exp, scale=float(HD) ** -0.5).then_inc(p_ready, 1)
                for s in range(2):
                    for b, (c0, c1) in enumerate(((0, 4), (4, 6))):
                        act.wait_ge(ot_done, 4 * i + 2 * s + b + 1)
                        nc.scalar.copy(OT[:, s, c0:c1, :],
                                       ps[:, (2 if s == 0 else 5) + b, 0:(c1 - c0) * R].rearrange(
                                           "p (c r) -> p c r", r=R)).then_inc(ot_copied, 1)

            act.wait_ge(resid_done, TILES)
            act.wait_ge(F["clear"], 1)

            def rows_act(call):
                for s in range(2):
                    act.wait_ge(L2["y"], L2["y before"] + 2 * call + s + 1)
                    act.wait_ge(F["ssq1"], 2 * call)
                    nc.scalar.activation(junk1[:, s, :], yn[:, s, :], ACT.Square, scale=float(D) ** -0.5,
                                         accum_out=ss[0][:, s:s + 1]
                                         ).then_inc(F["ssq1"], 1)

            def rows_round(call):
                act.wait_ge(F["small1"], 2 * call + 2)
                act.wait_ge(F["q1"], call)
                for s in range(2):
                    nc.scalar.activation(t1[:, s, :], xn[:, s, :], ACT.Identity, bias=magic[:, :],
                                         scale=qscale[0][:, s:s + 1]).then_inc(F["t1"], 1)

            def rows_out(call):
                act.wait_ge(F["up"], 2 * call)
                for s in range(2):
                    act.wait_ge(F["tr1"], 2 * call + s + 1)
                    nc.scalar.copy(q1T[:, s, :, 0:R], psb[:, s, 0:2 * (R + 1)].rearrange("p (k r) -> p k r", k=2)[:, :, 0:R]
                                   ).then_inc(F["q1T"], 1)

            rows_act(0)
            rows_round(0)
            rows_out(0)
            with act.Fori(0, PAIRS) as i:
                for s in range(2):
                    act.wait_ge(F["up"], 2 * i + s + 1)
                    act.wait_ge(F["z"], 2 * i)
                    nc.scalar.activation(sg[:, s, :], ps[0:R, 3 + 2 * s, :], ACT.Silu, scale=dscale[0][:, s:s + 1]
                                         ).then_inc(F["sg"], 1)
                rows_act(i + 1)
                for s in range(2):
                    act.wait_ge(F["z"], 2 * i + s + 1)
                    nc.scalar.activation(junk2[:, s, :], z[:, s, :], ACT.Square, scale=float(HF) ** -0.5,
                                         accum_out=ss[1][:, s:s + 1]
                                         ).then_inc(F["ssq2"], 1)
                act.wait_ge(F["small2"], 2 * i + 2)
                act.wait_ge(F["q2"], i)
                for s in range(2):
                    nc.scalar.activation(t2[:, s, :], zn[:, s, :], ACT.Identity, bias=magic[:, :],
                                         scale=qscale[1][:, s:s + 1]).then_inc(F["t2"], 1)
                rows_round(i + 1)
                act.wait_ge(F["down"], 2 * i)
                for s in range(2):
                    act.wait_ge(F["tr2"], 2 * i + s + 1)
                    nc.scalar.copy(q2T[:, s, :, 0:R], psb[:, 6 + s, 0:4 * (R + 1)].rearrange("p (k r) -> p k r", k=4)
                                   [:, :, 0:R]).then_inc(F["q2T"], 1)
                rows_out(i + 1)

            act.wait_ge(F["resid"], TILES)
            act.wait_ge(A1["clear"], A1["clear before"] + 2)

            def transposed_act(L, A, i):
                act.wait_ge(L["tr"], L["tr before"] + 2 * i + 2)
                act.wait_ge(A["v"], A["v before"] + 2 * i)
                nc.scalar.copy(xT[:, :, R:R2], ps[:, 1, 0:3 * R].rearrange("p (c r) -> p c r", c=3)
                               ).then_inc(A["tr_act"], 1)

            def values_act(A, i):
                act.wait_ge(A["pv"], A["pv before"] + 2 * i)
                for s in range(2):
                    act.wait_ge(A["v"], A["v before"] + 2 * i + s + 1)
                    nc.scalar.copy(V1[:, s, :, 0:HE], ps[0:R, 4 + s, 0:D].rearrange("p (n e) -> p n e", n=NH)
                                   ).then_inc(A["v_out"], 1)

            def outputs_act(A, i):
                act.wait_ge(A["op"], A["op before"] + 2 * i)
                for s in range(2):
                    act.wait_ge(A["ot"], A["ot before"] + 2 * i + s + 1)
                    nc.scalar.copy(OT1[:, s, :, :], ps[:, 2 * s, 0:R2].rearrange("p (c r) -> p c r", c=2)
                                   ).then_inc(A["ot_out"], 1)

            with act.Fori(0, PAIRS) as i:
                transposed_act(L3, A1, i)
                values_act(A1, i)
                for s in range(2):
                    act.wait_ge(A1["own"], A1["own before"] + 6 * i + 3 * s + 3)
                    act.wait_ge(A1["wt"], A1["wt before"] + 2 * i)
                    nc.scalar.activation(gel[:, s, :], own[:, s, :], ACT.Gelu, scale=2.0 ** 0.5 * float(HE) ** -0.5
                                         ).then_inc(A1["gel"], 1)
                outputs_act(A1, i)
            act.wait_ge(A1["resid"], A1["resid before"] + TILES)
            with act.Fori(0, PAIRS) as i:
                transposed_act(L4, A2, i)
                act.wait_ge(A2["st"], A2["st before"] + 6 * i)
                for g in range(3):
                    act.wait_ge(A2["k"], A2["k before"] + 3 * i + g + 1)
                    nc.scalar.copy(KT1[:, g, :], ps[:, 3, 0:R2]).then_inc(A2["kt"], 1)
                values_act(A2, i)
                for s in range(2):
                    for b in range(3):
                        act.wait_ge(A2["st"], A2["st before"] + 6 * i + 3 * s + b + 1)
                        nc.scalar.activation(Pt1[:, s, b * 4 * R:(b + 1) * 4 * R], ps[0:R, 3 * s + b, 0:4 * R],
                                             ACT.Exp, scale=float(HE) ** -0.5).then_inc(A2["p"], 1)
                outputs_act(A2, i)
            act.wait_ge(A2["resid"], A2["resid before"] + TILES)
            with act.Fori(0, PAIRS) as i:
                act.wait_ge(L5["tr"], L5["tr before"] + 2 * i + 2)
                act.wait_ge(RT["logits"], 2 * i)
                src = ps[:, 1, 0:3 * R].rearrange("p (c r) -> p c r", c=3)
                nc.scalar.copy(xT[:, :, R:R2], src).then_inc(RT["tr_act"], 1)
                nc.scalar.copy(xTm[:, :, bass.ds(i * R2 + R, R)], src).then_inc(RT["xm2"], 1)
            act.wait_ge(RT["k2"], 1)
            nc.scalar.activation(pr[:, 1, :], pr[:, 0, :], ACT.Exp).then_inc(RT["ex"], 1)
            def experts_scalar(e, c, tiles):
                base = 36 * e + 6 * c
                for m in range(FM):
                    act.wait_ge(EX["half"], base + m + 1)
                    if m < 2:
                        act.wait_ge(EX["gl"], base)
                    else:
                        act.wait_ge(EX["gl"], base + m - 1)
                    nc.scalar.activation(graw[:, m % 2, 0:tiles * R], ps[:, m % 4, 0:tiles * R], ACT.Gelu
                                         ).then_inc(EX["gelu"], 1)

            act.wait_ge(A2["resid"], A2["resid before"] + TILES)
            with act.Fori(0, E) as e:
                with act.Fori(0, TILES // E_CHUNK) as c:
                    experts_scalar(e, c, E_CHUNK)
                experts_scalar(e, TILES // E_CHUNK, TILES % E_CHUNK)

        @block.vector
        def _(dve):
            nc.vector.memset(h[:, TILES:TILES_ALL, :], 0.0).then_inc(chain, 1)
            dve.wait_ge(w1_in, 16)
            nc.vector.tensor_copy(wh1[:, :, :], stage1[:, :, :]).then_inc(w1_hi, 1)
            dve.wait_ge(w1_hi, 1)
            nc.vector.tensor_tensor(wl1[:, :, :], stage1[:, :, :], wh1[:, :, :].bitcast(F32),
                                    ALU.subtract).then_inc(w1_ready, 1)
            dve.wait_ge(Q["in"], 32)
            for n, src in enumerate((win_in, wout_in)):
                nc.vector.tensor_reduce(wsum[:, n:n + 1], src[:, :, :], AX.XY, ALU.add, apply_absolute_value=True
                                        ).then_inc(Q["summed"], 1)
            dve.wait_ge(Q["all"], 1)
            for n, size in enumerate((2 * HF * D, HF * D)):
                nc.vector.tensor_scalar(wmean[:, n:n + 1], wall[:, n:n + 1], 1.0 / size, 1e-5, ALU.mult, ALU.max
                                        ).then_inc(Q["step"], 1)
            dve.wait_ge(Q["step"], 2)
            nc.vector.reciprocal(wrec[:, :], wmean[:, :]).then_inc(Q["step"], 1)
            nc.vector.tensor_scalar(w127[:, :], wmean[:, :], 1.0 / 127.0, None, ALU.mult).then_inc(Q["step"], 1)
            dve.wait_ge(Q["step"], 4)
            for n, src in enumerate((win_in, wout_in)):
                nc.vector.tensor_scalar(src[:, :, :], src[:, :, :], wrec[:, n:n + 1], MAGIC, ALU.mult, ALU.add
                                        ).then_inc(Q["step"], 1)
            dve.wait_ge(Q["step"], 6)
            for n, src in enumerate((win_in, wout_in)):
                nc.vector.tensor_scalar(src[:, :, :], src[:, :, :], MAGIC, 1.0, ALU.subtract, ALU.min
                                        ).then_inc(Q["step"], 1)
            dve.wait_ge(Q["step"], 8)
            for src, dst in ((win_in, wq_in), (wout_in, wq_out)):
                nc.vector.tensor_scalar(dst[:, :, :], src[:, :, :], -1.0, None, ALU.max).then_inc(Q["ready"], 1)
            dve.wait_ge(const_in, 48)
            nc.vector.tensor_copy(identb[:, :], ident[:, :]).then_inc(consts_copied, 1)
            nc.vector.tensor_copy(key_rows[:, :], mask_in[:, 0:R]).then_inc(consts_copied, 1)
            nc.vector.tensor_copy(query_rows[:, :, :], mask_in[:, R:3 * R].rearrange("p (a r) -> p a r", a=2)
                                  ).then_inc(consts_copied, 1)
            nc.vector.tensor_copy(key_cols[:, :], mask_in[:, 3 * R:7 * R]).then_inc(consts_copied, 1)
            for s in range(2):
                nc.vector.tensor_copy(shift[s][:, :].rearrange("p (n r) -> p n r", n=NH),
                                      shift_in[:, 0, :].unsqueeze(1).to_broadcast([MK, NH, R])
                                      ).then_inc(consts_copied, 1)
            dve.wait_ge(consts_copied, 6)
            dve.wait_ge(pos_in, 16 * (IPT + 3))
            nc.vector.tensor_tensor(posb[:, :], posb[:, :], bo_t[:, :], ALU.add).then_inc(pos_ready, 1)
            dve.wait_ge(pos_ready, 1)
            dve.wait_ge(chain, 1)
            with dve.Fori(0, GROUPS // 2) as i:
                for n in range(2 * GT):
                    dve.wait_ge(tok_done, 12 * i + n + 1)
                    nc.vector.tensor_tensor(h[:, 2 * GT * i + n, :], ps[0:R, 4 + n % 4, 0:D], posb[:, :],
                                            ALU.add).then_inc(tok_h, 1)
            nc.vector.memset(mv[0:1, 0, 0:1], 0.0).then_inc(consts_ready, 1)
            dve.wait_ge(consts_ready, 1)
            dve.wait_ge(tok_h, TILES_ALL)
            dve.wait_ge(cleared, 6)
            ln_vector(dve, L1, 0)
            dve.wait_ge(L1["y"], L1["y before"] + 2)
            split_vector(dve, L1, 0, yn)
            dve.wait_ge(w3_in, 16)
            dve.wait_ge(qz_clear, 2)
            with dve.Fori(0, PAIRS) as i:
                dve.wait_ge(L1["tr"], L1["tr before"] + 2 * i + 1)
                dve.wait_ge(v_done, 4 * i)
                nc.vector.tensor_copy(xT[:, :, 0:R], ps[:, 0, 0:3 * R].rearrange("p (c r) -> p c r", c=3)
                                      ).then_inc(tr_copied_dve, 1)
                dve.wait_ge(st_done, 6 * i)
                for g in range(3):
                    dve.wait_ge(qk_done, 6 * i + 2 * g + 2)
                    for j in range(2):
                        m = 2 * g + j
                        nc.vector.tensor_scalar(KT[:, m, :], ps[:, 3, j * R2:(j + 1) * R2], bqk[:, 6 + m:7 + m], None,
                                                ALU.add).then_inc(k_copied, 1)
                for s in range(2):
                    for b in range(2):
                        dve.wait_ge(v_done, 4 * i + 2 * s + b + 1)
                        nc.vector.tensor_tensor(V[:, s, 6 * b:6 * b + 6, 0:HD],
                                                ps[0:R, 4 + 2 * s + b, 0:384].rearrange("p (n e) -> p n e", n=6),
                                                bv_t[:, 384 * b:384 * b + 384].rearrange("p (n e) -> p n e", n=6),
                                                ALU.add).then_inc(v_copied, 1)
                for s in range(2):
                    dve.wait_ge(s_done, 2 * i + s + 1)
                    nc.vector.tensor_reduce(nmx[:, s, :],
                                            ps[0:R, 3 * s:3 * s + 3, 0:4 * R].rearrange("p b (n r) -> p b n r", n=4),
                                            AX.X, ALU.max, negate=True).then_inc(nmx_ready, 1)
                    dve.wait_ge(mt_done, 2 * i + s + 1)
                    nc.vector.tensor_copy(nmT[:, s, :], ps[0:NH, 6, 0:R]).then_inc(nmT_ready, 1)
                cols = bass.ds(i * WSTEP, WSTEP)
                nc.vector.tensor_copy(wh3[:, :, cols], wst3[:, :, cols]).then_inc(w3_hi, 1)
                dve.wait_ge(w3_hi, i + 1)
                nc.vector.tensor_tensor(wl3[:, :, cols], wst3[:, :, cols], wh3[:, :, cols].bitcast(F32),
                                        ALU.subtract).then_inc(w3_ready, 1)
                ln_vector(dve, L1, i + 1)
                dve.wait_ge(L1["y"], L1["y before"] + 2 * i + 4)
                split_vector(dve, L1, i + 1, yn)
                for s in range(2):
                    b0 = 6 if s == 0 else 0
                    heads = ps[0:R, b0:b0 + 2, 0:6 * (HD + 1)].rearrange("p b (n e) -> p b n e", n=6)
                    dve.wait_ge(pv_done, 4 * i + 2 * s + 2)
                    nc.vector.reciprocal(rden[:, s, :].rearrange("p (b n) -> p b n", b=2),
                                         heads[:, :, :, HD]).then_inc(rden_ready, 1)
                    dve.wait_ge(rden_ready, 2 * i + s + 1)
                    nc.vector.tensor_tensor(O[:, s, :].rearrange("p (b n e) -> p b n e", b=2, n=6),
                                            heads[:, :, :, 0:HD],
                                            rden[:, s, :].rearrange("p (b n) -> p b n", b=2).unsqueeze(3)
                                            .to_broadcast([R, 2, 6, HD]), ALU.mult).then_inc(o_ready, 1)
                for s in range(2):
                    dve.wait_ge(hb_done, 2 * i + 2)
                    dve.wait_ge(op_done, 2 * i + s + 1)
                    nc.vector.tensor_tensor(h[:, 2 * i + s, :], ps[0:R, 4 + 3 * s, 0:D], h[:, 2 * i + s, :],
                                            ALU.add).then_inc(resid_done, 1)
            dve.wait_ge(resid_done, TILES)
            dve.wait_ge(F["gain_in"], 32)
            dve.wait_ge(F["clear"], 2)

            def quantise_scale(k, call, rows):
                nc.vector.tensor_reduce(amax[k][:, :], rows, AX.X, ALU.max, apply_absolute_value=True
                                        ).then_inc(F[f"amax{k + 1}"], 1)
                dve.wait_ge(F[f"amax{k + 1}"], call + 1)
                nc.vector.tensor_scalar(amaxc[k][:, :], amax[k][:, :], 1e-5, None, ALU.max).then_inc(F[f"amaxc{k + 1}"], 1)
                dve.wait_ge(F[f"amaxc{k + 1}"], call + 1)
                nc.vector.reciprocal(arec[k][:, :], amaxc[k][:, :]).then_inc(F[f"arec{k + 1}"], 1)
                nc.vector.tensor_scalar(dscale[k][:, :], amaxc[k][:, :], w127[0:R, k:k + 1], None, ALU.mult
                                        ).then_inc(F[f"small{k + 1}"], 1)
                dve.wait_ge(F[f"arec{k + 1}"], call + 1)
                nc.vector.tensor_scalar(qscale[k][:, :], arec[k][:, :], 127.0, None, ALU.mult
                                        ).then_inc(F[f"small{k + 1}"], 1)

            def rows_scaled(call):
                dve.wait_ge(F["rms1"], call + 1)
                for s in range(2):
                    nc.vector.scalar_tensor_tensor(xn[:, s, :], yn[:, s, :], rms[0][:, s:s + 1], g_in[:, :],
                                                   ALU.mult, ALU.mult).then_inc(F["xn"], 1)
                dve.wait_ge(F["xn"], 2 * call + 2)
                quantise_scale(0, call, xn[:, :, :])

            def rows_integer(call):
                dve.wait_ge(F["t1"], 2 * call + 2)
                dve.wait_ge(F["tr1"], 2 * call)
                nc.vector.tensor_scalar(q1[:, :, 0:D], t1[:, :, :], MAGIC, 127.0, ALU.subtract, ALU.min
                                        ).then_inc(F["q1"], 1)

            ln_vector(dve, L2, 0)
            rows_scaled(0)
            rows_integer(0)
            with dve.Fori(0, PAIRS) as i:
                ln_vector(dve, L2, i + 1)
                for s in range(2):
                    dve.wait_ge(F["sg"], 2 * i + s + 1)
                    nc.vector.scalar_tensor_tensor(z[:, s, :], ps[0:R, 2 + 2 * s, :], dscale[0][:, s:s + 1], sg[:, s, :],
                                                   ALU.mult, ALU.mult).then_inc(F["z"], 1)
                dve.wait_ge(F["rms2"], i + 1)
                for s in range(2):
                    nc.vector.scalar_tensor_tensor(zn[:, s, :], z[:, s, :], rms[1][:, s:s + 1], g_out[:, :],
                                                   ALU.mult, ALU.mult).then_inc(F["zn"], 1)
                dve.wait_ge(F["zn"], 2 * i + 2)
                quantise_scale(1, i, zn[:, :, :])
                rows_scaled(i + 1)
                dve.wait_ge(F["t2"], 2 * i + 2)
                nc.vector.tensor_scalar(q2[:, :, :], t2[:, :, :], MAGIC, 127.0, ALU.subtract, ALU.min
                                        ).then_inc(F["q2"], 1)
                rows_integer(i + 1)
                for s in range(2):
                    dve.wait_ge(F["down"], 2 * i + s + 1)
                    nc.vector.scalar_tensor_tensor(h[:, 2 * i + s, :], ps[0:R, s, 0:D], dscale[1][:, s:s + 1],
                                                   h[:, 2 * i + s, :], ALU.mult, ALU.add).then_inc(F["resid"], 1)
            dve.wait_ge(F["resid"], TILES)


            dve.wait_ge(A1["const_in"], A1["const_in before"] + 160)
            dve.wait_ge(A1["clear"], A1["clear before"] + 2)

            def transposed_vector(L, A, i):
                dve.wait_ge(L["tr"], L["tr before"] + 2 * i + 1)
                dve.wait_ge(A["v"], A["v before"] + 2 * i)
                nc.vector.tensor_copy(xT[:, :, 0:R], ps[:, 0, 0:3 * R].rearrange("p (c r) -> p c r", c=3)
                                      ).then_inc(A["tr_dve"], 1)

            def queries(A, i, g, table):
                dve.wait_ge(A["q"], A["q before"] + 3 * i + g + 1)
                nc.vector.tensor_tensor(Qz1[:, :, 4 * g:4 * g + 4, :],
                                        ps[:, 2, 0:R2].rearrange("p (s r) -> p s r", s=2).unsqueeze(2)
                                        .to_broadcast([128, 2, 4, R]), table, ALU.mult).then_inc(A["qz"], 1)

            def normalise(A, i, s, bank, least):
                heads = ps[0:R, bank, 0:NH * (HE + 1)].rearrange("p (n e) -> p n e", n=NH)
                dve.wait_ge(A["pv"], A["pv before"] + 2 * i + s + 1)
                if least:
                    nc.vector.tensor_scalar(den[:, s, :], heads[:, :, HE], least, None, ALU.max).then_inc(A["den"], 1)
                    dve.wait_ge(A["den"], A["den before"] + 2 * i + s + 1)
                    nc.vector.reciprocal(rden[:, s, :], den[:, s, :]).then_inc(A["rec"], 1)
                else:
                    nc.vector.reciprocal(rden[:, s, :], heads[:, :, HE]).then_inc(A["rec"], 1)
                dve.wait_ge(A["rec"], A["rec before"] + 2 * i + s + 1)
                nc.vector.tensor_tensor(O1[:, s, 0:D].rearrange("p (n e) -> p n e", n=NH), heads[:, :, 0:HE],
                                        rden[:, s, :].unsqueeze(2).to_broadcast([R, NH, HE]), ALU.mult
                                        ).then_inc(A["o"], 1)

            def residual(A, i, s, stream):
                dve.wait_ge(A["op"], A["op before"] + 2 * i + s + 1)
                nc.vector.tensor_tensor(stream[:, 2 * i + s, :], ps[0:R, 2 * s + 1, 0:D], stream[:, 2 * i + s, :],
                                        ALU.add).then_inc(A["resid"], 1)

            ln_vector(dve, L3, 0)
            dve.wait_ge(L3["y"], L3["y before"] + 2)
            split_vector(dve, L3, 0, yn)
            with dve.Fori(0, PAIRS) as i:
                transposed_vector(L3, A1, i)
                dve.wait_ge(A1["s"], A1["s before"] + 6 * i)
                dve.wait_ge(A1["kt"], A1["kt before"] + i)
                for g in range(3):
                    queries(A1, i, g, rope_q[:, :, :].unsqueeze(1).to_broadcast([128, 2, 4, R]))
                    dve.wait_ge(A1["k"], A1["k before"] + 3 * i + g + 1)
                    for part, dst in ((0, kc), (1, ks)):
                        nc.vector.tensor_tensor(dst[:, g, :], ps[:, 3, part * R2:(part + 1) * R2], rope_k[:, part, :],
                                                ALU.mult).then_inc(A1["ks"], 1)
                for s in range(2):
                    dve.wait_ge(A1["s"], A1["s before"] + 6 * i + 3 * s + 3)
                    dve.wait_ge(A1["gel"], A1["gel before"] + 2 * i)
                    scores = ps[0:R, 3 * s:3 * s + 3, :].rearrange("p b (n c) -> p (b n) c", n=4)
                    mine = own[:, s, :].rearrange("p (n q) -> p n q", n=NH)
                    nc.vector.tensor_scalar(mine, scores[:, :, 0:S], image[:, 0:1], TINY, ALU.mult, ALU.add
                                            ).then_inc(A1["own"], 1)
                    for m in range(1, IPT):
                        dve.wait_ge(A1["own"], A1["own before"] + 6 * i + 3 * s + m)
                        nc.vector.scalar_tensor_tensor(mine, scores[:, :, m * S:(m + 1) * S], image[:, m:m + 1], mine,
                                                       ALU.mult, ALU.add).then_inc(A1["own"], 1)
                ln_vector(dve, L3, i + 1)
                for s in range(2):
                    dve.wait_ge(A1["own"], A1["own before"] + 6 * i + 6)
                    nc.vector.reciprocal(rown[:, s, :], own[:, s, :]).then_inc(A1["rown"], 1)
                    dve.wait_ge(A1["rown"], A1["rown before"] + 2 * i + s + 1)
                    dve.wait_ge(A1["gel"], A1["gel before"] + 2 * i + s + 1)
                    dve.wait_ge(A1["pt"], A1["pt before"] + 2 * i)
                    nc.vector.tensor_tensor(wt1[:, s, :], gel[:, s, :], rown[:, s, :], ALU.mult
                                            ).then_inc(A1["wt"], 1)
                dve.wait_ge(L3["y"], L3["y before"] + 2 * i + 4)
                split_vector(dve, L3, i + 1, yn)
                dve.wait_ge(A1["ot"], A1["ot before"] + 2 * i)
                for s in range(2):
                    normalise(A1, i, s, 6 + s, 1e-6 / (2.0 * float(HE) ** 0.5 / 2.0 ** 0.5))
                for s in range(2):
                    residual(A1, i, s, h)
            dve.wait_ge(A1["resid"], A1["resid before"] + TILES)
            for s in range(2):
                nc.vector.tensor_copy(shift[s][:, :].rearrange("p (n r) -> p n r", n=NH),
                                      free_in[:, :].unsqueeze(1).to_broadcast([MK, NH, R])).then_inc(A2["copied"], 1)
            ln_vector(dve, L4, 0, dst=x1)
            dve.wait_ge(L4["y"], L4["y before"] + 2)
            ln_vector(dve, L4, 0, src=x1, count=1)
            dve.wait_ge(L4["affine"], L4["affine before"] + 1)
            split_vector(dve, L4, 0, yn2)
            with dve.Fori(0, PAIRS) as i:
                transposed_vector(L4, A2, i)
                dve.wait_ge(A2["st"], A2["st before"] + 6 * i)
                for g in range(3):
                    queries(A2, i, g, quarter[:, :].unsqueeze(1).unsqueeze(3).to_broadcast([128, 2, 4, R]))
                ln_vector(dve, L4, i + 1, dst=x1, count=2 * i + 2)
                dve.wait_ge(L4["y"], L4["y before"] + 4 * i + 6)
                nc.vector.memset(after_stats[0:1, :], 0.0)
                ln_vector(dve, L4, i + 1, src=x1, count=2 * i + 3)
                for s in range(2):
                    dve.wait_ge(A2["s"], A2["s before"] + 2 * i + s + 1)
                    nc.vector.tensor_reduce(nmx[:, s, :],
                                            ps[0:R, 3 * s:3 * s + 3, 0:4 * R].rearrange("p b (n r) -> p b n r", n=4),
                                            AX.X, ALU.max, negate=True).then_inc(A2["nmx"], 1)
                    dve.wait_ge(A2["mt"], A2["mt before"] + 2 * i + s + 1)
                    nc.vector.tensor_copy(nmT[:, s, :], ps[0:NH, 6, 0:R]).then_inc(A2["nmT"], 1)
                dve.wait_ge(L4["affine"], L4["affine before"] + i + 2)
                split_vector(dve, L4, i + 1, yn2)
                dve.wait_ge(A2["ot"], A2["ot before"] + 2 * i)
                for s in range(2):
                    normalise(A2, i, s, 7 - s, None)
                for s in range(2):
                    residual(A2, i, s, x1)
            dve.wait_ge(A2["resid"], A2["resid before"] + TILES)
            nc.vector.tensor_copy(router_h[:, :, :], router_in[:, :, :]).then_inc(RT["hi"], 1)
            dve.wait_ge(RT["hi"], 1)
            nc.vector.tensor_tensor(router_l[:, :, :], router_in[:, :, :], router_h[:, :, :].bitcast(F32), ALU.subtract
                                    ).then_inc(RT["split"], 1)

            def split_expert(e, q, part, parts=6):
                n1, n2 = 2 * FF // parts, FM * D // parts
                cols1, cols2 = slice(part * n1, (part + 1) * n1), slice(part * n2, (part + 1) * n2)
                if part == 0:
                    dve.wait_ge(EX["in1"], 16 * e + 16)
                    dve.wait_ge(EX["in2"], 16 * e + 16)
                both = ((est1[:, cols1], eh1[q][:, :, :].rearrange("p k n -> p (k n)")[:, cols1],
                         el1[q][:, :, :].rearrange("p k n -> p (k n)")[:, cols1]),
                        (est2[:, cols2], eh2[q][:, :, :].rearrange("p k n -> p (k n)")[:, cols2],
                         el2[q][:, :, :].rearrange("p k n -> p (k n)")[:, cols2]))
                for src, hi, lo in both:
                    nc.vector.tensor_copy(hi, src).then_inc(EX["hi"], 1)
                for n, (src, hi, lo) in enumerate(both):
                    dve.wait_ge(EX["hi"], 12 * e + 2 * part + n + 1)
                    nc.vector.tensor_tensor(lo, src, hi.bitcast(F32), ALU.subtract).then_inc(EX["lo"], 1)

            ln_vector(dve, L5, 0, src=x1)
            dve.wait_ge(L5["affine"], L5["affine before"] + 1)
            split_vector(dve, L5, 0, yn2)
            for part in range(6):
                split_expert(0, 0, part)
            with dve.Fori(0, PAIRS) as i:
                dve.wait_ge(L5["tr"], L5["tr before"] + 2 * i + 1)
                dve.wait_ge(RT["logits"], 2 * i)
                src = ps[:, 0, 0:3 * R].rearrange("p (c r) -> p c r", c=3)
                nc.vector.tensor_copy(xT[:, :, 0:R], src).then_inc(RT["tr_dve"], 1)
                nc.vector.tensor_copy(xTm[:, :, bass.ds(i * R2, R)], src).then_inc(RT["xm1"], 1)
                ln_vector(dve, L5, i + 1, src=x1)
                dve.wait_ge(L5["affine"], L5["affine before"] + i + 2)
                split_vector(dve, L5, i + 1, yn2)
                for s in range(2):
                    dve.wait_ge(RT["logits"], 2 * i + s + 1)
                    nc.vector.tensor_copy(logits[:, s, :], ps[0:R, 2 + s, 0:E]).then_inc(RT["raw"], 1)
                dve.wait_ge(RT["raw"], 2 * i + 2)
                nc.vector.memset(after_stats[0:1, :], 0.0)
                for s in range(2):
                    nc.vector.max(top8[:, s, :], logits[:, s, :]).then_inc(RT["top"], 1)
                dve.wait_ge(RT["top"], 2 * i + 2)
                nc.vector.memset(after_stats[0:1, :], 0.0)
                for s in range(2):
                    nc.vector.max_index(at8[:, s, :], top8[:, s, :], logits[:, s, :]).then_inc(RT["at"], 1)
                dve.wait_ge(RT["at"], 2 * i + 2)
                for n in range(2):
                    nc.vector.tensor_copy(top[:, n, bass.ds(2 * i, 2)], top8[:, :, n]).then_inc(RT["kept"], 1)
                    nc.vector.tensor_copy(top_at[:, n, bass.ds(2 * i, 2)], at8[:, :, n]).then_inc(RT["kept"], 1)
            dve.wait_ge(RT["kept"], 4 * PAIRS)
            nc.vector.tensor_tensor(pr[:, 0, :], top[:, 1, :], top[:, 0, :], ALU.subtract).then_inc(RT["k2"], 1)
            dve.wait_ge(RT["ex"], 1)
            nc.vector.tensor_scalar(pr[:, 2, :], pr[:, 1, :], 1.0, None, ALU.add).then_inc(RT["share"], 1)
            dve.wait_ge(RT["share"], 1)
            nc.vector.reciprocal(pr[:, 3, :], pr[:, 2, :]).then_inc(RT["share"], 1)
            dve.wait_ge(RT["share"], 2)
            nc.vector.tensor_tensor(pr[:, 0, :], pr[:, 1, :], pr[:, 3, :], ALU.mult).then_inc(RT["share"], 1)
            for n in range(2):
                nc.vector.tensor_tensor(share[:, n, :, :], lanes[:, :].unsqueeze(2).to_broadcast([R, E, TILES]),
                                        top_at[:, n, :].unsqueeze(1).to_broadcast([R, E, TILES]), ALU.is_equal
                                        ).then_inc(RT["share"], 1)
            dve.wait_ge(RT["share"], 5)
            for n, p in enumerate((3, 0)):
                nc.vector.tensor_tensor(share[:, n, :, :], share[:, n, :, :],
                                        pr[:, p, :].unsqueeze(1).to_broadcast([R, E, TILES]), ALU.mult
                                        ).then_inc(RT["share"], 1)
            dve.wait_ge(RT["share"], 7)
            nc.vector.tensor_tensor(we[:, :, :], share[:, 0, :, :], share[:, 1, :, :], ALU.add).then_inc(RT["share"], 1)
            dve.wait_ge(RT["share"], 8)

            def experts_vector(e, q, c, tiles, part, ahead):
                base = 36 * e + 6 * c
                for m in range(FM):
                    dve.wait_ge(EX["gelu"], base + m + 1)
                    if m == 0:
                        dve.wait_ge(EX["down"], TILES * e + 4 * c)
                    nc.vector.tensor_copy(gh[:, m, 0:tiles * R], graw[:, m % 2, 0:tiles * R]).then_inc(EX["gh"], 1)
                    dve.wait_ge(EX["gh"], base + m + 1)
                    nc.vector.tensor_tensor(gl[:, m, 0:tiles * R], graw[:, m % 2, 0:tiles * R],
                                            gh[:, m, 0:tiles * R].bitcast(F32), ALU.subtract).then_inc(EX["gl"], 1)
                if ahead:
                    part(1 - q)
                dve.wait_ge(EX["acc"], TILES * e)
                for tt in range(tiles):
                    dve.wait_ge(EX["down"], TILES * e + 4 * c + tt + 1)
                    row = h[:, 4 * c + tt, :]
                    nc.vector.scalar_tensor_tensor(row, ps[0:R, 4 + tt, 0:D], we[:, e, bass.ds(4 * c + tt, 1)], row,
                                                   ALU.mult, ALU.add).then_inc(EX["acc"], 1)

            def sixth(e, n):
                def split(q):
                    n1, n2 = 2 * FF // 6, FM * D // 6
                    both = []
                    for src, hi, lo, size in ((est1, eh1[q], el1[q], n1), (est2, eh2[q], el2[q], n2)):
                        cols = bass.ds(n * size, size)
                        both.append((src[:, cols], hi[:, :, :].rearrange("p k n -> p (k n)")[:, cols],
                                     lo[:, :, :].rearrange("p k n -> p (k n)")[:, cols]))
                    dve.wait_ge(EX["in1"], 16 * e + 16)
                    dve.wait_ge(EX["in2"], 16 * e + 16)
                    for src, hi, lo in both:
                        nc.vector.tensor_copy(hi, src).then_inc(EX["hi"], 1)
                    for m, (src, hi, lo) in enumerate(both):
                        dve.wait_ge(EX["hi"], 12 * e + 2 * n + m + 1)
                        nc.vector.tensor_tensor(lo, src, hi.bitcast(F32), ALU.subtract).then_inc(EX["lo"], 1)
                return split

            dve.wait_ge(RT["streams"], PAIRS)

            def expert(e, q, ahead):
                with dve.Fori(0, TILES // E_CHUNK) as c:
                    experts_vector(e, q, c, E_CHUNK, sixth(e + 1, c), ahead)
                last = TILES // E_CHUNK
                experts_vector(e, q, last, TILES % E_CHUNK, sixth(e + 1, last), ahead)

            with dve.Fori(0, E // 2 - 1) as pair:
                expert(2 * pair, 0, True)
                expert(2 * pair + 1, 1, True)
            expert(E - 2, 0, True)
            expert(E - 1, 1, False)


def k192(w):
    return np.ascontiguousarray(np.stack([w[0:K0], np.concatenate([w[K0:D], w[K0:D]])], axis=1))


def constants():
    f = np.float32
    tok = np.arange(R)
    pos, img = tok % S, tok // S
    key_rows = np.zeros((MK, R), f)
    key_rows[0:13] = 1
    key_rows[M_CAUSAL + pos, tok] = 1
    key_rows[M_IMAGE + img, tok] = 1
    later = np.where(np.arange(S)[:, None] > pos[None, :], BIG, 0).astype(f)
    other = np.where(np.arange(IPT)[:, None] != img[None, :], BIG, 0).astype(f)
    full = np.zeros((2, MK, R), f)
    full[0, M_CAUSAL:M_IMAGE] = later
    full[:, M_IMAGE:] = other
    cols = key_rows.copy()
    cols[0:13] = 0
    masks = np.concatenate([key_rows, full[0], full[1], np.tile(cols, (1, 4))], axis=1)
    shift = np.stack([full[0], full[1]], axis=1)
    sel = np.repeat(np.eye(NH, dtype=f), R, axis=1)
    freq = (1.0 / 10000.0 ** (np.arange(HE // 2, dtype=f) / f(HE // 2))).astype(f)
    angle = pos[None, :].astype(f) * np.repeat(freq, 2)[:, None]
    cos, sin = np.cos(angle).astype(f), np.sin(angle).astype(f)
    sin[0::2] *= -1
    row = np.arange(128)
    e, half, head = row % HE, row // HE % 2, row // (2 * HE)
    table = np.where(half[:, None] == 0, cos[e], sin[e])
    mine = (head[:, None] == np.arange(4)).astype(f)
    rope_q = table[:, None, :] * mine[:, :, None]
    rope_k = np.stack([np.tile(cos[e], (1, 2)), np.tile(sin[e], (1, 2))], axis=1)
    same = img[:, None] == img[None, :]
    causal = (same & (pos[:, None] <= pos[None, :])).astype(f)
    image = (img[:, None] == np.arange(IPT)).astype(f)
    lanes = np.tile(np.arange(E, dtype=f), (R, 1))
    return {"rope_q": rope_q.astype(f), "rope_k": rope_k.astype(f), "causal": causal, "image": image, "quarter": mine,
            "free": full[1], "lanes": lanes, "ident": np.eye(128, dtype=f), "masks": masks, "shift": np.ascontiguousarray(shift), "sel12": sel}


def lay_out(i):
    a = constants()
    a["x"] = np.ascontiguousarray(i["x"].reshape(B, C_IN, GRID, 2, PATCH // 2, GRID, PATCH)
                                  .transpose(0, 2, 1, 3, 5, 4, 6).reshape(B * GRID, C_IN * PW))
    a["wtok"] = np.ascontiguousarray(i["L0_tok_W"].reshape(NK, 128, D).transpose(1, 0, 2))
    near = np.arange(GRID) * 14 // GRID
    pos = i["L0_tok_positions"][0][:, near][:, :, near].reshape(D, GRID * GRID).T
    a["pos"] = np.ascontiguousarray(np.tile(np.concatenate([i["L0_tok_cls_embedding"][0], pos]), (IPT, 1)))
    a["tok_b"] = i["L0_tok_b"].reshape(1, D)
    qkv = [i[f"L0_attn_W_{c}"].transpose(1, 0, 2).reshape(D, NH * HD) for c in "QKV"]
    a["w1"] = k192(np.concatenate(qkv, axis=1))
    a["b_qk"] = np.ascontiguousarray(np.concatenate(
        [i["L0_attn_b_Q"].reshape(6, 128).T, i["L0_attn_b_K"].reshape(6, 128).T], axis=1))
    a["b_v"] = i["L0_attn_b_V"].reshape(1, NH * HD)
    a["b_o"] = i["L0_attn_b_O"].reshape(1, D)
    a["wo1"] = np.ascontiguousarray(i["L0_attn_W_O"].reshape(6, 128, D).transpose(1, 0, 2))
    win = np.zeros((256, 2 * HF), np.float32)
    win[0:D] = i["L0_ffn_w_in"].T
    a["win"] = np.ascontiguousarray(win.reshape(2, 128, 2 * HF).transpose(1, 0, 2))
    a["wout"] = np.ascontiguousarray(i["L0_ffn_w_out"].T.reshape(4, 128, D).transpose(1, 0, 2))
    a["g_in"] = i["L0_ffn_g_in"].reshape(1, D)
    a["g_out"] = i["L0_ffn_g_out"].reshape(1, HF)
    def heads(w, other):
        out = np.zeros((D, NH, 2, HE), np.float32)
        out[:, :, 0] = w.reshape(D, NH, HE)
        if other is not None:
            out[:, :, 1] = other.reshape(D, NH, HE)
        return out.reshape(D, NH * 2 * HE)

    def swapped(w):
        return w.reshape(D, NH, HE // 2, 2)[:, :, :, ::-1].reshape(D, D)

    q, k, v = (i[f"L1_attn_W{c}"].T for c in "qkv")
    q4, k4, v4 = (i["L1_ffn_Wqkv"][:, c * D:(c + 1) * D] for c in range(3))
    both = np.concatenate([heads(q, swapped(q)), heads(k, k), heads(swapped(k), swapped(k)), v,
                           heads(q4, None), heads(k4, None), v4, np.zeros((D, WPAD - WCOLS), np.float32)], axis=1)
    a["w3"] = k192(both)
    w, gap = [], 128
    for m in (i["L1_attn_Wproj"].T, i["L1_ffn_Wproj"]):
        padded = np.zeros((256, D), np.float32)
        padded[0:D] = m
        w.append(padded.reshape(2, 128, D).transpose(1, 0, 2))
    a["proj"] = np.ascontiguousarray(np.stack(w, axis=1))
    a["gains"] = np.stack([i[f"L1_ffn_ln{n}_{x}"] for n in (1, 2) for x in "gb"])[None]
    a["router"] = k192(i["L1_ffn_Wrouter"])
    a["moe1"] = np.stack([k192(m).reshape(128, 2 * FF) for m in i["L1_ffn_W1"]])
    a["moe2"] = np.ascontiguousarray(i["L1_ffn_W2"].reshape(E, FM, 128, D).transpose(0, 2, 1, 3)).reshape(E, 128, FM * D)
    return a


def kernel(**inputs):
    import numpy as _np
    import concourse.bacc as _bacc
    from concourse import mybir as _mybir
    from concourse.bass_utils import run_bass_kernel_spmd as _run

    nc = _bacc.Bacc("TRN2", target_bir_lowering=False, num_devices=1)
    arrays, tensors = {}, {}
    for name, a in lay_out({n: _np.asarray(v) for n, v in inputs.items()}).items():
        a = _np.ascontiguousarray(a)
        arrays[f"in_{name}_dram"] = a
        tensors[name] = nc.dram_tensor(f"in_{name}_dram", a.shape, _mybir.dt.from_np(a.dtype),
                                       kind="ExternalInput").ap()
    tensors["out"] = nc.dram_tensor("out_0_dram", (B, S, D), _mybir.dt.float32, kind="ExternalOutput").ap()
    build_program(nc, tensors)
    r = _run(nc, [arrays], core_ids=[0])
    return r.results[0]["out_0_dram"]
```

```python
import numpy as np
import concourse.bass as bass
from concourse import mybir
from contextlib import ExitStack

F32 = mybir.dt.float32
F32R = mybir.dt.float32r
BF16 = mybir.dt.bfloat16
U32 = mybir.dt.uint32
ALU = mybir.AluOpType
ACT = mybir.ActivationFunctionType
AX = mybir.AxisListType
RADD = bass.bass_isa.ReduceOp.add

B, C_IN, IMG, PATCH = 64, 3, 96, 16
GRID = IMG // PATCH
S = GRID * GRID + 1
D = 192
K0 = 128
IPT = 3
R = IPT * S
TILES = 22
TILES_ALL = 24
PAIRS = TILES // 2
R2 = 2 * R
GI = 18
GROUPS = 4
GT = GI // IPT
GROWS = GI * GRID
NK = C_IN * 2
PW = PATCH * IMG
NH = 12
HD = 64
HE = 16
HF = 512
E, FF = 8, 768
FM = FF // 128
NQ = NH * S
BIG = -1.0e30
TINY = 1.0e-20
MAGIC = 12582912.0
MK = 72
M_CAUSAL = 32
M_IMAGE = M_CAUSAL + S
W34 = 3 * 128 + 6 * 128 + D
W4 = 3 * 128 + 3 * 128 + D
WCOLS = W34 + W4
WSTEP = 210
WPAD = PAIRS * WSTEP
E_CHUNK = 4


def build_program(nc, t):
    ctx = ExitStack()
    with ctx:
        def sem(name):
            return ctx.enter_context(nc.semaphore(name))

        cursor = [16512]

        def put(name, shape, dt, at=None):
            where = cursor if at is None else at
            size = 4 if dt in (F32, F32R, U32) else 2
            n = size
            for d in shape[1:]:
                n *= d
            got = nc.alloc_sbuf_tensor_at(name, shape, dt, offset=where[0])
            where[0] += (n + 31) // 32 * 32
            assert where[0] <= 229344, (name, where[0])
            return got

        ps = ctx.enter_context(nc.psum_tensor("ps", [128, 8, 512], F32))

        h = put("h", [R, TILES_ALL, D], F32)
        ident = put("ident", [128, 128], F32)
        identb = put("identb", [128, 128], BF16)
        halfneg = put("halfneg", [R, 2], F32)
        eps_ln = put("eps_ln", [R, 2], F32)
        eps_rms = put("eps_rms", [R, 2], F32)
        after_stats = put("after_stats", [1, 1], F32)
        key_rows = put("key_rows", [MK, R], F32R)
        query_rows = put("query_rows", [MK, 2, R], F32R)
        key_cols = put("key_cols", [MK, 4 * R], F32R)
        shift = [put(f"shift{s}", [MK, NH * R], F32R) for s in range(2)]
        sel12 = put("sel12", [NH, NH * R], F32)
        posb = put("posb", [R, D], F32)
        bo_t = put("bo_t", [R, D], F32)
        bqk = put("bqk", [128, 12], F32)
        bv_t = put("bv_t", [R, NH * HD], F32)
        stats = put("stats", [R, 2, 6], F32)
        mv = put("mv", [R, 2, 2], F32)
        vare = put("vare", [R, 2], F32)
        rstd = put("rstd", [R, 2], F32)
        yn = put("yn", [R, 2, D], F32)
        yn2 = put("yn2", [R, 2, D], F32)
        xs = put("xs", [R, 2, 2 * D], F32R)
        nmx = put("nmx", [R, 2, NH], F32)
        nmT = put("nmT", [NH, 2, R], F32)
        rden = put("rden", [R, 2, NH], F32)
        xT = put("xT", [128, 3, R2], F32R)
        wq_in = put("wq_in", [128, 2, 2 * HF], BF16)
        wq_out = put("wq_out", [128, 4, D], BF16)
        g_in = put("g_in", [R, D], F32)
        g_out = put("g_out", [R, HF], F32)
        wsum = put("wsum", [128, 2], F32)
        wall = put("wall", [128, 2], F32)
        wmean = put("wmean", [128, 2], F32)
        wmean2 = put("wmean2", [128, 2], F32)
        wrec = put("wrec", [128, 2], F32)
        w127 = put("w127", [128, 2], F32)
        magic = put("magic", [R, 1], F32)
        ss, rq, rms, amax, amaxc, arec, qscale, dscale = (
            [put(f"{n}{k}", [R, 2], F32) for k in range(2)]
            for n in ("ss", "rq", "rms", "amax", "amaxc", "arec", "qscale", "dscale"))
        region_a = [cursor[0]]
        a0 = region_a[0]
        wh1 = put("wh1", [128, 2, 3 * NH * HD], F32R, region_a)
        wl1 = put("wl1", [128, 2, 3 * NH * HD], F32R, region_a)
        region_b = [region_a[0]]
        wh3 = put("wh3", [128, 2, WPAD], F32R, region_b)
        wl3 = put("wl3", [128, 2, WPAD], F32R, region_b)
        work0 = region_b[0]

        w = [work0]
        X = [put(f"X{p}", [128, C_IN * PW], F32, w) for p in range(2)]
        PT = [put(f"PT{p}", [128, NK, GI * S], F32, w) for p in range(2)]
        wtok = put("wtok", [128, NK, D], F32, w)
        w = [a0 + (region_b[0] - region_b[0])]
        w = [region_a[0]]
        stage1 = put("stage1", [128, 2, 2304], F32, w)
        mask_in = put("mask_in", [MK, R + 2 * R + 4 * R], F32, w)
        shift_in = put("shift_in", [MK, 2, R], F32, w)
        win_in = put("win_in", [128, 2, 2 * HF], F32, w)
        wout_in = put("wout_in", [128, 4, D], F32, w)
        assert w[0] <= work0, (w[0], work0)
        w = [work0]
        Qz = put("Qz", [128, 2, NH, R], F32, w)
        KT = put("KT", [128, 6, R2], F32, w)
        V = put("V", [R, 2, NH, HD + 1], F32, w)
        Pt = put("Pt", [R, 2, NH * R], F32, w)
        O = put("O", [R, 2, NH * HD], F32, w)
        OT = put("OT", [128, 2, 6, R], F32, w)
        wo1 = put("wo1", [128, 6, D], F32, w)
        wst3 = put("wst3", [128, 2, WPAD], F32, w)

        w = [work0]
        xn = put("xn", [R, 2, D], F32, w)
        t1 = put("t1", [R, 2, D], F32, w)
        q1 = put("q1", [R, 2, 2 * 128], BF16, w)
        q1T = put("q1T", [128, 2, 2, R + 1], BF16, w)
        sg = put("sg", [R, 2, HF], F32, w)
        z = put("z", [R, 2, HF], F32, w)
        zn = put("zn", [R, 2, HF], F32, w)
        t2 = put("t2", [R, 2, HF], F32, w)
        q2 = put("q2", [R, 2, HF], BF16, w)
        q2T = put("q2T", [128, 2, 4, R + 1], BF16, w)
        junk1 = put("junk1", [R, 2, D], F32, w)
        junk2 = put("junk2", [R, 2, HF], F32, w)
        psb = ps[:, :, :].bitcast(BF16)
        w = [a0]
        rope_q = put("rope_q", [128, 4, R], F32, w)
        rope_k = put("rope_k", [128, 2, R2], F32, w)
        causal = put("causal", [R, R], F32, w)
        image = put("image", [R, IPT], F32, w)
        quarter = put("quarter", [128, 4], F32, w)
        free_in = put("free_in", [MK, R], F32, w)
        proj = put("proj", [128, 2, 2, D], F32, w)
        gains = put("gains", [R, 4, D], F32, w)
        router_in = put("router_in", [128, 2, E], F32, w)
        router_h = put("router_h", [128, 2, E], F32R, w)
        router_l = put("router_l", [128, 2, E], F32R, w)
        lanes = put("lanes", [R, E], F32, w)
        logits = put("logits", [R, 2, E], F32, w)
        top8 = put("top8", [R, 2, 8], F32, w)
        at8 = put("at8", [R, 2, 8], U32, w)
        top = put("top", [R, 2, TILES], F32, w)
        top_at = put("top_at", [R, 2, TILES], F32, w)
        pr = put("pr", [R, 4, TILES], F32, w)
        share = put("share", [R, 2, E, TILES], F32, w)
        we = put("we", [R, E, TILES], F32, w)
        est1 = put("est1", [128, 2 * FF], F32, w)
        est2 = put("est2", [128, FM * D], F32, w)
        assert w[0] <= region_a[0]
        w = [work0]
        Qz1 = put("Qz1", [128, 2, NH, R], F32, w)
        KT1 = put("KT1", [128, 3, R2], F32, w)
        V1 = put("V1", [R, 2, NH, HE + 1], F32, w)
        Pt1 = put("Pt1", [R, 2, NH * R], F32, w)
        den = put("den", [R, 2, NH], F32, w)
        O1 = put("O1", [R, 2, 256], F32, w)
        OT1 = put("OT1", [128, 2, 2, R], F32, w)
        x1 = put("x1", [R, TILES_ALL, D], F32, list(w))
        kc = put("kc", [128, 3, R2], F32, w)
        ks = put("ks", [128, 3, R2], F32, w)
        own = put("own", [R, 2, NQ], F32, w)
        rown = put("rown", [R, 2, NQ], F32, w)
        gel = put("gel", [R, 2, NQ], F32, w)
        wt1 = put("wt1", [R, 2, NQ], F32, w)
        eh1, el1, eh2, el2 = [None] * 2, [None] * 2, [None] * 2, [None] * 2

        def expert_weights(q):
            eh1[q] = put(f"eh1{q}", [128, 2, FF], F32R, w)
            el1[q] = put(f"el1{q}", [128, 2, FF], F32R, w)
            eh2[q] = put(f"eh2{q}", [128, FM, D], F32R, w)
            el2[q] = put(f"el2{q}", [128, FM, D], F32R, w)

        expert_weights(0)
        w = [work0]
        expert_weights(1)
        graw = put("graw", [128, 2, 4 * R], F32, w)
        gh = put("gh", [128, FM, 4 * R], F32R, w)
        w2_ = [region_a[0]]
        xTm = put("xTm", [128, 3, TILES * R], F32R, w2_)
        gl_at = w2_
        gl = put("gl", [128, FM, 4 * R], F32R, w)

        x_in = [sem(f"x_in{p}") for p in range(2)]; ident_in = sem("ident_in"); wtok_in = sem("wtok_in"); const_in = sem("const_in"); w1_in = sem("w1_in")
        w3_in = sem("w3_in"); wo1_in = sem("wo1_in"); pos_in = sem("pos_in")
        cleared = sem("cleared")
        consts_ready = sem("consts_ready"); w1_hi = sem("w1_hi"); w1_ready = sem("w1_ready")
        w3_hi = sem("w3_hi")
        w3_ready = sem("w3_ready")
        pt_done = sem("pt_done"); pt_copied = sem("pt_copied"); tok_done = sem("tok_done"); tok_h = sem("tok_h")
        out_done = sem("out_done")

        def signals(stage, names):
            return {n: sem(f"{stage}_{n}") for n in names.split()}

        def counted(shared, before, own=None):
            got = {}
            for n, s in {**shared, **(own or {})}.items():
                got[n] = s
                got[n + " before"] = before.get(n, 0)
            return got

        ln = signals("ln", "stats mv vare rstd y affine hi xs tr")
        STEPS = PAIRS + 1

        def norm_stage(norms, splits, affines):
            return counted(ln, {"stats": 2 * STEPS * norms, "mv": 2 * STEPS * norms, "vare": STEPS * norms,
                                "rstd": STEPS * norms, "y": 2 * STEPS * norms, 
                                "affine": 2 * STEPS * affines, "hi": STEPS * splits, "xs": STEPS * splits,
                                "tr": TILES * splits})

        L1, L2, L3, L4, L5 = (norm_stage(*n) for n in ((0, 0, 0), (1, 1, 0), (2, 1, 0), (3, 2, 0), (5, 3, 1)))
        tr_copied_dve = sem("tr_copied_dve"); tr_copied_act = sem("tr_copied_act")

        def split5(hi, lo, a, b):
            return ((1, hi[:, 0, a:b]), (0, hi[:, 0, a:b]), (1, lo[:, 0, a:b]), (2, hi[:, 1, a:b]), (2, lo[:, 1, a:b]))

        def ln_stats(dve, L, call, src=h, count=None):
            n = call if count is None else count
            for s in range(2):
                nc.vector.bn_stats(stats[:, s, :], src[:, 2 * call + s, :]).then_inc(L["stats"], 1)
            dve.wait_ge(L["stats"], L["stats before"] + 2 * n + 2)
            nc.vector.memset(after_stats[0:1, :], 0.0)
            for s in range(2):
                nc.vector.bn_aggr(mv[:, s, :], stats[:, s, :]).then_inc(L["mv"], 1)

        def ln_apply(dve, L, call, src=h, dst=None, count=None):
            n = call if count is None else count
            dve.wait_ge(L["rstd"], L["rstd before"] + n + 1)
            for s in range(2):
                out = yn[:, s, :] if dst is None else dst[:, 2 * call + s, :]
                nc.vector.tensor_scalar(out, src[:, 2 * call + s, :], mv[:, s, 0:1], rstd[:, s:s + 1],
                                        ALU.subtract, ALU.mult).then_inc(L["y"], 1)

        def ln_vector(dve, L, call, src=h, dst=None, count=None):
            ln_stats(dve, L, call, src, count)
            ln_apply(dve, L, call, src, dst, count)

        def ln_affine(dve, L, call, src, g, b, count=None):
            n = call if count is None else count
            ln_stats(dve, L, call, src, count)
            dve.wait_ge(L["mv"], L["mv before"] + 2 * n + 2)
            for s in range(2):
                nc.vector.scalar_tensor_tensor(yn2[:, s, :], src[:, 2 * call + s, :], mv[:, s, 0:1], g,
                                               ALU.subtract, ALU.mult).then_inc(L["y"], 1)
            dve.wait_ge(L["y"], L["y before"] + 2 * n + 2)
            dve.wait_ge(L["rstd"], L["rstd before"] + n + 1)
            for s in range(2):
                nc.vector.scalar_tensor_tensor(yn2[:, s, :], yn2[:, s, :], rstd[:, s:s + 1], b,
                                               ALU.mult, ALU.add).then_inc(L["affine"], 1)

        def split_vector(dve, L, call, src):
            dve.wait_ge(L["tr"], L["tr before"] + 2 * call)
            nc.vector.tensor_copy(xs[:, :, K0:K0 + D], src[:, :, :]).then_inc(L["hi"], 1)
            dve.wait_ge(L["hi"], L["hi before"] + call + 1)
            nc.vector.tensor_tensor(xs[:, :, 0:K0], src[:, :, 0:K0], xs[:, :, K0:2 * K0].bitcast(F32),
                                    ALU.subtract)
            nc.vector.tensor_tensor(xs[:, :, K0 + D:2 * D], src[:, :, K0:D], xs[:, :, 2 * K0:K0 + D].bitcast(F32),
                                    ALU.subtract).then_inc(L["xs"], 1)

        def ln_pool(pool, L, call):
            pool.wait_ge(L["mv"], L["mv before"] + 2 * call + 2)
            nc.gpsimd.tensor_tensor(vare[:, :], mv[:, :, 1], eps_ln[:, :], ALU.add).then_inc(L["vare"], 1)
            pool.wait_ge(L["vare"], L["vare before"] + call + 1)
            nc.gpsimd.tensor_tensor(rstd[:, :], vare[:, :], halfneg[:, :], ALU.pow).then_inc(L["rstd"], 1)

        def transposes(L, s, bank):
            x = xs[:, s, :].bitcast(F32)
            for c in range(3):
                tr = nc.tensor.transpose(ps[:, bank, c * R:(c + 1) * R], x[:, c * K0:(c + 1) * K0], ident[0:R, 0:R])
            tr.then_inc(L["tr"], 1)

        chain = sem("chain"); consts_copied = sem("consts_copied"); pos_ready = sem("pos_ready")
        bo_in = sem("bo_in"); qz_clear = sem("qz_clear"); hb_done = sem("hb_done")
        nmT_ready = sem("nmT_ready"); st_done = sem("st_done"); shift_ready = sem("shift_ready")
        o_ready = sem("o_ready"); ot_copied = sem("ot_copied"); q_copied = sem("q_copied"); k_copied = sem("k_copied")
        qk_done = sem("qk_done"); resid_done = sem("resid_done"); v_done = sem("v_done"); v_copied = sem("v_copied")
        s_done = sem("s_done"); nmx_ready = sem("nmx_ready"); mt_done = sem("mt_done"); p_ready = sem("p_ready")
        pv_done = sem("pv_done"); ot_done = sem("ot_done"); op_done = sem("op_done"); rden_ready = sem("rden_ready")
        Q = signals("quant", "in summed all step ready")
        F = signals("ffn0", "clear gain_in ssq1 rq1 rms1 xn amax1 amaxc1 arec1 small1 t1 q1 tr1 q1T up sg z ssq2 rq2 rms2 "
                    "zn amax2 amaxc2 arec2 small2 t2 q2 tr2 q2T down resid")
        both = signals("attn", "tr_dve tr_act q k qz v v_out pv rec o ot ot_out op resid")
        A1 = counted(both, {}, signals("attn1", "const_in clear ks kt s own rown gel wt pt den"))
        A2 = counted(both, {"tr_dve": PAIRS, "tr_act": PAIRS, "q": 3 * PAIRS, "k": 3 * PAIRS, "qz": 3 * PAIRS,
                            **{n: TILES for n in "v v_out pv rec o ot ot_out op resid".split()}},
                     signals("attn2", "copied kt s nmx mt shift st p"))
        RT = signals("router", "streams hi split tr_dve tr_act xm1 xm2 logits raw top at kept k2 ex share")
        EX = signals("experts", "in1 in2 hi lo half gelu gh gl down acc")
        block = ctx.enter_context(nc.Block())

        @block.sync
        def _(sp):
            def load_group(g):
                n = min(GROWS, B * GRID - g * GROWS)
                sp.dma_start(X[g % 2][0:n, :], t["x"][g * GROWS:g * GROWS + n, :]).then_inc(x_in[g % 2], 16)

            load_group(0)
            sp.dma_start(ident[:, :], t["ident"]).then_inc(ident_in, 16)
            sp.dma_start(wtok[:, :, :], t["wtok"]).then_inc(wtok_in, 16)
            sp.dma_start(stage1[:, :, :], t["w1"]).then_inc(w1_in, 16)
            load_group(1)
            sp.dma_start(win_in[:, :, :], t["win"]).then_inc(Q["in"], 16)
            sp.dma_start(wout_in[:, :, :], t["wout"]).then_inc(Q["in"], 16)
            sp.dma_start(mask_in[:, :], t["masks"]).then_inc(const_in, 16)
            sp.dma_start(shift_in[:, :, :], t["shift"]).then_inc(const_in, 16)
            sp.dma_start(sel12[:, :], t["sel12"]).then_inc(const_in, 16)
            for g in range(2, GROUPS):
                sp.wait_ge(pt_done, 12 * (g - 1))
                load_group(g)
            sp.wait_ge(tok_done, GROUPS * GT)
            sp.wait_ge(pt_done, GROUPS * 12)
            sp.dma_start(wo1[:, :, :], t["wo1"]).then_inc(wo1_in, 16)
            sp.dma_start(wst3[:, :, :], t["w3"]).then_inc(w3_in, 16)
            sp.wait_ge(w3_in, 16)
            sp.wait_ge(resid_done, TILES)
            for name, dst in (("rope_q", rope_q), ("rope_k", rope_k), ("causal", causal), ("image", image),
                              ("quarter", quarter), ("free", free_in), ("proj", proj), ("gains", gains),
                              ("router", router_in), ("lanes", lanes)):
                if name == "gains":
                    sp.dma_start(dst[:, :, :], t[name].to_broadcast([R, 4, D])).then_inc(A1["const_in"], 16)
                else:
                    sp.dma_start(dst[tuple(slice(None) for _ in dst.shape)], t[name]).then_inc(A1["const_in"], 16)
            for e in range(E):
                if e:
                    sp.wait_ge(EX["lo"], 12 * e)
                sp.dma_start(est1[:, :], t["moe1"][e]).then_inc(EX["in1"], 16)
                sp.dma_start(est2[:, :], t["moe2"][e]).then_inc(EX["in2"], 16)
            rows = t["out"].rearrange("b s d -> (b s) d")
            for c in range(6):
                sp.wait_ge(EX["acc"], TILES * (E - 1) + min(4 * c + 4, TILES))
                t0, t1 = 4 * c, min(4 * c + 4, B // IPT)
                sp.dma_start(rows[t0 * R:t1 * R, :].rearrange("(t r) d -> r t d", r=R), h[:, t0:t1, :]
                             ).then_inc(out_done, 16)
            rest = B * S - (B // IPT) * R
            sp.dma_start(rows[B * S - rest:B * S, :], h[0:rest, TILES - 1, :]).then_inc(out_done, 16)
            sp.wait_ge(out_done, 16 * 7)

        @block.gpsimd
        def _(pool):
            nc.gpsimd.dma_start(posb[:, :], t["pos"]).then_inc(pos_in, 16)
            nc.gpsimd.memset(bo_t[:, :], 0.0).then_inc(cleared, 1)
            for p in range(2):
                cls = PT[p][:, :, :].rearrange("p k (b s) -> p k b s", s=S)[:, :, :, 0]
                nc.gpsimd.memset(cls, 0.0).then_inc(cleared, 1)
            nc.gpsimd.memset(halfneg[:, :], -0.5).then_inc(cleared, 1)
            nc.gpsimd.memset(eps_ln[:, :], 1e-5).then_inc(cleared, 1)
            nc.gpsimd.memset(eps_rms[:, :], 1e-6).then_inc(cleared, 1)
            pool.wait_ge(cleared, 1)
            for i in range(IPT):
                nc.gpsimd.dma_start(bo_t[i * S + 1:(i + 1) * S, :],
                                    t["tok_b"].to_broadcast([S - 1, D])).then_inc(pos_in, 16)
            nc.gpsimd.dma_start(bv_t[:, :], t["b_v"].to_broadcast([R, NH * HD])).then_inc(pos_in, 16)
            nc.gpsimd.dma_start(bqk[:, :], t["b_qk"]).then_inc(pos_in, 16)
            nc.gpsimd.dma_start(g_in[:, :], t["g_in"].to_broadcast([R, D])).then_inc(F["gain_in"], 16)
            nc.gpsimd.dma_start(g_out[:, :], t["g_out"].to_broadcast([R, HF])).then_inc(F["gain_in"], 16)
            nc.gpsimd.memset(magic[:, :], MAGIC).then_inc(F["clear"], 1)
            pool.wait_ge(Q["summed"], 2)
            nc.gpsimd.partition_all_reduce(wall[:, :], wsum[:, :], 128, RADD).then_inc(Q["all"], 1)
            pool.wait_ge(pos_ready, 1)
            nc.gpsimd.dma_start(bo_t[:, :], t["b_o"].to_broadcast([R, D])).then_inc(bo_in, 16)
            pool.wait_ge(tok_done, GROUPS * GT)
            nc.gpsimd.memset(Qz[:, :, :, :].rearrange("p s n r -> p (s n r)"), 0.0).then_inc(qz_clear, 1)
            nc.gpsimd.memset(V[:, :, :, HD:HD + 1], 1.0).then_inc(qz_clear, 1)
            ln_pool(pool, L1, 0)
            ln_pool(pool, L1, 1)
            pool.wait_ge(bo_in, 16)

            def bias_pool(i):
                pool.wait_ge(L1["xs"], L1["xs before"] + i + 1)
                for s in range(2):
                    nc.gpsimd.tensor_tensor(h[:, 2 * i + s, :], h[:, 2 * i + s, :], bo_t[:, :],
                                            ALU.add).then_inc(hb_done, 1)

            with pool.Fori(0, PAIRS - 1) as i:
                ln_pool(pool, L1, i + 2)
                bias_pool(i)
            bias_pool(PAIRS - 1)
            pool.wait_ge(resid_done, TILES)
            nc.gpsimd.memset(q1[:, :, D:2 * 128], 0.0).then_inc(F["clear"], 1)

            def root(k, call):
                pool.wait_ge(F[f"ssq{k + 1}"], 2 * call + 2)
                nc.gpsimd.tensor_tensor(rq[k][:, :], ss[k][:, :], eps_rms[:, :], ALU.add).then_inc(F[f"rq{k + 1}"], 1)
                pool.wait_ge(F[f"rq{k + 1}"], call + 1)
                nc.gpsimd.tensor_tensor(rms[k][:, :], rq[k][:, :], halfneg[:, :], ALU.pow
                                        ).then_inc(F[f"rms{k + 1}"], 1)

            for n in range(2):
                ln_pool(pool, L2, n)
                root(0, n)
            with pool.Fori(0, PAIRS - 1) as i:
                root(1, i)
                ln_pool(pool, L2, i + 2)
                root(0, i + 2)
            root(1, PAIRS - 1)

            pool.wait_ge(F["resid"], TILES)
            nc.gpsimd.memset(V1[:, :, :, HE:HE + 1], 1.0).then_inc(A1["clear"], 1)
            nc.gpsimd.memset(O1[:, :, D:256], 0.0).then_inc(A1["clear"], 1)
            pool.wait_ge(A1["const_in"], A1["const_in before"] + 160)
            ln_pool(pool, L3, 0)
            ln_pool(pool, L3, 1)

            def keys_pool(j):
                pool.wait_ge(A1["s"], A1["s before"] + 6 * j)
                for g in range(3):
                    pool.wait_ge(A1["ks"], A1["ks before"] + 6 * j + 2 * g + 2)
                    nc.gpsimd.tensor_tensor(KT1[:, g, :], kc[:, g, :], ks[:, g, :], ALU.add).then_inc(A1["kt"], 1)

            def weights_pool(i, s):
                pool.wait_ge(A1["wt"], A1["wt before"] + 2 * i + s + 1)
                pool.wait_ge(A1["pv"], A1["pv before"] + 2 * i)
                nc.gpsimd.tensor_tensor(
                    Pt1[:, s, :].rearrange("p (n i q) -> p n i q", n=NH, i=IPT),
                    wt1[:, s, :].rearrange("p (n q) -> p n q", n=NH).unsqueeze(2).to_broadcast([R, NH, IPT, S]),
                    causal[:, :].rearrange("p (i q) -> p i q", i=IPT).unsqueeze(1).to_broadcast([R, NH, IPT, S]),
                    ALU.mult).then_inc(A1["pt"], 1)

            keys_pool(0)
            with pool.Fori(0, PAIRS - 1) as i:
                ln_pool(pool, L3, i + 2)
                weights_pool(i, 0)
                keys_pool(i + 1)
                weights_pool(i, 1)
            weights_pool(PAIRS - 1, 0)
            weights_pool(PAIRS - 1, 1)
            pool.wait_ge(A1["resid"], A1["resid before"] + TILES)
            for n in range(4):
                ln_pool(pool, L4, n)
            with pool.Fori(0, PAIRS - 1) as i:
                ln_pool(pool, L4, 2 * i + 4)
                ln_pool(pool, L4, 2 * i + 5)
            pool.wait_ge(A2["resid"], A2["resid before"] + TILES)
            ln_pool(pool, L5, 0)
            with pool.Fori(0, PAIRS) as i:
                ln_pool(pool, L5, i + 1)
                nc.gpsimd.tensor_tensor(h[:, bass.ds(2 * i, 2), :], h[:, bass.ds(2 * i, 2), :],
                                        x1[:, bass.ds(2 * i, 2), :], ALU.add).then_inc(RT["streams"], 1)

        @block.tensor
        def _(pe):
            pe.wait_ge(ident_in, 16)
            with pe.Fori(0, GROUPS // 2) as i:
                for p in range(2):
                    pe.wait_ge(x_in[p], 16 * i + 16)
                    src = X[p][:, :].rearrange("p (k g w) -> p k g w", k=NK, g=GRID)
                    for k in range(NK):
                        for half in range(2):
                            n = 12 * p + 2 * k + half
                            if n < 4:
                                pe.wait_ge(pt_copied, 24 * i)
                            else:
                                pe.wait_ge(pt_copied, 24 * i + n - 3)
                            for j in range(3):
                                gw = 3 * half + j
                                tr = nc.tensor.transpose(ps[:, n % 4, j * GROWS:(j + 1) * GROWS],
                                                         src[0:GROWS, k, gw, :],
                                                         ident[0:GROWS, 0:GROWS])
                            tr.then_inc(pt_done, 1)
                pe.wait_ge(wtok_in, 16)
                for p in range(2):
                    pe.wait_ge(pt_copied, 24 * i + 12 * p + 12)
                    for m in range(GT):
                        n = GT * p + m
                        if n < 4:
                            pe.wait_ge(tok_h, 12 * i)
                        else:
                            pe.wait_ge(tok_h, 12 * i + n - 3)
                        for k in range(NK):
                            mm = nc.tensor.matmul(ps[0:R, 4 + n % 4, 0:D], PT[p][:, k, m * R:(m + 1) * R],
                                                  wtok[:, k, :], start=(k == 0), stop=(k == NK - 1))
                        mm.then_inc(tok_done, 1)
            pe.wait_ge(tok_h, TILES_ALL)
            pe.wait_ge(w1_ready, 1)
            pe.wait_ge(consts_ready, 1)
            pe.wait_ge(const_in, 48)
            pe.wait_ge(qz_clear, 2)
            pe.wait_ge(wo1_in, 16)

            def rows_in0(j):
                pe.wait_ge(L1["xs"], L1["xs before"] + j + 1)
                pe.wait_ge(v_copied, 4 * j)
                transposes(L1, 0, 6)
                transposes(L1, 1, 7)

            def queries_keys0(j):
                pe.wait_ge(tr_copied_dve, j + 1)
                pe.wait_ge(tr_copied_act, j + 1)
                for side in range(2):
                    pe.wait_ge(p_ready, 6 * j)
                    for g in range(3):
                        for n2 in range(2):
                            m = 6 * side + 2 * g + n2
                            for n, (x, wt) in enumerate(split5(wh1, wl1, 128 * m, 128 * m + 128)):
                                mm = nc.tensor.matmul(ps[:, 3 * side + g, n2 * R2:(n2 + 1) * R2], wt, xT[:, x, :],
                                                      start=(n == 0), stop=(n == 4))
                        mm.then_inc(qk_done, 1)

            def scores0(j, s):
                pe.wait_ge(q_copied, 12 * j + 12)
                pe.wait_ge(k_copied, 6 * j + 6)
                for b in range(3):
                    bank = 3 * s + b
                    nc.tensor.matmul(ps[0:R, bank, 0:4 * R], query_rows[:, 0, :], key_cols[:, :], start=True, stop=False)
                    for m in range(4):
                        n = 4 * b + m
                        mm = nc.tensor.matmul(ps[0:R, bank, m * R:(m + 1) * R], Qz[:, s, n, :],
                                              KT[:, n // 2, s * R:(s + 1) * R], start=False, stop=(m == 3))
                mm.then_inc(s_done, 1)

            def maxima0(j):
                pe.wait_ge(nmx_ready, 2 * j + 2)
                for s in range(2):
                    nc.tensor.transpose(ps[0:NH, 4 + s, 0:R], nmx[:, s, :], ident[0:R, 0:R]).then_inc(mt_done, 1)

            def values0(j, s):
                if s == 1:
                    pe.wait_ge(v_copied, 4 * j + 2)
                for b in range(2):
                    c = 2 * NH * HD + 384 * b
                    for n, (x, wt) in enumerate(split5(wh1, wl1, c, c + 384)):
                        mm = nc.tensor.matmul(ps[0:R, 6 + b, 0:384], xT[:, x, s * R:(s + 1) * R], wt,
                                              start=(n == 0), stop=(n == 4))
                    mm.then_inc(v_done, 1)

            def shifted0(i, s):
                pe.wait_ge(shift_ready, 2 * i + s + 1)
                pe.wait_ge(resid_done, 2 * i)
                for b in range(3):
                    bank = 3 * s + b
                    nc.tensor.matmul(ps[0:R, bank, 0:4 * R], key_rows[:, :],
                                     shift[s][:, b * 4 * R:(b + 1) * 4 * R], start=True, stop=False)
                    for m in range(2):
                        n = 4 * b + 2 * m
                        mm = nc.tensor.matmul(ps[0:R, bank, m * R2:(m + 1) * R2], KT[:, n // 2, s * R:(s + 1) * R],
                                              Qz[:, s, n:n + 2, :].rearrange("p n r -> p (n r)"),
                                              start=False, stop=(m == 1))
                    mm.then_inc(st_done, 1)

            def weighted0(i, s):
                pe.wait_ge(p_ready, 6 * i + 3 * s + 3)
                if s == 0:
                    pe.wait_ge(v_copied, 4 * i + 4)
                else:
                    pe.wait_ge(o_ready, 2 * i + 1)
                for b in range(2):
                    for m in range(6):
                        n = 6 * b + m
                        mm = nc.tensor.matmul(ps[0:R, 6 + b, m * (HD + 1):(m + 1) * (HD + 1)],
                                              Pt[:, s, n * R:(n + 1) * R], V[:, s, n, :], start=True, stop=True)
                    mm.then_inc(pv_done, 1)

            def outputs_turned0(i, s):
                pe.wait_ge(o_ready, 2 * i + 2)
                for b, (c0, c1) in enumerate(((0, 4), (4, 6))):
                    for c in range(c0, c1):
                        mm = nc.tensor.transpose(ps[:, (6, 0)[s] + b, (c - c0) * R:(c - c0 + 1) * R],
                                                 O[:, s, 128 * c:128 * c + 128], ident[0:R, 0:R])
                    mm.then_inc(ot_done, 1)

            def outputs0(i, s):
                pe.wait_ge(ot_copied, 4 * i + 2 * s + 2)
                for c in range(6):
                    mm = nc.tensor.matmul(ps[0:R, 2 + s, 0:D], OT[:, s, c, :], wo1[:, c, :],
                                          start=(c == 0), stop=(c == 5))
                mm.then_inc(op_done, 1)

            def attention0_tensor(i, ahead):
                shifted0(i, 0)
                if ahead:
                    rows_in0(i + 1)
                shifted0(i, 1)
                if ahead:
                    queries_keys0(i + 1)
                weighted0(i, 0)
                if ahead:
                    scores0(i + 1, 0)
                weighted0(i, 1)
                if ahead:
                    scores0(i + 1, 1)
                outputs_turned0(i, 0)
                if ahead:
                    pe.wait_ge(nmx_ready, 2 * i + 3)
                outputs_turned0(i, 1)
                if ahead:
                    maxima0(i + 1)
                outputs0(i, 0)
                if ahead:
                    values0(i + 1, 0)
                outputs0(i, 1)
                if ahead:
                    values0(i + 1, 1)

            rows_in0(0)
            queries_keys0(0)
            for s in range(2):
                scores0(0, s)
            maxima0(0)
            for s in range(2):
                values0(0, s)
            with pe.Fori(0, PAIRS - 1) as i:
                attention0_tensor(i, True)
            attention0_tensor(PAIRS - 1, False)
            pe.wait_ge(resid_done, TILES)
            pe.wait_ge(Q["ready"], 2)
            pe.wait_ge(consts_ready, 1)

            def rows_in(call, added):
                pe.wait_ge(F["q1"], call + 1)
                pe.wait_ge(F["resid"], added)
                for s in range(2):
                    for k in range(2):
                        tr = nc.tensor.transpose(psb[:, s, k * (R + 1):k * (R + 1) + R], q1[:, s, 128 * k:128 * k + 128],
                                                 identb[0:R, 0:R])
                    tr.then_inc(F["tr1"], 1)

            def up_tensor(j):
                pe.wait_ge(F["q1T"], 2 * j + 2)
                pe.wait_ge(F["z"], 2 * j)
                for s in range(2):
                    for part in range(2):
                        for k in range(2):
                            mm = nc.tensor.matmul(ps[0:R, 2 + 2 * s + part, :], q1T[:, s, k, 0:R],
                                                  wq_in[:, k, part * HF:(part + 1) * HF], start=(k == 0), stop=(k == 1))
                    mm.then_inc(F["up"], 1)

            def ffn_tensor(i, ahead):
                if ahead:
                    up_tensor(i + 1)
                pe.wait_ge(F["q2"], i + 1)
                pe.wait_ge(F["q2T"], 2 * i)
                for s in range(2):
                    for k in range(4):
                        tr = nc.tensor.transpose(psb[:, 6 + s, k * (R + 1):k * (R + 1) + R],
                                                 q2[:, s, 128 * k:128 * k + 128], identb[0:R, 0:R])
                    tr.then_inc(F["tr2"], 1)
                pe.wait_ge(F["q1T"], 2 * PAIRS + 2 if not ahead else 2 * i + 4)
                for s in range(2):
                    pe.wait_ge(F["q2T"], 2 * i + s + 1)
                    for k in range(4):
                        mm = nc.tensor.matmul(ps[0:R, s, 0:D], q2T[:, s, k, 0:R], wq_out[:, k, :],
                                              start=(k == 0), stop=(k == 3))
                    mm.then_inc(F["down"], 1)
                if ahead:
                    rows_in(i + 2, 2 * i + 2)

            rows_in(0, 0)
            up_tensor(0)
            rows_in(1, 0)
            with pe.Fori(0, PAIRS - 1) as i:
                ffn_tensor(i, True)
            ffn_tensor(PAIRS - 1, False)

            pe.wait_ge(F["resid"], TILES)
            pe.wait_ge(F["q1T"], 2 * (PAIRS + 1))
            pe.wait_ge(w3_ready, PAIRS)
            pe.wait_ge(A1["const_in"], A1["const_in before"] + 160)
            pe.wait_ge(A1["clear"], A1["clear before"] + 2)

            def project(c, bank, o):
                for n, (k, wt) in enumerate(split5(wh3, wl3, c, c + 128)):
                    mm = nc.tensor.matmul(ps[:, bank, o:o + R2], wt, xT[:, k, :], start=(n == 0), stop=(n == 4))
                return mm

            def rows_in1(L, A, j, banks):
                pe.wait_ge(L["xs"], L["xs before"] + j + 1)
                pe.wait_ge(A["v_out"], A["v_out before"] + 2 * j)
                transposes(L, 0, banks[0])
                transposes(L, 1, banks[1])

            def values(A, c, bank):
                for s in range(2):
                    for n, (k, wt) in enumerate(split5(wh3, wl3, c, c + D)):
                        mm = nc.tensor.matmul(ps[0:R, bank + s, 0:D], xT[:, k, s * R:(s + 1) * R], wt,
                                              start=(n == 0), stop=(n == 4))
                    mm.then_inc(A["v"], 1)

            def pv_products(A, i, s):
                pe.wait_ge(A["v_out"], A["v_out before"] + 2 * i + 2)
                pe.wait_ge(A["resid"], A["resid before"] + 2 * i)
                for n in range(NH):
                    mm = nc.tensor.matmul(ps[0:R, 6 + s, n * (HE + 1):(n + 1) * (HE + 1)], Pt1[:, s, n * R:(n + 1) * R],
                                          V1[:, s, n, :], start=True, stop=True)
                mm.then_inc(A["pv"], 1)

            def project_out(A, i, layer, between=None):
                for s in range(2):
                    pe.wait_ge(A["o"], A["o before"] + 2 * i + s + 1)
                    for c in range(2):
                        tr = nc.tensor.transpose(ps[:, 6 + s, c * R:(c + 1) * R], O1[:, s, 128 * c:128 * c + 128],
                                                 ident[0:R, 0:R])
                    tr.then_inc(A["ot"], 1)
                if between:
                    between()
                for s in range(2):
                    pe.wait_ge(A["ot_out"], A["ot_out before"] + 2 * i + s + 1)
                    for c in range(2):
                        mm = nc.tensor.matmul(ps[0:R, 6 + s, 256:256 + D], OT1[:, s, c, :], proj[:, layer, c, :],
                                              start=(c == 0), stop=(c == 1))
                    mm.then_inc(A["op"], 1)

            def queries_keys(j):
                pe.wait_ge(A1["tr_dve"], A1["tr_dve before"] + j + 1)
                pe.wait_ge(A1["tr_act"], A1["tr_act before"] + j + 1)
                for g in range(3):
                    project(128 * g, g, 0).then_inc(A1["q"], 1)
                    project(384 + 128 * g, 3 + g, 0)
                    project(768 + 128 * g, 3 + g, R2).then_inc(A1["k"], 1)
                for s in range(2):
                    for b in range(3):
                        if s == 0:
                            pe.wait_ge(A1["qz"], A1["qz before"] + 3 * j + b + 1)
                            pe.wait_ge(A1["kt"], A1["kt before"] + 3 * j + b + 1)
                        nc.tensor.matmul(ps[0:R, 3 * s + b, :].rearrange("p (n r) -> p n r", n=4)[:, :, 0:R],
                                         KT1[:, b, s * R:(s + 1) * R], Qz1[:, s, 4 * b:4 * b + 4, :],
                                         start=True, stop=True).then_inc(A1["s"], 1)

            def attention1_tensor(i, ahead):
                if ahead:
                    rows_in1(L3, A1, i + 1, (2, 3))
                    queries_keys(i + 1)
                for s in range(2):
                    pe.wait_ge(A1["pt"], A1["pt before"] + 2 * i + s + 1)
                    pv_products(A1, i, s)
                if ahead:
                    pe.wait_ge(A1["own"], A1["own before"] + 6 * i + 12)
                    values(A1, W34 - D, 4)
                project_out(A1, i, 0)

            rows_in1(L3, A1, 0, (2, 3))
            queries_keys(0)
            pe.wait_ge(A1["own"], A1["own before"] + 6)
            values(A1, W34 - D, 4)
            with pe.Fori(0, PAIRS - 1) as i:
                attention1_tensor(i, True)
            attention1_tensor(PAIRS - 1, False)
            pe.wait_ge(A1["resid"], A1["resid before"] + TILES)
            pe.wait_ge(A2["copied"], A2["copied before"] + 2)

            def project_rows(j):
                if not isinstance(j, int) or j > 0:
                    pe.wait_ge(A2["p"], A2["p before"] + 6 * j - 3)
                for g in range(3):
                    project(W34 + 128 * g, g, 0).then_inc(A2["q"], 1)
                pe.wait_ge(A2["p"], A2["p before"] + 6 * j)
                for g in range(3):
                    project(W34 + 384 + 128 * g, 3 + g, 0).then_inc(A2["k"], 1)

            def scores_for_maximum(j):
                pe.wait_ge(A2["qz"], A2["qz before"] + 3 * j + 3)
                pe.wait_ge(A2["kt"], A2["kt before"] + 3 * j + 3)
                for s in range(2):
                    for b in range(3):
                        nc.tensor.matmul(ps[0:R, 3 * s + b, 0:4 * R], query_rows[:, 1, :], key_cols[:, :],
                                         start=True, stop=False)
                        for n in range(4):
                            mm = nc.tensor.matmul(ps[0:R, 3 * s + b, n * R:(n + 1) * R], Qz1[:, s, 4 * b + n, :],
                                                  KT1[:, b, s * R:(s + 1) * R], start=False, stop=(n == 3))
                    mm.then_inc(A2["s"], 1)

            def maxima(j):
                for s in range(2):
                    pe.wait_ge(A2["nmx"], A2["nmx before"] + 2 * j + s + 1)
                    nc.tensor.transpose(ps[0:NH, 3 * s, 0:R], nmx[:, s, :], ident[0:R, 0:R]).then_inc(A2["mt"], 1)

            def attention2_tensor(i, ahead):
                for s in range(2):
                    if s == 1 and ahead:
                        rows_in1(L4, A2, i + 1, (6, 7))
                    pe.wait_ge(A2["shift"], A2["shift before"] + 2 * i + s + 1)
                    for b in range(3):
                        nc.tensor.matmul(ps[0:R, 3 * s + b, 0:4 * R], key_rows[:, :],
                                         shift[s][:, b * 4 * R:(b + 1) * 4 * R], start=True, stop=False)
                        nc.tensor.matmul(ps[0:R, 3 * s + b, 0:4 * R], KT1[:, b, s * R:(s + 1) * R],
                                         Qz1[:, s, 4 * b:4 * b + 4, :].rearrange("p n r -> p (n r)"),
                                         start=False, stop=True).then_inc(A2["st"], 1)
                if ahead:
                    pe.wait_ge(A2["tr_dve"], A2["tr_dve before"] + i + 2)
                    pe.wait_ge(A2["tr_act"], A2["tr_act before"] + i + 2)
                    project_rows(i + 1)
                for s in range(2):
                    pe.wait_ge(A2["p"], A2["p before"] + 6 * i + 3 * s + 3)
                    pv_products(A2, i, s)
                if ahead:
                    scores_for_maximum(i + 1)
                project_out(A2, i, 1, (lambda: maxima(i + 1)) if ahead else None)
                if ahead:
                    pe.wait_ge(A2["resid"], A2["resid before"] + 2 * i + 2)
                    values(A2, WCOLS - D, 6)

            rows_in1(L4, A2, 0, (6, 7))
            pe.wait_ge(A2["tr_dve"], A2["tr_dve before"] + 1)
            pe.wait_ge(A2["tr_act"], A2["tr_act before"] + 1)
            project_rows(0)
            scores_for_maximum(0)
            maxima(0)
            values(A2, WCOLS - D, 6)
            with pe.Fori(0, PAIRS - 1) as i:
                attention2_tensor(i, True)
            attention2_tensor(PAIRS - 1, False)
            pe.wait_ge(A2["resid"], A2["resid before"] + TILES)
            pe.wait_ge(RT["split"], 1)
            with pe.Fori(0, PAIRS) as i:
                pe.wait_ge(L5["xs"], L5["xs before"] + i + 1)
                pe.wait_ge(RT["xm1"], i)
                pe.wait_ge(RT["xm2"], i)
                transposes(L5, 0, 0)
                transposes(L5, 1, 1)
                pe.wait_ge(RT["tr_dve"], i + 1)
                pe.wait_ge(RT["tr_act"], i + 1)
                pe.wait_ge(RT["raw"], 2 * i)
                for s in range(2):
                    for n, (k, wt) in enumerate(split5(router_h, router_l, 0, E)):
                        mm = nc.tensor.matmul(ps[0:R, 2 + s, 0:E], xT[:, k, s * R:(s + 1) * R], wt,
                                              start=(n == 0), stop=(n == 4))
                    mm.then_inc(RT["logits"], 1)
            pe.wait_ge(RT["raw"], TILES)
            pe.wait_ge(RT["xm1"], PAIRS)
            pe.wait_ge(RT["xm2"], PAIRS)

            def experts_tensor(e, q, c, tiles):
                base = 36 * e + 6 * c
                cols = tiles * R
                at = c * (E_CHUNK * R)
                pe.wait_ge(EX["lo"], 12 * e + 12)
                for step in range(FM + 2):
                    if step < FM:
                        m = step
                        if m < 4:
                            pe.wait_ge(EX["gelu"], base)
                        else:
                            pe.wait_ge(EX["gelu"], base + m - 3)
                        for n, (k, wt) in enumerate(split5(eh1[q], el1[q], 128 * m, 128 * m + 128)):
                            mm = nc.tensor.matmul(ps[:, m % 4, 0:cols], wt, xTm[:, k, bass.ds(at, cols)],
                                                  start=(n == 0), stop=(n == 4))
                        mm.then_inc(EX["half"], 1)
                    if step >= 2:
                        k = step - 2
                        pe.wait_ge(EX["gl"], base + k + 1)
                        if k == 0:
                            pe.wait_ge(EX["acc"], TILES * e + 4 * c)
                        for tt in range(tiles):
                            rows = slice(tt * R, (tt + 1) * R)
                            nc.tensor.matmul(ps[0:R, 4 + tt, 0:D], gh[:, k, rows], eh2[q][:, k, :],
                                             start=(k == 0), stop=False)
                            nc.tensor.matmul(ps[0:R, 4 + tt, 0:D], gh[:, k, rows], el2[q][:, k, :],
                                             start=False, stop=False)
                            mm = nc.tensor.matmul(ps[0:R, 4 + tt, 0:D], gl[:, k, rows], eh2[q][:, k, :],
                                                  start=False, stop=(k == FM - 1))
                            if k == FM - 1:
                                mm.then_inc(EX["down"], 1)

            with pe.Fori(0, E // 2) as pair:
                for q in range(2):
                    with pe.Fori(0, TILES // E_CHUNK) as c:
                        experts_tensor(2 * pair + q, q, c, E_CHUNK)
                    experts_tensor(2 * pair + q, q, TILES // E_CHUNK, TILES % E_CHUNK)

        @block.scalar
        def _(act):
            act.wait_ge(cleared, 3)
            with act.Fori(0, GROUPS // 2) as i:
                for p in range(2):
                    for k in range(NK):
                        for half in range(2):
                            n = 12 * p + 2 * k + half
                            act.wait_ge(pt_done, 24 * i + n + 1)
                            slots = PT[p][:, k, :].rearrange("p (b s) -> p b s", s=S)[:, :, 1:S]
                            slots = slots.rearrange("p b (g w) -> p w b g", w=GRID)
                            nc.scalar.copy(slots[:, 3 * half:3 * half + 3, :, :],
                                           ps[:, n % 4, 0:3 * GROWS].rearrange("p (w b g) -> p w b g", w=3, b=GI)
                                           ).then_inc(pt_copied, 1)
            act.wait_ge(pos_in, 16 * (IPT + 3))
            act.wait_ge(qz_clear, 1)

            def transposed0(j):
                act.wait_ge(L1["tr"], L1["tr before"] + 2 * j + 2)
                act.wait_ge(v_done, 4 * j)
                nc.scalar.copy(xT[:, :, R:R2], ps[:, 7, 0:3 * R].rearrange("p (c r) -> p c r", c=3)
                               ).then_inc(tr_copied_act, 1)

            def queries0(j):
                act.wait_ge(st_done, 6 * j)
                for g in range(3):
                    act.wait_ge(qk_done, 6 * j + g + 1)
                    for n2 in range(2):
                        for hh in range(2):
                            n = 4 * g + 2 * n2 + hh
                            rows = slice(64 * hh, 64 * hh + 64)
                            nc.scalar.activation(Qz[rows, :, n, :],
                                                 ps[rows, g, n2 * R2:(n2 + 1) * R2].rearrange("p (s r) -> p s r", s=2),
                                                 ACT.Identity, bias=bqk[rows, n // 2:n // 2 + 1]).then_inc(q_copied, 1)

            def attention0_scalar(i, ahead):
                act.wait_ge(pv_done, 4 * i)
                for s in range(2):
                    for b in range(3):
                        act.wait_ge(st_done, 6 * i + 3 * s + b + 1)
                        nc.scalar.activation(Pt[:, s, b * 4 * R:(b + 1) * 4 * R], ps[0:R, 3 * s + b, 0:4 * R],
                                             ACT.Exp, scale=float(HD) ** -0.5).then_inc(p_ready, 1)
                    if s == 0 and ahead:
                        transposed0(i + 1)
                if ahead:
                    queries0(i + 1)
                for s in range(2):
                    for b, (c0, c1) in enumerate(((0, 4), (4, 6))):
                        act.wait_ge(ot_done, 4 * i + 2 * s + b + 1)
                        nc.scalar.copy(OT[:, s, c0:c1, :],
                                       ps[:, (6, 0)[s] + b, 0:(c1 - c0) * R].rearrange(
                                           "p (c r) -> p c r", r=R)).then_inc(ot_copied, 1)

            transposed0(0)
            queries0(0)
            with act.Fori(0, PAIRS - 1) as i:
                attention0_scalar(i, True)
            attention0_scalar(PAIRS - 1, False)
            act.wait_ge(resid_done, TILES)
            act.wait_ge(F["clear"], 1)

            def rows_act(call):
                for s in range(2):
                    act.wait_ge(L2["y"], L2["y before"] + 2 * call + s + 1)
                    act.wait_ge(F["ssq1"], 2 * call)
                    nc.scalar.activation(junk1[:, s, :], yn[:, s, :], ACT.Square, scale=float(D) ** -0.5,
                                         accum_out=ss[0][:, s:s + 1]
                                         ).then_inc(F["ssq1"], 1)

            def rows_round(call):
                act.wait_ge(F["small1"], 2 * call + 2)
                act.wait_ge(F["q1"], call)
                for s in range(2):
                    nc.scalar.activation(t1[:, s, :], xn[:, s, :], ACT.Identity, bias=magic[:, :],
                                         scale=qscale[0][:, s:s + 1]).then_inc(F["t1"], 1)

            def rows_out(call):
                act.wait_ge(F["up"], 2 * call)
                for s in range(2):
                    act.wait_ge(F["tr1"], 2 * call + s + 1)
                    nc.scalar.copy(q1T[:, s, :, 0:R], psb[:, s, 0:2 * (R + 1)].rearrange("p (k r) -> p k r", k=2)[:, :, 0:R]
                                   ).then_inc(F["q1T"], 1)

            def gates(j):
                for s in range(2):
                    act.wait_ge(F["up"], 2 * j + s + 1)
                    act.wait_ge(F["z"], 2 * j)
                    nc.scalar.activation(sg[:, s, :], ps[0:R, 3 + 2 * s, :], ACT.Silu, scale=dscale[0][:, s:s + 1]
                                         ).then_inc(F["sg"], 1)

            def ffn_scalar(i, ahead):
                act.wait_ge(F["ssq2"], 2 * i)
                for s in range(2):
                    act.wait_ge(F["z"], 2 * i + s + 1)
                    nc.scalar.activation(junk2[:, s, :], z[:, s, :], ACT.Square, scale=float(HF) ** -0.5,
                                         accum_out=ss[1][:, s:s + 1]).then_inc(F["ssq2"], 1)
                if ahead:
                    gates(i + 1)
                act.wait_ge(F["small2"], 2 * i + 2)
                act.wait_ge(F["q2"], i)
                for s in range(2):
                    nc.scalar.activation(t2[:, s, :], zn[:, s, :], ACT.Identity, bias=magic[:, :],
                                         scale=qscale[1][:, s:s + 1]).then_inc(F["t2"], 1)
                if ahead:
                    rows_act(i + 2)
                act.wait_ge(F["down"], 2 * i)
                for s in range(2):
                    act.wait_ge(F["tr2"], 2 * i + s + 1)
                    nc.scalar.copy(q2T[:, s, :, 0:R], psb[:, 6 + s, 0:4 * (R + 1)].rearrange("p (k r) -> p k r", k=4)
                                   [:, :, 0:R]).then_inc(F["q2T"], 1)
                if ahead:
                    rows_round(i + 2)
                    rows_out(i + 2)

            rows_act(0)
            rows_round(0)
            rows_out(0)
            rows_act(1)
            gates(0)
            rows_round(1)
            rows_out(1)
            with act.Fori(0, PAIRS - 1) as i:
                ffn_scalar(i, True)
            ffn_scalar(PAIRS - 1, False)

            act.wait_ge(F["resid"], TILES)
            act.wait_ge(A1["clear"], A1["clear before"] + 2)

            def transposed_act(L, A, j, bank=7):
                act.wait_ge(L["tr"], L["tr before"] + 2 * j + 2)
                act.wait_ge(A["v"], A["v before"] + 2 * j)
                nc.scalar.copy(xT[:, :, R:R2], ps[:, bank, 0:3 * R].rearrange("p (c r) -> p c r", c=3)
                               ).then_inc(A["tr_act"], 1)

            def values_act(A, j, bank=6):
                act.wait_ge(A["pv"], A["pv before"] + 2 * j)
                for s in range(2):
                    act.wait_ge(A["v"], A["v before"] + 2 * j + s + 1)
                    nc.scalar.copy(V1[:, s, :, 0:HE], ps[0:R, bank + s, 0:D].rearrange("p (n e) -> p n e", n=NH)
                                   ).then_inc(A["v_out"], 1)

            def outputs_act(A, i):
                act.wait_ge(A["op"], A["op before"] + 2 * i)
                for s in range(2):
                    act.wait_ge(A["ot"], A["ot before"] + 2 * i + s + 1)
                    nc.scalar.copy(OT1[:, s, :, :], ps[:, 6 + s, 0:R2].rearrange("p (c r) -> p c r", c=2)
                                   ).then_inc(A["ot_out"], 1)

            def attention1_act(i, ahead):
                for s in range(2):
                    act.wait_ge(A1["own"], A1["own before"] + 6 * i + 3 * s + 3)
                    act.wait_ge(A1["wt"], A1["wt before"] + 2 * i)
                    nc.scalar.activation(gel[:, s, :], own[:, s, :], ACT.Gelu, scale=2.0 ** 0.5 * float(HE) ** -0.5
                                         ).then_inc(A1["gel"], 1)
                if ahead:
                    transposed_act(L3, A1, i + 1, 3)
                    values_act(A1, i + 1, 4)
                outputs_act(A1, i)

            transposed_act(L3, A1, 0, 3)
            values_act(A1, 0, 4)
            with act.Fori(0, PAIRS - 1) as i:
                attention1_act(i, True)
            attention1_act(PAIRS - 1, False)
            act.wait_ge(A1["resid"], A1["resid before"] + TILES)

            def keys_act(j):
                act.wait_ge(A2["st"], A2["st before"] + 6 * j)
                for g in range(3):
                    act.wait_ge(A2["k"], A2["k before"] + 3 * j + g + 1)
                    nc.scalar.copy(KT1[:, g, :], ps[:, 3 + g, 0:R2]).then_inc(A2["kt"], 1)

            def attention2_act(i, ahead):
                act.wait_ge(A2["pv"], A2["pv before"] + 2 * i)
                for s in range(2):
                    for b in range(3):
                        act.wait_ge(A2["st"], A2["st before"] + 6 * i + 3 * s + b + 1)
                        nc.scalar.activation(Pt1[:, s, b * 4 * R:(b + 1) * 4 * R], ps[0:R, 3 * s + b, 0:4 * R],
                                             ACT.Exp, scale=float(HE) ** -0.5).then_inc(A2["p"], 1)
                    if s == 0 and ahead:
                        transposed_act(L4, A2, i + 1)
                if ahead:
                    keys_act(i + 1)
                outputs_act(A2, i)
                if ahead:
                    values_act(A2, i + 1)

            transposed_act(L4, A2, 0)
            keys_act(0)
            values_act(A2, 0)
            with act.Fori(0, PAIRS - 1) as i:
                attention2_act(i, True)
            attention2_act(PAIRS - 1, False)
            act.wait_ge(A2["resid"], A2["resid before"] + TILES)
            with act.Fori(0, PAIRS) as i:
                act.wait_ge(L5["tr"], L5["tr before"] + 2 * i + 2)
                act.wait_ge(RT["logits"], 2 * i)
                src = ps[:, 1, 0:3 * R].rearrange("p (c r) -> p c r", c=3)
                nc.scalar.copy(xT[:, :, R:R2], src).then_inc(RT["tr_act"], 1)
                nc.scalar.copy(xTm[:, :, bass.ds(i * R2 + R, R)], src).then_inc(RT["xm2"], 1)
            act.wait_ge(RT["k2"], 1)
            nc.scalar.activation(pr[:, 1, :], pr[:, 0, :], ACT.Exp).then_inc(RT["ex"], 1)
            def experts_scalar(e, c, tiles):
                base = 36 * e + 6 * c
                for m in range(FM):
                    act.wait_ge(EX["half"], base + m + 1)
                    if m < 2:
                        act.wait_ge(EX["gl"], base)
                    else:
                        act.wait_ge(EX["gl"], base + m - 1)
                    nc.scalar.activation(graw[:, m % 2, 0:tiles * R], ps[:, m % 4, 0:tiles * R], ACT.Gelu
                                         ).then_inc(EX["gelu"], 1)

            act.wait_ge(A2["resid"], A2["resid before"] + TILES)
            with act.Fori(0, E) as e:
                with act.Fori(0, TILES // E_CHUNK) as c:
                    experts_scalar(e, c, E_CHUNK)
                experts_scalar(e, TILES // E_CHUNK, TILES % E_CHUNK)

        @block.vector
        def _(dve):
            nc.vector.memset(h[:, TILES:TILES_ALL, :], 0.0).then_inc(chain, 1)
            dve.wait_ge(w1_in, 16)
            nc.vector.tensor_copy(wh1[:, :, :], stage1[:, :, :]).then_inc(w1_hi, 1)
            dve.wait_ge(w1_hi, 1)
            nc.vector.tensor_tensor(wl1[:, :, :], stage1[:, :, :], wh1[:, :, :].bitcast(F32),
                                    ALU.subtract).then_inc(w1_ready, 1)
            dve.wait_ge(Q["in"], 32)
            for n, src in enumerate((win_in, wout_in)):
                nc.vector.tensor_reduce(wsum[:, n:n + 1], src[:, :, :], AX.XY, ALU.add, apply_absolute_value=True
                                        ).then_inc(Q["summed"], 1)
            dve.wait_ge(Q["all"], 1)
            for n, size in enumerate((2 * HF * D, HF * D)):
                nc.vector.tensor_scalar(wmean[:, n:n + 1], wall[:, n:n + 1], 1.0 / size, 1e-5, ALU.mult, ALU.max
                                        ).then_inc(Q["step"], 1)
            dve.wait_ge(Q["step"], 2)
            nc.vector.reciprocal(wrec[:, :], wmean[:, :]).then_inc(Q["step"], 1)
            nc.vector.tensor_scalar(w127[:, :], wmean[:, :], 1.0 / 127.0, None, ALU.mult).then_inc(Q["step"], 1)
            dve.wait_ge(Q["step"], 4)
            for n, src in enumerate((win_in, wout_in)):
                nc.vector.tensor_scalar(src[:, :, :], src[:, :, :], wrec[:, n:n + 1], MAGIC, ALU.mult, ALU.add
                                        ).then_inc(Q["step"], 1)
            dve.wait_ge(Q["step"], 6)
            for n, src in enumerate((win_in, wout_in)):
                nc.vector.tensor_scalar(src[:, :, :], src[:, :, :], MAGIC, 1.0, ALU.subtract, ALU.min
                                        ).then_inc(Q["step"], 1)
            dve.wait_ge(Q["step"], 8)
            for src, dst in ((win_in, wq_in), (wout_in, wq_out)):
                nc.vector.tensor_scalar(dst[:, :, :], src[:, :, :], -1.0, None, ALU.max).then_inc(Q["ready"], 1)
            dve.wait_ge(const_in, 48)
            nc.vector.tensor_copy(identb[:, :], ident[:, :]).then_inc(consts_copied, 1)
            nc.vector.tensor_copy(key_rows[:, :], mask_in[:, 0:R]).then_inc(consts_copied, 1)
            nc.vector.tensor_copy(query_rows[:, :, :], mask_in[:, R:3 * R].rearrange("p (a r) -> p a r", a=2)
                                  ).then_inc(consts_copied, 1)
            nc.vector.tensor_copy(key_cols[:, :], mask_in[:, 3 * R:7 * R]).then_inc(consts_copied, 1)
            for s in range(2):
                nc.vector.tensor_copy(shift[s][:, :].rearrange("p (n r) -> p n r", n=NH),
                                      shift_in[:, 0, :].unsqueeze(1).to_broadcast([MK, NH, R])
                                      ).then_inc(consts_copied, 1)
            dve.wait_ge(consts_copied, 6)
            dve.wait_ge(pos_in, 16 * (IPT + 3))
            nc.vector.tensor_tensor(posb[:, :], posb[:, :], bo_t[:, :], ALU.add).then_inc(pos_ready, 1)
            dve.wait_ge(pos_ready, 1)
            dve.wait_ge(chain, 1)
            with dve.Fori(0, GROUPS // 2) as i:
                for n in range(2 * GT):
                    dve.wait_ge(tok_done, 12 * i + n + 1)
                    nc.vector.tensor_tensor(h[:, 2 * GT * i + n, :], ps[0:R, 4 + n % 4, 0:D], posb[:, :],
                                            ALU.add).then_inc(tok_h, 1)
            nc.vector.memset(mv[0:1, 0, 0:1], 0.0).then_inc(consts_ready, 1)
            dve.wait_ge(consts_ready, 1)
            dve.wait_ge(tok_h, TILES_ALL)
            dve.wait_ge(cleared, 6)

            def transposed0(j):
                dve.wait_ge(L1["tr"], L1["tr before"] + 2 * j + 1)
                dve.wait_ge(v_done, 4 * j)
                nc.vector.tensor_copy(xT[:, :, 0:R], ps[:, 6, 0:3 * R].rearrange("p (c r) -> p c r", c=3)
                                      ).then_inc(tr_copied_dve, 1)

            def keys0(j):
                dve.wait_ge(st_done, 6 * j)
                for g in range(3):
                    dve.wait_ge(qk_done, 6 * j + g + 4)
                    for n2 in range(2):
                        m = 2 * g + n2
                        nc.vector.tensor_scalar(KT[:, m, :], ps[:, 3 + g, n2 * R2:(n2 + 1) * R2], bqk[:, 6 + m:7 + m],
                                                None, ALU.add).then_inc(k_copied, 1)

            def values0(j, s):
                dve.wait_ge(pv_done, 4 * j)
                for b in range(2):
                    dve.wait_ge(v_done, 4 * j + 2 * s + b + 1)
                    nc.vector.tensor_tensor(V[:, s, 6 * b:6 * b + 6, 0:HD],
                                            ps[0:R, 6 + b, 0:384].rearrange("p (n e) -> p n e", n=6),
                                            bv_t[:, 384 * b:384 * b + 384].rearrange("p (n e) -> p n e", n=6),
                                            ALU.add).then_inc(v_copied, 1)

            def maximum0(j, s):
                dve.wait_ge(s_done, 2 * j + s + 1)
                dve.wait_ge(mt_done, 2 * j)
                nc.vector.tensor_reduce(nmx[:, s, :],
                                        ps[0:R, 3 * s:3 * s + 3, 0:4 * R].rearrange("p b (n r) -> p b n r", n=4),
                                        AX.X, ALU.max, negate=True).then_inc(nmx_ready, 1)

            def spread0(j, s):
                dve.wait_ge(mt_done, 2 * j + s + 1)
                dve.wait_ge(st_done, 6 * j)
                nc.vector.tensor_tensor(shift[s][0:NH, :].rearrange("p (n r) -> p n r", n=NH),
                                        ps[0:NH, 4 + s, 0:R].unsqueeze(1).to_broadcast([NH, NH, R]),
                                        sel12[:, :].rearrange("p (n r) -> p n r", n=NH),
                                        ALU.mult).then_inc(shift_ready, 1)

            def split_weights(i):
                cols = bass.ds(i * WSTEP, WSTEP)
                nc.vector.tensor_copy(wh3[:, :, cols], wst3[:, :, cols]).then_inc(w3_hi, 1)
                dve.wait_ge(w3_hi, i + 1)
                nc.vector.tensor_tensor(wl3[:, :, cols], wst3[:, :, cols], wh3[:, :, cols].bitcast(F32),
                                        ALU.subtract).then_inc(w3_ready, 1)

            def normalise0(i, s):
                heads = ps[0:R, 6:8, 0:6 * (HD + 1)].rearrange("p b (n e) -> p b n e", n=6)
                dve.wait_ge(pv_done, 4 * i + 2 * s + 2)
                nc.vector.reciprocal(rden[:, s, :].rearrange("p (b n) -> p b n", b=2),
                                     heads[:, :, :, HD]).then_inc(rden_ready, 1)
                dve.wait_ge(rden_ready, 2 * i + s + 1)
                dve.wait_ge(ot_done, 4 * i)
                nc.vector.tensor_tensor(O[:, s, :].rearrange("p (b n e) -> p b n e", b=2, n=6),
                                        heads[:, :, :, 0:HD],
                                        rden[:, s, :].rearrange("p (b n) -> p b n", b=2).unsqueeze(3)
                                        .to_broadcast([R, 2, 6, HD]), ALU.mult).then_inc(o_ready, 1)

            def residual0(i, s):
                dve.wait_ge(hb_done, 2 * i + 2)
                dve.wait_ge(op_done, 2 * i + s + 1)
                nc.vector.tensor_tensor(h[:, 2 * i + s, :], ps[0:R, 2 + s, 0:D], h[:, 2 * i + s, :],
                                        ALU.add).then_inc(resid_done, 1)

            def rows0(j):
                dve.wait_ge(L1["y"], L1["y before"] + 2 * j + 2)
                split_vector(dve, L1, j, yn)

            def attention0_vector(i, ahead):
                if ahead:
                    ln_vector(dve, L1, i + 2)
                    transposed0(i + 1)
                    rows0(i + 2)
                split_weights(i)
                if ahead:
                    keys0(i + 1)
                normalise0(i, 0)
                normalise0(i, 1)
                if ahead:
                    maximum0(i + 1, 0)
                    maximum0(i + 1, 1)
                    spread0(i + 1, 0)
                    spread0(i + 1, 1)
                residual0(i, 0)
                if ahead:
                    values0(i + 1, 0)
                residual0(i, 1)
                if ahead:
                    values0(i + 1, 1)

            ln_vector(dve, L1, 0)
            rows0(0)
            transposed0(0)
            ln_vector(dve, L1, 1)
            rows0(1)
            dve.wait_ge(w3_in, 16)
            dve.wait_ge(qz_clear, 2)
            keys0(0)
            for s in range(2):
                maximum0(0, s)
            for s in range(2):
                spread0(0, s)
            for s in range(2):
                values0(0, s)
            with dve.Fori(0, PAIRS - 1) as i:
                attention0_vector(i, True)
            attention0_vector(PAIRS - 1, False)
            dve.wait_ge(resid_done, TILES)
            dve.wait_ge(F["gain_in"], 32)
            dve.wait_ge(F["clear"], 2)

            def largest(k, call, rows):
                nc.vector.tensor_reduce(amax[k][:, :], rows, AX.X, ALU.max, apply_absolute_value=True
                                        ).then_inc(F[f"amax{k + 1}"], 1)

            def scales(k, call):
                dve.wait_ge(F[f"rms{k + 1}"], call + 1)
                dve.wait_ge(F[f"amax{k + 1}"], call + 1)
                for s in range(2):
                    nc.vector.tensor_scalar(amaxc[k][:, s:s + 1], amax[k][:, s:s + 1], rms[k][:, s:s + 1], 1e-5,
                                            ALU.mult, ALU.max).then_inc(F[f"amaxc{k + 1}"], 1)
                dve.wait_ge(F[f"amaxc{k + 1}"], 2 * call + 2)
                nc.vector.reciprocal(arec[k][:, :], amaxc[k][:, :]).then_inc(F[f"arec{k + 1}"], 1)
                nc.vector.tensor_scalar(dscale[k][:, :], amaxc[k][:, :], w127[0:R, k:k + 1], None, ALU.mult
                                        ).then_inc(F[f"small{k + 1}"], 1)
                dve.wait_ge(F[f"arec{k + 1}"], call + 1)
                nc.vector.scalar_tensor_tensor(qscale[k][:, :], arec[k][:, :], 127.0, rms[k][:, :], ALU.mult, ALU.mult
                                               ).then_inc(F[f"small{k + 1}"], 1)

            def rows_scaled(call):
                dve.wait_ge(L2["y"], L2["y before"] + 2 * call + 2)
                nc.vector.tensor_tensor(xn[:, :, :], yn[:, :, :], g_in[:, :].unsqueeze(1).to_broadcast([R, 2, D]),
                                        ALU.mult).then_inc(F["xn"], 1)
                dve.wait_ge(F["xn"], call + 1)
                largest(0, call, xn[:, :, :])

            def rows_integer(call):
                dve.wait_ge(F["t1"], 2 * call + 2)
                dve.wait_ge(F["tr1"], 2 * call)
                nc.vector.tensor_scalar(q1[:, :, 0:D], t1[:, :, :], MAGIC, 127.0, ALU.subtract, ALU.min
                                        ).then_inc(F["q1"], 1)

            def gated(j):
                dve.wait_ge(F["ssq2"], 2 * j)
                for s in range(2):
                    dve.wait_ge(F["sg"], 2 * j + s + 1)
                    nc.vector.scalar_tensor_tensor(z[:, s, :], ps[0:R, 2 + 2 * s, :], dscale[0][:, s:s + 1], sg[:, s, :],
                                                   ALU.mult, ALU.mult).then_inc(F["z"], 1)

            def ffn_vector(i, ahead):
                dve.wait_ge(F["z"], 2 * i + 2)
                nc.vector.tensor_tensor(zn[:, :, :], z[:, :, :], g_out[:, :].unsqueeze(1).to_broadcast([R, 2, HF]),
                                        ALU.mult).then_inc(F["zn"], 1)
                dve.wait_ge(F["zn"], i + 1)
                largest(1, i, zn[:, :, :])
                if ahead:
                    ln_stats(dve, L2, i + 2)
                scales(1, i)
                if ahead:
                    ln_apply(dve, L2, i + 2)
                    gated(i + 1)
                dve.wait_ge(F["t2"], 2 * i + 2)
                dve.wait_ge(F["tr2"], 2 * i)
                nc.vector.tensor_scalar(q2[:, :, :], t2[:, :, :], MAGIC, 127.0, ALU.subtract, ALU.min
                                        ).then_inc(F["q2"], 1)
                if ahead:
                    rows_scaled(i + 2)
                    scales(0, i + 2)
                    rows_integer(i + 2)
                for s in range(2):
                    dve.wait_ge(F["down"], 2 * i + s + 1)
                    nc.vector.scalar_tensor_tensor(h[:, 2 * i + s, :], ps[0:R, s, 0:D], dscale[1][:, s:s + 1],
                                                   h[:, 2 * i + s, :], ALU.mult, ALU.add).then_inc(F["resid"], 1)

            for n in range(2):
                ln_vector(dve, L2, n)
                rows_scaled(n)
                if n == 1:
                    gated(0)
                scales(0, n)
                rows_integer(n)
            with dve.Fori(0, PAIRS - 1) as i:
                ffn_vector(i, True)
            ffn_vector(PAIRS - 1, False)
            dve.wait_ge(F["resid"], TILES)


            dve.wait_ge(A1["const_in"], A1["const_in before"] + 160)
            dve.wait_ge(A1["clear"], A1["clear before"] + 2)

            def transposed_vector(L, A, j, bank=6):
                dve.wait_ge(L["tr"], L["tr before"] + 2 * j + 1)
                dve.wait_ge(A["v"], A["v before"] + 2 * j)
                nc.vector.tensor_copy(xT[:, :, 0:R], ps[:, bank, 0:3 * R].rearrange("p (c r) -> p c r", c=3)
                                      ).then_inc(A["tr_dve"], 1)

            def queries(A, j, g, table):
                dve.wait_ge(A["q"], A["q before"] + 3 * j + g + 1)
                nc.vector.tensor_tensor(Qz1[:, :, 4 * g:4 * g + 4, :],
                                        ps[:, g, 0:R2].rearrange("p (s r) -> p s r", s=2).unsqueeze(2)
                                        .to_broadcast([128, 2, 4, R]), table, ALU.mult).then_inc(A["qz"], 1)

            def normalise(A, i, least):
                heads = [ps[0:R, 6 + s, 0:NH * (HE + 1)].rearrange("p (n e) -> p n e", n=NH) for s in range(2)]
                dve.wait_ge(A["ot"], A["ot before"] + 2 * i)
                for s in range(2):
                    dve.wait_ge(A["pv"], A["pv before"] + 2 * i + s + 1)
                    if least:
                        nc.vector.tensor_scalar(den[:, s, :], heads[s][:, :, HE], least, None, ALU.max
                                                ).then_inc(A["den"], 1)
                        dve.wait_ge(A["den"], A["den before"] + 2 * i + s + 1)
                        nc.vector.reciprocal(rden[:, s, :], den[:, s, :]).then_inc(A["rec"], 1)
                    else:
                        nc.vector.reciprocal(rden[:, s, :], heads[s][:, :, HE]).then_inc(A["rec"], 1)
                    dve.wait_ge(A["rec"], A["rec before"] + 2 * i + s + 1)
                    nc.vector.tensor_tensor(O1[:, s, 0:D].rearrange("p (n e) -> p n e", n=NH), heads[s][:, :, 0:HE],
                                            rden[:, s, :].unsqueeze(2).to_broadcast([R, NH, HE]), ALU.mult
                                            ).then_inc(A["o"], 1)

            def residual(A, i, stream):
                for s in range(2):
                    dve.wait_ge(A["op"], A["op before"] + 2 * i + s + 1)
                    nc.vector.tensor_tensor(stream[:, 2 * i + s, :], ps[0:R, 6 + s, 256:256 + D],
                                            stream[:, 2 * i + s, :], ALU.add).then_inc(A["resid"], 1)

            def queries_keys_vector(j):
                dve.wait_ge(A1["s"], A1["s before"] + 6 * j)
                dve.wait_ge(A1["kt"], A1["kt before"] + 3 * j)
                for g in range(3):
                    queries(A1, j, g, rope_q[:, :, :].unsqueeze(1).to_broadcast([128, 2, 4, R]))
                    dve.wait_ge(A1["k"], A1["k before"] + 3 * j + g + 1)
                    for part, dst in ((0, kc), (1, ks)):
                        nc.vector.tensor_tensor(dst[:, g, :], ps[:, 3 + g, part * R2:(part + 1) * R2],
                                                rope_k[:, part, :], ALU.mult).then_inc(A1["ks"], 1)

            def own_scores(j):
                dve.wait_ge(A1["gel"], A1["gel before"] + 2 * j)
                for s in range(2):
                    dve.wait_ge(A1["s"], A1["s before"] + 6 * j + 3 * s + 3)
                    scores = ps[0:R, 3 * s:3 * s + 3, :].rearrange("p b (n c) -> p (b n) c", n=4)
                    mine = own[:, s, :].rearrange("p (n q) -> p n q", n=NH)
                    nc.vector.tensor_scalar(mine, scores[:, :, 0:S], image[:, 0:1], TINY, ALU.mult, ALU.add
                                            ).then_inc(A1["own"], 1)
                    for m in range(1, IPT):
                        dve.wait_ge(A1["own"], A1["own before"] + 6 * j + 3 * s + m)
                        nc.vector.scalar_tensor_tensor(mine, scores[:, :, m * S:(m + 1) * S], image[:, m:m + 1],
                                                       mine, ALU.mult, ALU.add).then_inc(A1["own"], 1)

            def reciprocals(i, s):
                dve.wait_ge(A1["own"], A1["own before"] + 6 * i + 3 * s + 3)
                nc.vector.reciprocal(rown[:, s, :], own[:, s, :]).then_inc(A1["rown"], 1)

            def weights_vector(i, s):
                dve.wait_ge(A1["rown"], A1["rown before"] + 2 * i + s + 1)
                dve.wait_ge(A1["gel"], A1["gel before"] + 2 * i + s + 1)
                dve.wait_ge(A1["pt"], A1["pt before"] + 2 * i)
                nc.vector.tensor_tensor(wt1[:, s, :], gel[:, s, :], rown[:, s, :], ALU.mult
                                        ).then_inc(A1["wt"], 1)

            def attention1_vector(i, ahead):
                weights_vector(i, 0)
                if ahead:
                    transposed_vector(L3, A1, i + 1, 2)
                    ln_stats(dve, L3, i + 2)
                reciprocals(i, 1)
                weights_vector(i, 1)
                if ahead:
                    queries_keys_vector(i + 1)
                    ln_apply(dve, L3, i + 2)
                    dve.wait_ge(L3["y"], L3["y before"] + 2 * i + 6)
                    split_vector(dve, L3, i + 2, yn)
                    own_scores(i + 1)
                normalise(A1, i, 1e-6 / (2.0 * float(HE) ** 0.5 / 2.0 ** 0.5))
                if ahead:
                    reciprocals(i + 1, 0)
                residual(A1, i, h)

            for j in range(2):
                ln_vector(dve, L3, j)
                dve.wait_ge(L3["y"], L3["y before"] + 2 * j + 2)
                split_vector(dve, L3, j, yn)
                if j == 0:
                    transposed_vector(L3, A1, 0, 2)
            queries_keys_vector(0)
            own_scores(0)
            reciprocals(0, 0)
            with dve.Fori(0, PAIRS - 1) as i:
                attention1_vector(i, True)
            attention1_vector(PAIRS - 1, False)
            dve.wait_ge(A1["resid"], A1["resid before"] + TILES)
            for s in range(2):
                nc.vector.tensor_copy(shift[s][:, :].rearrange("p (n r) -> p n r", n=NH),
                                      free_in[:, :].unsqueeze(1).to_broadcast([MK, NH, R])).then_inc(A2["copied"], 1)
            dve.wait_ge(A2["copied"], A2["copied before"] + 2)

            def rows_once(j):
                ln_vector(dve, L4, j, dst=x1, count=2 * j)

            def rows_again(j):
                dve.wait_ge(L4["y"], L4["y before"] + 4 * j + 2)
                nc.vector.memset(after_stats[0:1, :], 0.0)
                ln_affine(dve, L4, j, x1, gains[:, 0, :], gains[:, 1, :], count=2 * j + 1)

            def split_rows(j):
                dve.wait_ge(L4["affine"], L4["affine before"] + 2 * j + 2)
                split_vector(dve, L4, j, yn2)

            def queries_vector(j):
                dve.wait_ge(A2["st"], A2["st before"] + 6 * j)
                for g in range(3):
                    queries(A2, j, g, quarter[:, :].unsqueeze(1).unsqueeze(3).to_broadcast([128, 2, 4, R]))

            def maximum(j, s):
                dve.wait_ge(A2["s"], A2["s before"] + 2 * j + s + 1)
                dve.wait_ge(A2["mt"], A2["mt before"] + 2 * j)
                nc.vector.tensor_reduce(nmx[:, s, :],
                                        ps[0:R, 3 * s:3 * s + 3, 0:4 * R].rearrange("p b (n r) -> p b n r", n=4),
                                        AX.X, ALU.max, negate=True).then_inc(A2["nmx"], 1)

            def spread(j, s):
                dve.wait_ge(A2["st"], A2["st before"] + 6 * j)
                dve.wait_ge(A2["mt"], A2["mt before"] + 2 * j + s + 1)
                nc.vector.tensor_tensor(shift[s][0:NH, :].rearrange("p (n r) -> p n r", n=NH),
                                        ps[0:NH, 3 * s, 0:R].unsqueeze(1).to_broadcast([NH, NH, R]),
                                        sel12[:, :].rearrange("p (n r) -> p n r", n=NH),
                                        ALU.mult).then_inc(A2["shift"], 1)

            def attention2_vector(i, ahead):
                if ahead:
                    rows_once(i + 2)
                    transposed_vector(L4, A2, i + 1)
                    rows_again(i + 2)
                    queries_vector(i + 1)
                    split_rows(i + 2)
                normalise(A2, i, None)
                if ahead:
                    maximum(i + 1, 0)
                    maximum(i + 1, 1)
                    spread(i + 1, 0)
                residual(A2, i, x1)
                if ahead:
                    spread(i + 1, 1)

            rows_once(0)
            rows_again(0)
            split_rows(0)
            transposed_vector(L4, A2, 0)
            rows_once(1)
            rows_again(1)
            split_rows(1)
            queries_vector(0)
            for s in range(2):
                maximum(0, s)
            for s in range(2):
                spread(0, s)
            with dve.Fori(0, PAIRS - 1) as i:
                attention2_vector(i, True)
            attention2_vector(PAIRS - 1, False)
            dve.wait_ge(A2["resid"], A2["resid before"] + TILES)
            nc.vector.tensor_copy(router_h[:, :, :], router_in[:, :, :]).then_inc(RT["hi"], 1)
            dve.wait_ge(RT["hi"], 1)
            nc.vector.tensor_tensor(router_l[:, :, :], router_in[:, :, :], router_h[:, :, :].bitcast(F32), ALU.subtract
                                    ).then_inc(RT["split"], 1)

            def split_expert(e, q, part, parts=6):
                n1, n2 = 2 * FF // parts, FM * D // parts
                cols1, cols2 = slice(part * n1, (part + 1) * n1), slice(part * n2, (part + 1) * n2)
                if part == 0:
                    dve.wait_ge(EX["in1"], 16 * e + 16)
                    dve.wait_ge(EX["in2"], 16 * e + 16)
                both = ((est1[:, cols1], eh1[q][:, :, :].rearrange("p k n -> p (k n)")[:, cols1],
                         el1[q][:, :, :].rearrange("p k n -> p (k n)")[:, cols1]),
                        (est2[:, cols2], eh2[q][:, :, :].rearrange("p k n -> p (k n)")[:, cols2],
                         el2[q][:, :, :].rearrange("p k n -> p (k n)")[:, cols2]))
                for src, hi, lo in both:
                    nc.vector.tensor_copy(hi, src).then_inc(EX["hi"], 1)
                for n, (src, hi, lo) in enumerate(both):
                    dve.wait_ge(EX["hi"], 12 * e + 2 * part + n + 1)
                    nc.vector.tensor_tensor(lo, src, hi.bitcast(F32), ALU.subtract).then_inc(EX["lo"], 1)

            ln_affine(dve, L5, 0, x1, gains[:, 2, :], gains[:, 3, :])
            dve.wait_ge(L5["affine"], L5["affine before"] + 2)
            split_vector(dve, L5, 0, yn2)
            for part in range(6):
                split_expert(0, 0, part)
            with dve.Fori(0, PAIRS) as i:
                dve.wait_ge(L5["tr"], L5["tr before"] + 2 * i + 1)
                dve.wait_ge(RT["logits"], 2 * i)
                src = ps[:, 0, 0:3 * R].rearrange("p (c r) -> p c r", c=3)
                nc.vector.tensor_copy(xT[:, :, 0:R], src).then_inc(RT["tr_dve"], 1)
                nc.vector.tensor_copy(xTm[:, :, bass.ds(i * R2, R)], src).then_inc(RT["xm1"], 1)
                ln_affine(dve, L5, i + 1, x1, gains[:, 2, :], gains[:, 3, :])
                dve.wait_ge(L5["affine"], L5["affine before"] + 2 * i + 4)
                split_vector(dve, L5, i + 1, yn2)
                for s in range(2):
                    dve.wait_ge(RT["logits"], 2 * i + s + 1)
                    nc.vector.tensor_copy(logits[:, s, :], ps[0:R, 2 + s, 0:E]).then_inc(RT["raw"], 1)
                dve.wait_ge(RT["raw"], 2 * i + 2)
                nc.vector.memset(after_stats[0:1, :], 0.0)
                for s in range(2):
                    nc.vector.max(top8[:, s, :], logits[:, s, :]).then_inc(RT["top"], 1)
                dve.wait_ge(RT["top"], 2 * i + 2)
                nc.vector.memset(after_stats[0:1, :], 0.0)
                for s in range(2):
                    nc.vector.max_index(at8[:, s, :], top8[:, s, :], logits[:, s, :]).then_inc(RT["at"], 1)
                dve.wait_ge(RT["at"], 2 * i + 2)
                for n in range(2):
                    nc.vector.tensor_copy(top[:, n, bass.ds(2 * i, 2)], top8[:, :, n]).then_inc(RT["kept"], 1)
                    nc.vector.tensor_copy(top_at[:, n, bass.ds(2 * i, 2)], at8[:, :, n]).then_inc(RT["kept"], 1)
            dve.wait_ge(RT["kept"], 4 * PAIRS)
            nc.vector.tensor_tensor(pr[:, 0, :], top[:, 1, :], top[:, 0, :], ALU.subtract).then_inc(RT["k2"], 1)
            dve.wait_ge(RT["ex"], 1)
            nc.vector.tensor_scalar(pr[:, 2, :], pr[:, 1, :], 1.0, None, ALU.add).then_inc(RT["share"], 1)
            dve.wait_ge(RT["share"], 1)
            nc.vector.reciprocal(pr[:, 3, :], pr[:, 2, :]).then_inc(RT["share"], 1)
            dve.wait_ge(RT["share"], 2)
            nc.vector.tensor_tensor(pr[:, 0, :], pr[:, 1, :], pr[:, 3, :], ALU.mult).then_inc(RT["share"], 1)
            for n in range(2):
                nc.vector.tensor_tensor(share[:, n, :, :], lanes[:, :].unsqueeze(2).to_broadcast([R, E, TILES]),
                                        top_at[:, n, :].unsqueeze(1).to_broadcast([R, E, TILES]), ALU.is_equal
                                        ).then_inc(RT["share"], 1)
            dve.wait_ge(RT["share"], 5)
            for n, p in enumerate((3, 0)):
                nc.vector.tensor_tensor(share[:, n, :, :], share[:, n, :, :],
                                        pr[:, p, :].unsqueeze(1).to_broadcast([R, E, TILES]), ALU.mult
                                        ).then_inc(RT["share"], 1)
            dve.wait_ge(RT["share"], 7)
            nc.vector.tensor_tensor(we[:, :, :], share[:, 0, :, :], share[:, 1, :, :], ALU.add).then_inc(RT["share"], 1)
            dve.wait_ge(RT["share"], 8)

            def experts_vector(e, q, c, tiles, part, ahead):
                base = 36 * e + 6 * c
                for m in range(FM):
                    dve.wait_ge(EX["gelu"], base + m + 1)
                    if m == 0:
                        dve.wait_ge(EX["down"], TILES * e + 4 * c)
                    nc.vector.tensor_copy(gh[:, m, 0:tiles * R], graw[:, m % 2, 0:tiles * R]).then_inc(EX["gh"], 1)
                    dve.wait_ge(EX["gh"], base + m + 1)
                    nc.vector.tensor_tensor(gl[:, m, 0:tiles * R], graw[:, m % 2, 0:tiles * R],
                                            gh[:, m, 0:tiles * R].bitcast(F32), ALU.subtract).then_inc(EX["gl"], 1)
                if ahead:
                    part(1 - q)
                dve.wait_ge(EX["acc"], TILES * e)
                for tt in range(tiles):
                    dve.wait_ge(EX["down"], TILES * e + 4 * c + tt + 1)
                    row = h[:, 4 * c + tt, :]
                    nc.vector.scalar_tensor_tensor(row, ps[0:R, 4 + tt, 0:D], we[:, e, bass.ds(4 * c + tt, 1)], row,
                                                   ALU.mult, ALU.add).then_inc(EX["acc"], 1)

            def sixth(e, n):
                def split(q):
                    n1, n2 = 2 * FF // 6, FM * D // 6
                    both = []
                    for src, hi, lo, size in ((est1, eh1[q], el1[q], n1), (est2, eh2[q], el2[q], n2)):
                        cols = bass.ds(n * size, size)
                        both.append((src[:, cols], hi[:, :, :].rearrange("p k n -> p (k n)")[:, cols],
                                     lo[:, :, :].rearrange("p k n -> p (k n)")[:, cols]))
                    dve.wait_ge(EX["in1"], 16 * e + 16)
                    dve.wait_ge(EX["in2"], 16 * e + 16)
                    for src, hi, lo in both:
                        nc.vector.tensor_copy(hi, src).then_inc(EX["hi"], 1)
                    for m, (src, hi, lo) in enumerate(both):
                        dve.wait_ge(EX["hi"], 12 * e + 2 * n + m + 1)
                        nc.vector.tensor_tensor(lo, src, hi.bitcast(F32), ALU.subtract).then_inc(EX["lo"], 1)
                return split

            dve.wait_ge(RT["streams"], PAIRS)

            def expert(e, q, ahead):
                with dve.Fori(0, TILES // E_CHUNK) as c:
                    experts_vector(e, q, c, E_CHUNK, sixth(e + 1, c), ahead)
                last = TILES // E_CHUNK
                experts_vector(e, q, last, TILES % E_CHUNK, sixth(e + 1, last), ahead)

            with dve.Fori(0, E // 2 - 1) as pair:
                expert(2 * pair, 0, True)
                expert(2 * pair + 1, 1, True)
            expert(E - 2, 0, True)
            expert(E - 1, 1, False)


def k192(w):
    return np.ascontiguousarray(np.stack([w[0:K0], np.concatenate([w[K0:D], w[K0:D]])], axis=1))


def constants():
    f = np.float32
    tok = np.arange(R)
    pos, img = tok % S, tok // S
    key_rows = np.zeros((MK, R), f)
    key_rows[0:13] = 1
    key_rows[M_CAUSAL + pos, tok] = 1
    key_rows[M_IMAGE + img, tok] = 1
    later = np.where(np.arange(S)[:, None] > pos[None, :], BIG, 0).astype(f)
    other = np.where(np.arange(IPT)[:, None] != img[None, :], BIG, 0).astype(f)
    full = np.zeros((2, MK, R), f)
    full[0, M_CAUSAL:M_IMAGE] = later
    full[:, M_IMAGE:] = other
    cols = key_rows.copy()
    cols[0:13] = 0
    masks = np.concatenate([key_rows, full[0], full[1], np.tile(cols, (1, 4))], axis=1)
    shift = np.stack([full[0], full[1]], axis=1)
    sel = np.repeat(np.eye(NH, dtype=f), R, axis=1)
    freq = (1.0 / 10000.0 ** (np.arange(HE // 2, dtype=f) / f(HE // 2))).astype(f)
    angle = pos[None, :].astype(f) * np.repeat(freq, 2)[:, None]
    cos, sin = np.cos(angle).astype(f), np.sin(angle).astype(f)
    sin[0::2] *= -1
    row = np.arange(128)
    e, half, head = row % HE, row // HE % 2, row // (2 * HE)
    table = np.where(half[:, None] == 0, cos[e], sin[e])
    mine = (head[:, None] == np.arange(4)).astype(f)
    rope_q = table[:, None, :] * mine[:, :, None]
    rope_k = np.stack([np.tile(cos[e], (1, 2)), np.tile(sin[e], (1, 2))], axis=1)
    same = img[:, None] == img[None, :]
    causal = (same & (pos[:, None] <= pos[None, :])).astype(f)
    image = (img[:, None] == np.arange(IPT)).astype(f)
    lanes = np.tile(np.arange(E, dtype=f), (R, 1))
    return {"rope_q": rope_q.astype(f), "rope_k": rope_k.astype(f), "causal": causal, "image": image, "quarter": mine,
            "free": full[1], "lanes": lanes, "ident": np.eye(128, dtype=f), "masks": masks, "shift": np.ascontiguousarray(shift), "sel12": sel}


def lay_out(i):
    a = constants()
    a["x"] = np.ascontiguousarray(i["x"].reshape(B, C_IN, GRID, 2, PATCH // 2, GRID, PATCH)
                                  .transpose(0, 2, 1, 3, 5, 4, 6).reshape(B * GRID, C_IN * PW))
    a["wtok"] = np.ascontiguousarray(i["L0_tok_W"].reshape(NK, 128, D).transpose(1, 0, 2))
    near = np.arange(GRID) * 14 // GRID
    pos = i["L0_tok_positions"][0][:, near][:, :, near].reshape(D, GRID * GRID).T
    a["pos"] = np.ascontiguousarray(np.tile(np.concatenate([i["L0_tok_cls_embedding"][0], pos]), (IPT, 1)))
    a["tok_b"] = i["L0_tok_b"].reshape(1, D)
    qkv = [i[f"L0_attn_W_{c}"].transpose(1, 0, 2).reshape(D, NH * HD) for c in "QKV"]
    a["w1"] = k192(np.concatenate(qkv, axis=1))
    a["b_qk"] = np.ascontiguousarray(np.concatenate(
        [i["L0_attn_b_Q"].reshape(6, 128).T, i["L0_attn_b_K"].reshape(6, 128).T], axis=1))
    a["b_v"] = i["L0_attn_b_V"].reshape(1, NH * HD)
    a["b_o"] = i["L0_attn_b_O"].reshape(1, D)
    a["wo1"] = np.ascontiguousarray(i["L0_attn_W_O"].reshape(6, 128, D).transpose(1, 0, 2))
    win = np.zeros((256, 2 * HF), np.float32)
    win[0:D] = i["L0_ffn_w_in"].T
    a["win"] = np.ascontiguousarray(win.reshape(2, 128, 2 * HF).transpose(1, 0, 2))
    a["wout"] = np.ascontiguousarray(i["L0_ffn_w_out"].T.reshape(4, 128, D).transpose(1, 0, 2))
    a["g_in"] = i["L0_ffn_g_in"].reshape(1, D)
    a["g_out"] = i["L0_ffn_g_out"].reshape(1, HF)
    def heads(w, other):
        out = np.zeros((D, NH, 2, HE), np.float32)
        out[:, :, 0] = w.reshape(D, NH, HE)
        if other is not None:
            out[:, :, 1] = other.reshape(D, NH, HE)
        return out.reshape(D, NH * 2 * HE)

    def swapped(w):
        return w.reshape(D, NH, HE // 2, 2)[:, :, :, ::-1].reshape(D, D)

    q, k, v = (i[f"L1_attn_W{c}"].T for c in "qkv")
    q4, k4, v4 = (i["L1_ffn_Wqkv"][:, c * D:(c + 1) * D] for c in range(3))
    both = np.concatenate([heads(q, swapped(q)), heads(k, k), heads(swapped(k), swapped(k)), v,
                           heads(q4, None), heads(k4, None), v4, np.zeros((D, WPAD - WCOLS), np.float32)], axis=1)
    a["w3"] = k192(both)
    w, gap = [], 128
    for m in (i["L1_attn_Wproj"].T, i["L1_ffn_Wproj"]):
        padded = np.zeros((256, D), np.float32)
        padded[0:D] = m
        w.append(padded.reshape(2, 128, D).transpose(1, 0, 2))
    a["proj"] = np.ascontiguousarray(np.stack(w, axis=1))
    a["gains"] = np.stack([i[f"L1_ffn_ln{n}_{x}"] for n in (1, 2) for x in "gb"])[None]
    a["router"] = k192(i["L1_ffn_Wrouter"])
    a["moe1"] = np.stack([k192(m).reshape(128, 2 * FF) for m in i["L1_ffn_W1"]])
    a["moe2"] = np.ascontiguousarray(i["L1_ffn_W2"].reshape(E, FM, 128, D).transpose(0, 2, 1, 3)).reshape(E, 128, FM * D)
    return a


def kernel(**inputs):
    import numpy as _np
    import concourse.bacc as _bacc
    from concourse import mybir as _mybir
    from concourse.bass_utils import run_bass_kernel_spmd as _run

    nc = _bacc.Bacc("TRN2", target_bir_lowering=False, num_devices=1)
    arrays, tensors = {}, {}
    for name, a in lay_out({n: _np.asarray(v) for n, v in inputs.items()}).items():
        a = _np.ascontiguousarray(a)
        arrays[f"in_{name}_dram"] = a
        tensors[name] = nc.dram_tensor(f"in_{name}_dram", a.shape, _mybir.dt.from_np(a.dtype),
                                       kind="ExternalInput").ap()
    tensors["out"] = nc.dram_tensor("out_0_dram", (B, S, D), _mybir.dt.float32, kind="ExternalOutput").ap()
    build_program(nc, tensors)
    r = _run(nc, [arrays], core_ids=[0])
    return r.results[0]["out_0_dram"]
```

```python
import numpy as np
import concourse.bass as bass
from concourse import mybir
from contextlib import ExitStack

F32 = mybir.dt.float32
F32R = mybir.dt.float32r
BF16 = mybir.dt.bfloat16
U32 = mybir.dt.uint32
ALU = mybir.AluOpType
ACT = mybir.ActivationFunctionType
AX = mybir.AxisListType
RADD = bass.bass_isa.ReduceOp.add

B, C_IN, IMG, PATCH = 64, 3, 96, 16
GRID = IMG // PATCH
S = GRID * GRID + 1
D = 192
K0 = 128
IPT = 3
R = IPT * S
TILES = 22
TILES_ALL = 24
PAIRS = TILES // 2
R2 = 2 * R
GI = 18
GROUPS = 4
GT = GI // IPT
GROWS = GI * GRID
NK = C_IN * 2
PW = PATCH * IMG
NH = 12
HD = 64
HE = 16
HF = 512
E, FF = 8, 768
FM = FF // 128
NQ = NH * S
BIG = -1.0e30
TINY = 1.0e-20
MAGIC = 12582912.0
MK = 72
M_CAUSAL = 32
M_IMAGE = M_CAUSAL + S
W34 = 3 * 128 + 6 * 128 + D
W4 = 3 * 128 + 3 * 128 + D
WCOLS = W34 + W4
WSTEP = 210
WPAD = PAIRS * WSTEP
E_CHUNK = 4


def build_program(nc, t):
    ctx = ExitStack()
    with ctx:
        def sem(name):
            return ctx.enter_context(nc.semaphore(name))

        cursor = [16512]

        def put(name, shape, dt, at=None):
            where = cursor if at is None else at
            size = 4 if dt in (F32, F32R, U32) else 2
            n = size
            for d in shape[1:]:
                n *= d
            got = nc.alloc_sbuf_tensor_at(name, shape, dt, offset=where[0])
            where[0] += (n + 31) // 32 * 32
            assert where[0] <= 229344, (name, where[0])
            return got

        ps = ctx.enter_context(nc.psum_tensor("ps", [128, 8, 512], F32))

        h = put("h", [R, TILES_ALL, D], F32)
        ident = put("ident", [128, 128], F32)
        identb = put("identb", [128, 128], BF16)
        halfneg = put("halfneg", [R, 2], F32)
        eps_ln = put("eps_ln", [R, 2], F32)
        eps_rms = put("eps_rms", [R, 2], F32)
        after_stats = put("after_stats", [1, 1], F32)
        tiny = put("tiny", [R, 1], F32)
        spare = put("spare", [R, 1], F32)
        query_rows = put("query_rows", [MK, 2, R], F32R)
        key_cols = put("key_cols", [MK, 4 * R], F32R)
        prob = put("prob", [R, 2, NH * R], F32)
        posb = put("posb", [R, D], F32)
        bo_t = put("bo_t", [R, D], F32)
        bqk = put("bqk", [128, 12], F32)
        bv_t = put("bv_t", [R, NH * HD], F32)
        stats = put("stats", [R, 2, 6], F32)
        mv = put("mv", [R, 2, 2], F32)
        vare = put("vare", [R, 2], F32)
        rstd = put("rstd", [R, 2], F32)
        yn = put("yn", [R, 2, D], F32)
        yn2 = put("yn2", [R, 2, D], F32)
        xs = put("xs", [R, 2, 2 * D], F32R)
        peak = put("peak", [R, 2, NH], F32)
        rden = put("rden", [R, 2, NH], F32)
        xT = put("xT", [128, 3, R2], F32R)
        wq_in = put("wq_in", [128, 2, 2 * HF], BF16)
        wq_out = put("wq_out", [128, 4, D], BF16)
        g_in = put("g_in", [R, D], F32)
        g_out = put("g_out", [R, HF], F32)
        wsum = put("wsum", [128, 2], F32)
        wall = put("wall", [128, 2], F32)
        wmean = put("wmean", [128, 2], F32)
        wrec = put("wrec", [128, 2], F32)
        w127 = put("w127", [128, 2], F32)
        magic = put("magic", [R, 1], F32)
        ss, rq, rms, amax, amaxc, arec, qscale, dscale = (
            [put(f"{n}{k}", [R, 2], F32) for k in range(2)]
            for n in ("ss", "rq", "rms", "amax", "amaxc", "arec", "qscale", "dscale"))
        region_a = [cursor[0]]
        a0 = region_a[0]
        wh1 = put("wh1", [128, 2, 3 * NH * HD], F32R, region_a)
        wl1 = put("wl1", [128, 2, 3 * NH * HD], F32R, region_a)
        region_b = [region_a[0]]
        wh3 = put("wh3", [128, 2, WPAD], F32R, region_b)
        wl3 = put("wl3", [128, 2, WPAD], F32R, region_b)
        work0 = region_b[0]

        w = [work0]
        X = [put(f"X{p}", [128, C_IN * PW], F32, w) for p in range(2)]
        PT = [put(f"PT{p}", [128, NK, GI * S], F32, w) for p in range(2)]
        wtok = put("wtok", [128, NK, D], F32, w)
        w = [region_a[0]]
        stage1 = put("stage1", [128, 2, 2304], F32, w)
        mask_in = put("mask_in", [MK, 2 * R + 4 * R], F32, w)
        win_in = put("win_in", [128, 2, 2 * HF], F32, w)
        wout_in = put("wout_in", [128, 4, D], F32, w)
        assert w[0] <= work0, (w[0], work0)
        w = [work0]
        Qz = put("Qz", [128, 2, NH, R], F32, w)
        KT = put("KT", [128, 6, R2], F32, w)
        V = put("V", [R, 2, NH, HD + 1], F32, w)
        Pt = put("Pt", [R, 2, NH * R], F32, w)
        O = put("O", [R, 2, NH * HD], F32, w)
        OT = put("OT", [128, 2, 6, R], F32, w)
        wo1 = put("wo1", [128, 6, D], F32, w)
        wst3 = put("wst3", [128, 2, WPAD], F32, w)

        w = [work0]
        xn = put("xn", [R, 2, D], F32, w)
        t1 = put("t1", [R, 2, D], F32, w)
        q1 = put("q1", [R, 2, 2 * 128], BF16, w)
        q1T = put("q1T", [128, 2, 2, R + 1], BF16, w)
        sg = put("sg", [R, 2, HF], F32, w)
        z = put("z", [R, 2, HF], F32, w)
        zn = put("zn", [R, 2, HF], F32, w)
        t2 = put("t2", [R, 2, HF], F32, w)
        q2 = put("q2", [R, 2, HF], BF16, w)
        q2T = put("q2T", [128, 2, 4, R + 1], BF16, w)
        junk1 = put("junk1", [R, 2, D], F32, w)
        junk2 = put("junk2", [R, 2, HF], F32, w)
        psb = ps[:, :, :].bitcast(BF16)
        w = [a0]
        rope_q = put("rope_q", [128, 4, R], F32, w)
        rope_k = put("rope_k", [128, 2, R2], F32, w)
        causal = put("causal", [R, R], F32, w)
        image = put("image", [R, IPT], F32, w)
        quarter = put("quarter", [128, 4], F32, w)
        proj = put("proj", [128, 2, 2, D], F32, w)
        gains = put("gains", [R, 4, D], F32, w)
        router_in = put("router_in", [128, 2, E], F32, w)
        router_h = put("router_h", [128, 2, E], F32R, w)
        router_l = put("router_l", [128, 2, E], F32R, w)
        ranks = put("ranks", [R, E], F32, w)
        logits = put("logits", [R, 2, TILES, E], F32, w)
        best = put("best", [R, 2, TILES], F32, w)
        rank = put("rank", [R, TILES, E], F32, w)
        best_rank = put("best_rank", [R, 2, TILES], F32, w)
        pr = put("pr", [R, 4, TILES], F32, w)
        share = put("share", [R, 2, TILES, E], F32, w)
        we = put("we", [R, E, TILES], F32, w)
        est1 = put("est1", [128, 2 * FF], F32, w)
        est2 = put("est2", [128, FM * D], F32, w)
        assert w[0] <= region_a[0]
        w = [work0]
        Qz1 = put("Qz1", [128, 2, NH, R], F32, w)
        KT1 = put("KT1", [128, 3, R2], F32, w)
        V1 = put("V1", [R, 2, NH, HE + 1], F32, w)
        Pt1 = put("Pt1", [R, 2, NH * R], F32, w)
        den = put("den", [R, 2, NH], F32, w)
        O1 = put("O1", [R, 2, 256], F32, w)
        OT1 = put("OT1", [128, 2, 2, R], F32, w)
        x1 = put("x1", [R, TILES_ALL, D], F32, list(w))
        kc = put("kc", [128, 3, R2], F32, w)
        ks = put("ks", [128, 3, R2], F32, w)
        own = put("own", [R, 2, NQ], F32, w)
        rown = put("rown", [R, 2, NQ], F32, w)
        gel = put("gel", [R, 2, NQ], F32, w)
        wt1 = put("wt1", [R, 2, NQ], F32, w)
        eh1, el1, eh2, el2 = [None] * 2, [None] * 2, [None] * 2, [None] * 2

        def expert_weights(q):
            eh1[q] = put(f"eh1{q}", [128, 2, FF], F32R, w)
            el1[q] = put(f"el1{q}", [128, 2, FF], F32R, w)
            eh2[q] = put(f"eh2{q}", [128, FM, D], F32R, w)
            el2[q] = put(f"el2{q}", [128, FM, D], F32R, w)

        expert_weights(0)
        w = [work0]
        expert_weights(1)
        graw = put("graw", [128, 2, 4 * R], F32, w)
        gh = put("gh", [128, FM, 4 * R], F32R, w)
        xTm = put("xTm", [128, 3, TILES * R], F32R, [region_a[0]])
        gl = put("gl", [128, FM, 4 * R], F32R, w)

        x_in = [sem(f"x_in{p}") for p in range(2)]
        ident_in = sem("ident_in")
        wtok_in = sem("wtok_in")
        const_in = sem("const_in")
        w1_in = sem("w1_in")
        w3_in = sem("w3_in")
        wo1_in = sem("wo1_in")
        pos_in = sem("pos_in")
        bo_in = sem("bo_in")
        cleared = sem("cleared")
        chain = sem("chain")
        consts_copied = sem("consts_copied")
        consts_ready = sem("consts_ready")
        w1_hi = sem("w1_hi")
        w1_ready = sem("w1_ready")
        w3_hi = sem("w3_hi")
        w3_ready = sem("w3_ready")
        pos_ready = sem("pos_ready")
        pt_done = sem("pt_done")
        pt_copied = sem("pt_copied")
        tok_done = sem("tok_done")
        tok_h = sem("tok_h")
        out_done = sem("out_done")

        def signals(stage, names):
            return {n: sem(f"{stage}_{n}") for n in names.split()}

        def counted(shared, before, own=None):
            got = {}
            for n, s in {**shared, **(own or {})}.items():
                got[n] = s
                got[n + " before"] = before.get(n, 0)
            return got

        ln = signals("ln", "stats mv vare rstd y affine hi xs tr")
        STEPS = PAIRS + 1

        def norm_stage(norms, splits, affines):
            return counted(ln, {"stats": 2 * STEPS * norms, "mv": 2 * STEPS * norms, "vare": STEPS * norms,
                                "rstd": STEPS * norms, "y": 2 * STEPS * norms, 
                                "affine": 2 * STEPS * affines, "hi": STEPS * splits, "xs": STEPS * splits,
                                "tr": TILES * splits})

        L1, L2, L3, L4, L5 = (norm_stage(*n) for n in ((0, 0, 0), (1, 1, 0), (2, 1, 0), (3, 2, 0), (5, 3, 1)))

        def split5(hi, lo, a, b):
            return ((1, hi[:, 0, a:b]), (0, hi[:, 0, a:b]), (1, lo[:, 0, a:b]), (2, hi[:, 1, a:b]), (2, lo[:, 1, a:b]))

        def ln_stats(dve, L, call, src=h, count=None):
            n = call if count is None else count
            for s in range(2):
                nc.vector.bn_stats(stats[:, s, :], src[:, 2 * call + s, :]).then_inc(L["stats"], 1)
            dve.wait_ge(L["stats"], L["stats before"] + 2 * n + 2)
            nc.vector.memset(after_stats[0:1, :], 0.0)
            for s in range(2):
                nc.vector.bn_aggr(mv[:, s, :], stats[:, s, :]).then_inc(L["mv"], 1)

        def ln_apply(dve, L, call, src=h, dst=None, count=None):
            n = call if count is None else count
            dve.wait_ge(L["rstd"], L["rstd before"] + n + 1)
            for s in range(2):
                out = yn[:, s, :] if dst is None else dst[:, 2 * call + s, :]
                nc.vector.tensor_scalar(out, src[:, 2 * call + s, :], mv[:, s, 0:1], rstd[:, s:s + 1],
                                        ALU.subtract, ALU.mult).then_inc(L["y"], 1)

        def ln_vector(dve, L, call, src=h, dst=None, count=None):
            ln_stats(dve, L, call, src, count)
            ln_apply(dve, L, call, src, dst, count)

        def ln_affine(dve, L, call, src, g, b, count=None):
            n = call if count is None else count
            ln_stats(dve, L, call, src, count)
            dve.wait_ge(L["mv"], L["mv before"] + 2 * n + 2)
            for s in range(2):
                nc.vector.scalar_tensor_tensor(yn2[:, s, :], src[:, 2 * call + s, :], mv[:, s, 0:1], g,
                                               ALU.subtract, ALU.mult).then_inc(L["y"], 1)
            dve.wait_ge(L["y"], L["y before"] + 2 * n + 2)
            dve.wait_ge(L["rstd"], L["rstd before"] + n + 1)
            for s in range(2):
                nc.vector.scalar_tensor_tensor(yn2[:, s, :], yn2[:, s, :], rstd[:, s:s + 1], b,
                                               ALU.mult, ALU.add).then_inc(L["affine"], 1)

        def split_vector(dve, L, call, src):
            dve.wait_ge(L["tr"], L["tr before"] + 2 * call)
            nc.vector.tensor_copy(xs[:, :, K0:K0 + D], src[:, :, :]).then_inc(L["hi"], 1)
            dve.wait_ge(L["hi"], L["hi before"] + call + 1)
            nc.vector.tensor_tensor(xs[:, :, 0:K0], src[:, :, 0:K0], xs[:, :, K0:2 * K0].bitcast(F32),
                                    ALU.subtract)
            nc.vector.tensor_tensor(xs[:, :, K0 + D:2 * D], src[:, :, K0:D], xs[:, :, 2 * K0:K0 + D].bitcast(F32),
                                    ALU.subtract).then_inc(L["xs"], 1)

        def ln_pool(pool, L, call):
            pool.wait_ge(L["mv"], L["mv before"] + 2 * call + 2)
            nc.gpsimd.tensor_tensor(vare[:, :], mv[:, :, 1], eps_ln[:, :], ALU.add).then_inc(L["vare"], 1)
            pool.wait_ge(L["vare"], L["vare before"] + call + 1)
            nc.gpsimd.tensor_tensor(rstd[:, :], vare[:, :], halfneg[:, :], ALU.pow).then_inc(L["rstd"], 1)

        def transposes(L, s, bank):
            x = xs[:, s, :].bitcast(F32)
            for c in range(3):
                tr = nc.tensor.transpose(ps[:, bank, c * R:(c + 1) * R], x[:, c * K0:(c + 1) * K0], ident[0:R, 0:R])
            tr.then_inc(L["tr"], 1)

        tr_copied_dve = sem("tr_copied_dve")
        tr_copied_act = sem("tr_copied_act")
        qz_clear = sem("qz_clear")
        hb_done = sem("hb_done")
        qk_done = sem("qk_done")
        q_copied = sem("q_copied")
        k_copied = sem("k_copied")
        v_done = sem("v_done")
        v_copied = sem("v_copied")
        s_done = sem("s_done")
        peak_ready = sem("peak_ready")
        less_ready = sem("less_ready")
        exp_ready = sem("exp_ready")
        turned = sem("turned")
        p_ready = sem("p_ready")
        pv_done = sem("pv_done")
        rden_ready = sem("rden_ready")
        o_ready = sem("o_ready")
        ot_done = sem("ot_done")
        ot_copied = sem("ot_copied")
        op_done = sem("op_done")
        resid_done = sem("resid_done")
        Q = signals("quant", "in summed all step ready")
        F = signals("ffn0", "clear gain_in ssq1 rq1 rms1 xn amax1 amaxc1 arec1 small1 t1 q1 tr1 q1T up sg z ssq2 rq2 rms2 "
                    "zn amax2 amaxc2 arec2 small2 t2 q2 tr2 q2T down resid")
        both = signals("attn", "tr_dve tr_act q k qz v v_out pv rec o ot ot_out op resid")
        A1 = counted(both, {}, signals("attn1", "const_in clear ks kt s own0 own rown gel wt pt den"))
        A2 = counted(both, {"tr_dve": PAIRS, "tr_act": PAIRS, "q": 3 * PAIRS, "k": 3 * PAIRS, "qz": 3 * PAIRS,
                            **{n: TILES for n in "v v_out pv rec o ot ot_out op resid".split()}},
                     signals("attn2", "kt s peak less exp turned p"))
        RT = signals("router", "streams hi split tr_act xm logits raw pick k2 ex share")
        EX = signals("experts", "in1 in2 hi lo half gelu gh gl down acc")
        block = ctx.enter_context(nc.Block())

        @block.sync
        def _(sp):
            def load_group(g):
                n = min(GROWS, B * GRID - g * GROWS)
                sp.dma_start(X[g % 2][0:n, :], t["x"][g * GROWS:g * GROWS + n, :]).then_inc(x_in[g % 2], 16)

            load_group(0)
            sp.dma_start(ident[:, :], t["ident"]).then_inc(ident_in, 16)
            sp.dma_start(wtok[:, :, :], t["wtok"]).then_inc(wtok_in, 16)
            load_group(1)
            sp.dma_start(mask_in[:, :], t["masks"]).then_inc(const_in, 16)
            sp.dma_start(stage1[:, :, :], t["w1"]).then_inc(w1_in, 16)
            sp.dma_start(win_in[:, :, :], t["win"]).then_inc(Q["in"], 16)
            sp.dma_start(wout_in[:, :, :], t["wout"]).then_inc(Q["in"], 16)
            for g in range(2, GROUPS):
                sp.wait_ge(pt_done, 12 * (g - 1))
                load_group(g)
            sp.wait_ge(tok_done, GROUPS * GT)
            sp.wait_ge(pt_done, GROUPS * 12)
            sp.dma_start(wo1[:, :, :], t["wo1"]).then_inc(wo1_in, 16)
            sp.dma_start(wst3[:, :, :], t["w3"]).then_inc(w3_in, 16)
            sp.wait_ge(w3_in, 16)
            sp.wait_ge(resid_done, TILES)
            for name, dst in (("rope_q", rope_q), ("rope_k", rope_k), ("causal", causal), ("image", image),
                              ("quarter", quarter), ("proj", proj), ("gains", gains),
                              ("router", router_in), ("ranks", ranks)):
                if name == "gains":
                    sp.dma_start(dst[:, :, :], t[name].to_broadcast([R, 4, D])).then_inc(A1["const_in"], 16)
                else:
                    sp.dma_start(dst[tuple(slice(None) for _ in dst.shape)], t[name]).then_inc(A1["const_in"], 16)
            for e in range(E):
                if e:
                    sp.wait_ge(EX["lo"], 12 * e)
                sp.dma_start(est1[:, :], t["moe1"][e]).then_inc(EX["in1"], 16)
                sp.dma_start(est2[:, :], t["moe2"][e]).then_inc(EX["in2"], 16)
            rows = t["out"].rearrange("b s d -> (b s) d")
            for c in range(6):
                sp.wait_ge(EX["acc"], TILES * (E - 1) + min(4 * c + 4, TILES))
                t0, t1 = 4 * c, min(4 * c + 4, B // IPT)
                sp.dma_start(rows[t0 * R:t1 * R, :].rearrange("(t r) d -> r t d", r=R), h[:, t0:t1, :]
                             ).then_inc(out_done, 16)
            rest = B * S - (B // IPT) * R
            sp.dma_start(rows[B * S - rest:B * S, :], h[0:rest, TILES - 1, :]).then_inc(out_done, 16)
            sp.wait_ge(out_done, 16 * 7)

        @block.gpsimd
        def _(pool):
            nc.gpsimd.dma_start(posb[:, :], t["pos"]).then_inc(pos_in, 16)
            nc.gpsimd.memset(bo_t[:, :], 0.0).then_inc(cleared, 1)
            for p in range(2):
                cls = PT[p][:, :, :].rearrange("p k (b s) -> p k b s", s=S)[:, :, :, 0]
                nc.gpsimd.memset(cls, 0.0).then_inc(cleared, 1)
            nc.gpsimd.memset(halfneg[:, :], -0.5).then_inc(cleared, 1)
            nc.gpsimd.memset(eps_ln[:, :], 1e-5).then_inc(cleared, 1)
            nc.gpsimd.memset(eps_rms[:, :], 1e-6).then_inc(cleared, 1)
            pool.wait_ge(cleared, 1)
            for i in range(IPT):
                nc.gpsimd.dma_start(bo_t[i * S + 1:(i + 1) * S, :],
                                    t["tok_b"].to_broadcast([S - 1, D])).then_inc(pos_in, 16)
            nc.gpsimd.dma_start(bv_t[:, :], t["b_v"].to_broadcast([R, NH * HD])).then_inc(pos_in, 16)
            nc.gpsimd.dma_start(bqk[:, :], t["b_qk"]).then_inc(pos_in, 16)
            nc.gpsimd.dma_start(g_in[:, :], t["g_in"].to_broadcast([R, D])).then_inc(F["gain_in"], 16)
            nc.gpsimd.dma_start(g_out[:, :], t["g_out"].to_broadcast([R, HF])).then_inc(F["gain_in"], 16)
            nc.gpsimd.memset(magic[:, :], MAGIC).then_inc(F["clear"], 1)
            ln_pool(pool, L1, 0)
            pool.wait_ge(Q["summed"], 2)
            nc.gpsimd.partition_all_reduce(wall[:, :], wsum[:, :], 128, RADD).then_inc(Q["all"], 1)
            pool.wait_ge(pos_ready, 1)
            nc.gpsimd.dma_start(bo_t[:, :], t["b_o"].to_broadcast([R, D])).then_inc(bo_in, 16)
            pool.wait_ge(tok_done, GROUPS * GT)
            nc.gpsimd.memset(Qz[:, :, :, :].rearrange("p s n r -> p (s n r)"), 0.0).then_inc(qz_clear, 1)
            nc.gpsimd.memset(V[:, :, :, HD:HD + 1], 1.0).then_inc(qz_clear, 1)
            ln_pool(pool, L1, 1)
            pool.wait_ge(bo_in, 16)

            def bias_pool(i):
                pool.wait_ge(L1["xs"], L1["xs before"] + i + 1)
                for s in range(2):
                    nc.gpsimd.tensor_tensor(h[:, 2 * i + s, :], h[:, 2 * i + s, :], bo_t[:, :],
                                            ALU.add).then_inc(hb_done, 1)

            with pool.Fori(0, PAIRS - 1) as i:
                ln_pool(pool, L1, i + 2)
                bias_pool(i)
            bias_pool(PAIRS - 1)
            ln_pool(pool, L2, 0)
            pool.wait_ge(resid_done, TILES)
            nc.gpsimd.memset(q1[:, :, D:2 * 128], 0.0).then_inc(F["clear"], 1)

            def root(k, call):
                pool.wait_ge(F[f"ssq{k + 1}"], 2 * call + 2)
                nc.gpsimd.tensor_tensor(rq[k][:, :], ss[k][:, :], eps_rms[:, :], ALU.add).then_inc(F[f"rq{k + 1}"], 1)
                pool.wait_ge(F[f"rq{k + 1}"], call + 1)
                nc.gpsimd.tensor_tensor(rms[k][:, :], rq[k][:, :], halfneg[:, :], ALU.pow
                                        ).then_inc(F[f"rms{k + 1}"], 1)

            root(0, 0)
            ln_pool(pool, L2, 1)
            root(0, 1)
            with pool.Fori(0, PAIRS - 1) as i:
                root(1, i)
                ln_pool(pool, L2, i + 2)
                root(0, i + 2)
            root(1, PAIRS - 1)
            ln_pool(pool, L3, 0)

            pool.wait_ge(F["resid"], TILES)
            nc.gpsimd.memset(V1[:, :, :, HE:HE + 1], 1.0).then_inc(A1["clear"], 1)
            nc.gpsimd.memset(O1[:, :, D:256], 0.0).then_inc(A1["clear"], 1)
            nc.gpsimd.memset(tiny[:, :], TINY).then_inc(A1["clear"], 1)
            pool.wait_ge(A1["const_in"], A1["const_in before"] + 144)
            ln_pool(pool, L3, 1)

            def keys_pool(j):
                pool.wait_ge(A1["s"], A1["s before"] + 6 * j)
                for g in range(3):
                    pool.wait_ge(A1["ks"], A1["ks before"] + 6 * j + 2 * g + 2)
                    nc.gpsimd.tensor_tensor(KT1[:, g, :], kc[:, g, :], ks[:, g, :], ALU.add).then_inc(A1["kt"], 1)

            def weights_pool(i, s):
                pool.wait_ge(A1["wt"], A1["wt before"] + 2 * i + s + 1)
                pool.wait_ge(A1["pv"], A1["pv before"] + 2 * i)
                nc.gpsimd.tensor_tensor(
                    Pt1[:, s, :].rearrange("p (n i q) -> p n i q", n=NH, i=IPT),
                    wt1[:, s, :].rearrange("p (n q) -> p n q", n=NH).unsqueeze(2).to_broadcast([R, NH, IPT, S]),
                    causal[:, :].rearrange("p (i q) -> p i q", i=IPT).unsqueeze(1).to_broadcast([R, NH, IPT, S]),
                    ALU.mult).then_inc(A1["pt"], 1)

            keys_pool(0)
            with pool.Fori(0, PAIRS - 1) as i:
                ln_pool(pool, L3, i + 2)
                weights_pool(i, 0)
                weights_pool(i, 1)
                keys_pool(i + 1)
            weights_pool(PAIRS - 1, 0)
            weights_pool(PAIRS - 1, 1)
            for n in range(2):
                ln_pool(pool, L4, n)
            pool.wait_ge(A1["resid"], A1["resid before"] + TILES)
            for n in range(2, 4):
                ln_pool(pool, L4, n)
            with pool.Fori(0, PAIRS - 1) as i:
                ln_pool(pool, L4, 2 * i + 4)
                ln_pool(pool, L4, 2 * i + 5)
            pool.wait_ge(EX["in1"], 16)
            pool.wait_ge(EX["in2"], 16)
            halves = ((est1[:, :], eh1[0][:, :, :].rearrange("p k n -> p (k n)"),
                       el1[0][:, :, :].rearrange("p k n -> p (k n)")),
                      (est2[:, :], eh2[0][:, :, :].rearrange("p k n -> p (k n)"),
                       el2[0][:, :, :].rearrange("p k n -> p (k n)")))
            for src, hi, lo in halves:
                nc.gpsimd.tensor_copy(hi, src).then_inc(EX["hi"], 6)
            for n, (src, hi, lo) in enumerate(halves):
                pool.wait_ge(EX["hi"], 6 * n + 6)
                nc.gpsimd.tensor_tensor(lo, src, hi.bitcast(F32), ALU.subtract).then_inc(EX["lo"], 6)
            ln_pool(pool, L5, 0)
            pool.wait_ge(A2["resid"], A2["resid before"] + TILES)
            with pool.Fori(0, PAIRS) as i:
                ln_pool(pool, L5, i + 1)
                nc.gpsimd.tensor_tensor(h[:, bass.ds(2 * i, 2), :], h[:, bass.ds(2 * i, 2), :],
                                        x1[:, bass.ds(2 * i, 2), :], ALU.add).then_inc(RT["streams"], 1)

        @block.tensor
        def _(pe):
            pe.wait_ge(ident_in, 16)
            with pe.Fori(0, GROUPS // 2) as i:
                for p in range(2):
                    pe.wait_ge(x_in[p], 16 * i + 16)
                    src = X[p][:, :].rearrange("p (k g w) -> p k g w", k=NK, g=GRID)
                    for k in range(NK):
                        for half in range(2):
                            n = 12 * p + 2 * k + half
                            if n < 4:
                                pe.wait_ge(pt_copied, 24 * i)
                            else:
                                pe.wait_ge(pt_copied, 24 * i + n - 3)
                            for j in range(3):
                                gw = 3 * half + j
                                tr = nc.tensor.transpose(ps[:, n % 4, j * GROWS:(j + 1) * GROWS],
                                                         src[0:GROWS, k, gw, :],
                                                         ident[0:GROWS, 0:GROWS])
                            tr.then_inc(pt_done, 1)
                pe.wait_ge(wtok_in, 16)
                for p in range(2):
                    pe.wait_ge(pt_copied, 24 * i + 12 * p + 12)
                    for m in range(GT):
                        n = GT * p + m
                        if n < 4:
                            pe.wait_ge(tok_h, 12 * i)
                        else:
                            pe.wait_ge(tok_h, 12 * i + n - 3)
                        for k in range(NK):
                            mm = nc.tensor.matmul(ps[0:R, 4 + n % 4, 0:D], PT[p][:, k, m * R:(m + 1) * R],
                                                  wtok[:, k, :], start=(k == 0), stop=(k == NK - 1))
                        mm.then_inc(tok_done, 1)
            pe.wait_ge(tok_h, TILES_ALL)
            pe.wait_ge(w1_ready, 1)
            pe.wait_ge(consts_ready, 1)
            pe.wait_ge(const_in, 16)
            pe.wait_ge(qz_clear, 2)
            pe.wait_ge(wo1_in, 16)

            def rows_in0(j):
                pe.wait_ge(L1["xs"], L1["xs before"] + j + 1)
                pe.wait_ge(v_copied, 4 * j)
                transposes(L1, 0, 6)
                transposes(L1, 1, 7)

            def queries_keys0(j, first=False):
                pe.wait_ge(tr_copied_dve, j + 1)
                pe.wait_ge(tr_copied_act, j + 1)
                for side in range(2):
                    if not first:
                        pe.wait_ge(p_ready, 6 * j - 3 + 3 * side)
                    for g in range(3):
                        for n2 in range(2):
                            m = 6 * side + 2 * g + n2
                            for n, (x, wt) in enumerate(split5(wh1, wl1, 128 * m, 128 * m + 128)):
                                mm = nc.tensor.matmul(ps[:, 3 * side + g, n2 * R2:(n2 + 1) * R2], wt, xT[:, x, :],
                                                      start=(n == 0), stop=(n == 4))
                        mm.then_inc(qk_done, 1)

            def scores0(j, s):
                pe.wait_ge(q_copied, 12 * j + 12)
                pe.wait_ge(k_copied, 6 * j + 6)
                for b in range(3):
                    bank = 3 * s + b
                    nc.tensor.matmul(ps[0:R, bank, 0:4 * R], query_rows[:, 0, :], key_cols[:, :], start=True, stop=False)
                    for m in range(4):
                        n = 4 * b + m
                        mm = nc.tensor.matmul(ps[0:R, bank, m * R:(m + 1) * R], Qz[:, s, n, :],
                                              KT[:, n // 2, s * R:(s + 1) * R], start=False, stop=(m == 3))
                mm.then_inc(s_done, 1)

            def values0(j, s):
                if s == 1:
                    pe.wait_ge(v_copied, 4 * j + 2)
                for b in range(2):
                    c = 2 * NH * HD + 384 * b
                    for n, (x, wt) in enumerate(split5(wh1, wl1, c, c + 384)):
                        mm = nc.tensor.matmul(ps[0:R, 6 + b, 0:384], xT[:, x, s * R:(s + 1) * R], wt,
                                              start=(n == 0), stop=(n == 4))
                    mm.then_inc(v_done, 1)

            def turned0(i, s):
                pe.wait_ge(resid_done, 2 * i)
                for b in range(3):
                    pe.wait_ge(exp_ready, 6 * i + 3 * s + b + 1)
                    for m in range(4):
                        n = 4 * b + m
                        mm = nc.tensor.transpose(ps[0:R, 3 * s + b, m * R:(m + 1) * R], prob[:, s, n * R:(n + 1) * R],
                                                 ident[0:R, 0:R])
                    mm.then_inc(turned, 1)

            def weighted0(i, s):
                pe.wait_ge(p_ready, 6 * i + 3 * s + 3)
                if s == 0:
                    pe.wait_ge(v_copied, 4 * i + 4)
                else:
                    pe.wait_ge(o_ready, 2 * i + 1)
                for b in range(2):
                    for m in range(6):
                        n = 6 * b + m
                        mm = nc.tensor.matmul(ps[0:R, 6 + b, m * (HD + 1):(m + 1) * (HD + 1)],
                                              Pt[:, s, n * R:(n + 1) * R], V[:, s, n, :], start=True, stop=True)
                    mm.then_inc(pv_done, 1)

            def outputs_turned0(i, s):
                pe.wait_ge(o_ready, 2 * i + 2)
                for b, (c0, c1) in enumerate(((0, 4), (4, 6))):
                    for c in range(c0, c1):
                        mm = nc.tensor.transpose(ps[:, (6, 0)[s] + b, (c - c0) * R:(c - c0 + 1) * R],
                                                 O[:, s, 128 * c:128 * c + 128], ident[0:R, 0:R])
                    mm.then_inc(ot_done, 1)

            def outputs0(i, s):
                pe.wait_ge(ot_copied, 4 * i + 2 * s + 2)
                for c in range(6):
                    mm = nc.tensor.matmul(ps[0:R, 2 + s, 0:D], OT[:, s, c, :], wo1[:, c, :],
                                          start=(c == 0), stop=(c == 5))
                mm.then_inc(op_done, 1)

            def attention0_tensor(i, ahead):
                turned0(i, 0)
                if ahead:
                    rows_in0(i + 1)
                turned0(i, 1)
                if ahead:
                    queries_keys0(i + 1)
                weighted0(i, 0)
                if ahead:
                    scores0(i + 1, 0)
                weighted0(i, 1)
                if ahead:
                    scores0(i + 1, 1)
                outputs_turned0(i, 0)
                if ahead:
                    pe.wait_ge(less_ready, 6 * i + 9)
                outputs_turned0(i, 1)
                outputs0(i, 0)
                if ahead:
                    values0(i + 1, 0)
                    pe.wait_ge(less_ready, 6 * i + 12)
                outputs0(i, 1)
                if ahead:
                    values0(i + 1, 1)

            rows_in0(0)
            queries_keys0(0, first=True)
            for s in range(2):
                scores0(0, s)
            for s in range(2):
                values0(0, s)
            with pe.Fori(0, PAIRS - 1) as i:
                attention0_tensor(i, True)
            attention0_tensor(PAIRS - 1, False)
            pe.wait_ge(resid_done, TILES)
            pe.wait_ge(Q["ready"], 2)
            pe.wait_ge(consts_ready, 1)

            def rows_in(call, added):
                pe.wait_ge(F["q1"], call + 1)
                pe.wait_ge(F["resid"], added)
                for s in range(2):
                    for k in range(2):
                        tr = nc.tensor.transpose(psb[:, s, k * (R + 1):k * (R + 1) + R], q1[:, s, 128 * k:128 * k + 128],
                                                 identb[0:R, 0:R])
                    tr.then_inc(F["tr1"], 1)

            def up_tensor(j):
                pe.wait_ge(F["q1T"], 2 * j + 2)
                pe.wait_ge(F["z"], 2 * j)
                for s in range(2):
                    for part in range(2):
                        for k in range(2):
                            mm = nc.tensor.matmul(ps[0:R, 2 + 2 * s + part, :], q1T[:, s, k, 0:R],
                                                  wq_in[:, k, part * HF:(part + 1) * HF], start=(k == 0), stop=(k == 1))
                    mm.then_inc(F["up"], 1)

            def ffn_tensor(i, ahead):
                if ahead:
                    up_tensor(i + 1)
                pe.wait_ge(F["q2"], i + 1)
                pe.wait_ge(F["q2T"], 2 * i)
                for s in range(2):
                    for k in range(4):
                        tr = nc.tensor.transpose(psb[:, 6 + s, k * (R + 1):k * (R + 1) + R],
                                                 q2[:, s, 128 * k:128 * k + 128], identb[0:R, 0:R])
                    tr.then_inc(F["tr2"], 1)
                pe.wait_ge(F["q1T"], 2 * PAIRS + 2 if not ahead else 2 * i + 4)
                for s in range(2):
                    pe.wait_ge(F["q2T"], 2 * i + s + 1)
                    for k in range(4):
                        mm = nc.tensor.matmul(ps[0:R, s, 0:D], q2T[:, s, k, 0:R], wq_out[:, k, :],
                                              start=(k == 0), stop=(k == 3))
                    mm.then_inc(F["down"], 1)
                if ahead:
                    rows_in(i + 2, 2 * i + 2)

            rows_in(0, 0)
            up_tensor(0)
            rows_in(1, 0)
            with pe.Fori(0, PAIRS - 1) as i:
                ffn_tensor(i, True)
            ffn_tensor(PAIRS - 1, False)

            pe.wait_ge(F["resid"], TILES)
            pe.wait_ge(F["q1T"], 2 * (PAIRS + 1))
            pe.wait_ge(w3_ready, PAIRS)
            pe.wait_ge(A1["const_in"], A1["const_in before"] + 144)
            pe.wait_ge(A1["clear"], A1["clear before"] + 3)

            def project(c, bank, o):
                for n, (k, wt) in enumerate(split5(wh3, wl3, c, c + 128)):
                    mm = nc.tensor.matmul(ps[:, bank, o:o + R2], wt, xT[:, k, :], start=(n == 0), stop=(n == 4))
                return mm

            def rows_in1(L, A, j, banks):
                pe.wait_ge(L["xs"], L["xs before"] + j + 1)
                pe.wait_ge(A["v_out"], A["v_out before"] + 2 * j)
                transposes(L, 0, banks[0])
                transposes(L, 1, banks[1])

            def values(A, c, bank):
                for s in range(2):
                    for n, (k, wt) in enumerate(split5(wh3, wl3, c, c + D)):
                        mm = nc.tensor.matmul(ps[0:R, bank + s, 0:D], xT[:, k, s * R:(s + 1) * R], wt,
                                              start=(n == 0), stop=(n == 4))
                    mm.then_inc(A["v"], 1)

            def pv_products(A, i, s):
                pe.wait_ge(A["v_out"], A["v_out before"] + 2 * i + 2)
                pe.wait_ge(A["resid"], A["resid before"] + 2 * i)
                for n in range(NH):
                    mm = nc.tensor.matmul(ps[0:R, 6 + s, n * (HE + 1):(n + 1) * (HE + 1)], Pt1[:, s, n * R:(n + 1) * R],
                                          V1[:, s, n, :], start=True, stop=True)
                mm.then_inc(A["pv"], 1)

            def outputs_turned(A, i):
                for s in range(2):
                    pe.wait_ge(A["o"], A["o before"] + 2 * i + s + 1)
                    for c in range(2):
                        tr = nc.tensor.transpose(ps[:, 6 + s, c * R:(c + 1) * R], O1[:, s, 128 * c:128 * c + 128],
                                                 ident[0:R, 0:R])
                    tr.then_inc(A["ot"], 1)

            def project_out(A, i, layer):
                for s in range(2):
                    pe.wait_ge(A["ot_out"], A["ot_out before"] + 2 * i + s + 1)
                    for c in range(2):
                        mm = nc.tensor.matmul(ps[0:R, 6 + s, 256:256 + D], OT1[:, s, c, :], proj[:, layer, c, :],
                                              start=(c == 0), stop=(c == 1))
                    mm.then_inc(A["op"], 1)

            def queries_keys(j):
                pe.wait_ge(A1["tr_dve"], A1["tr_dve before"] + j + 1)
                pe.wait_ge(A1["tr_act"], A1["tr_act before"] + j + 1)
                for g in range(3):
                    project(128 * g, g, 0).then_inc(A1["q"], 1)
                    project(384 + 128 * g, 3 + g, 0)
                    project(768 + 128 * g, 3 + g, R2).then_inc(A1["k"], 1)

            def scores1(j, s):
                for b in range(3):
                    if s == 0:
                        pe.wait_ge(A1["qz"], A1["qz before"] + 3 * j + b + 1)
                        pe.wait_ge(A1["kt"], A1["kt before"] + 3 * j + b + 1)
                    nc.tensor.matmul(ps[0:R, 3 * s + b, :].rearrange("p (n r) -> p n r", n=4)[:, :, 0:R],
                                     KT1[:, b, s * R:(s + 1) * R], Qz1[:, s, 4 * b:4 * b + 4, :],
                                     start=True, stop=True).then_inc(A1["s"], 1)

            def attention1_tensor(i, ahead):
                if ahead:
                    rows_in1(L3, A1, i + 1, (2, 3))
                    queries_keys(i + 1)
                for s in range(2):
                    pe.wait_ge(A1["pt"], A1["pt before"] + 2 * i + s + 1)
                    pv_products(A1, i, s)
                    if ahead:
                        scores1(i + 1, s)
                outputs_turned(A1, i)
                project_out(A1, i, 0)
                if ahead:
                    pe.wait_ge(A1["own"], A1["own before"] + 4 * i + 8)
                    values(A1, W34 - D, 4)

            rows_in1(L3, A1, 0, (2, 3))
            queries_keys(0)
            for s in range(2):
                scores1(0, s)
            pe.wait_ge(A1["own"], A1["own before"] + 4)
            values(A1, W34 - D, 4)
            with pe.Fori(0, PAIRS - 1) as i:
                attention1_tensor(i, True)
            attention1_tensor(PAIRS - 1, False)
            pe.wait_ge(A1["resid"], A1["resid before"] + TILES)

            def project_rows(j, first=False):
                if not first:
                    pe.wait_ge(A2["p"], A2["p before"] + 6 * j - 3)
                for g in range(3):
                    project(W34 + 128 * g, g, 0).then_inc(A2["q"], 1)
                pe.wait_ge(A2["p"], A2["p before"] + 6 * j)
                for g in range(3):
                    project(W34 + 384 + 128 * g, 3 + g, 0).then_inc(A2["k"], 1)

            def scores2(j, s):
                pe.wait_ge(A2["qz"], A2["qz before"] + 3 * j + 3)
                pe.wait_ge(A2["kt"], A2["kt before"] + 3 * j + 3)
                for b in range(3):
                    nc.tensor.matmul(ps[0:R, 3 * s + b, 0:4 * R], query_rows[:, 1, :], key_cols[:, :],
                                     start=True, stop=False)
                    for n in range(4):
                        mm = nc.tensor.matmul(ps[0:R, 3 * s + b, n * R:(n + 1) * R], Qz1[:, s, 4 * b + n, :],
                                              KT1[:, b, s * R:(s + 1) * R], start=False, stop=(n == 3))
                mm.then_inc(A2["s"], 1)

            def attention2_tensor(i, ahead):
                for s in range(2):
                    if s == 1 and ahead:
                        rows_in1(L4, A2, i + 1, (6, 7))
                    for b in range(3):
                        pe.wait_ge(A2["exp"], A2["exp before"] + 6 * i + 3 * s + b + 1)
                        for m in range(4):
                            n = 4 * b + m
                            mm = nc.tensor.transpose(ps[0:R, 3 * s + b, m * R:(m + 1) * R],
                                                     prob[:, s, n * R:(n + 1) * R], ident[0:R, 0:R])
                        mm.then_inc(A2["turned"], 1)
                if ahead:
                    pe.wait_ge(A2["tr_dve"], A2["tr_dve before"] + i + 2)
                    pe.wait_ge(A2["tr_act"], A2["tr_act before"] + i + 2)
                    project_rows(i + 1)
                for s in range(2):
                    pe.wait_ge(A2["p"], A2["p before"] + 6 * i + 3 * s + 3)
                    pv_products(A2, i, s)
                    if ahead:
                        scores2(i + 1, s)
                outputs_turned(A2, i)
                project_out(A2, i, 1)
                if ahead:
                    pe.wait_ge(A2["resid"], A2["resid before"] + 2 * i + 2)
                    values(A2, WCOLS - D, 6)

            rows_in1(L4, A2, 0, (6, 7))
            pe.wait_ge(A2["tr_dve"], A2["tr_dve before"] + 1)
            pe.wait_ge(A2["tr_act"], A2["tr_act before"] + 1)
            project_rows(0, first=True)
            for s in range(2):
                scores2(0, s)
            values(A2, WCOLS - D, 6)
            with pe.Fori(0, PAIRS - 1) as i:
                attention2_tensor(i, True)
            attention2_tensor(PAIRS - 1, False)
            pe.wait_ge(A2["resid"], A2["resid before"] + TILES)
            pe.wait_ge(RT["split"], 1)
            with pe.Fori(0, PAIRS) as i:
                pe.wait_ge(L5["xs"], L5["xs before"] + i + 1)
                pe.wait_ge(RT["xm"], 2 * i)
                transposes(L5, 0, 0)
                transposes(L5, 1, 1)
                pe.wait_ge(RT["tr_act"], 2 * i + 2)
                pe.wait_ge(RT["raw"], 2 * i)
                for s in range(2):
                    for n, (k, wt) in enumerate(split5(router_h, router_l, 0, E)):
                        mm = nc.tensor.matmul(ps[0:R, 2 + s, 0:E], xT[:, k, s * R:(s + 1) * R], wt,
                                              start=(n == 0), stop=(n == 4))
                    mm.then_inc(RT["logits"], 1)
            pe.wait_ge(RT["raw"], TILES)
            pe.wait_ge(RT["xm"], TILES)

            def experts_tensor(e, q, c, tiles):
                base = 36 * e + 6 * c
                cols = tiles * R
                at = c * (E_CHUNK * R)
                pe.wait_ge(EX["lo"], 12 * e + 12)
                for step in range(FM + 2):
                    if step < FM:
                        m = step
                        if m < 4:
                            pe.wait_ge(EX["gelu"], base)
                        else:
                            pe.wait_ge(EX["gelu"], base + m - 3)
                        for n, (k, wt) in enumerate(split5(eh1[q], el1[q], 128 * m, 128 * m + 128)):
                            mm = nc.tensor.matmul(ps[:, m % 4, 0:cols], wt, xTm[:, k, bass.ds(at, cols)],
                                                  start=(n == 0), stop=(n == 4))
                        mm.then_inc(EX["half"], 1)
                    if step >= 2:
                        k = step - 2
                        pe.wait_ge(EX["gl"], base + k + 1)
                        if k == 0:
                            pe.wait_ge(EX["acc"], TILES * e + 4 * c)
                        for tt in range(tiles):
                            rows = slice(tt * R, (tt + 1) * R)
                            nc.tensor.matmul(ps[0:R, 4 + tt, 0:D], gh[:, k, rows], eh2[q][:, k, :],
                                             start=(k == 0), stop=False)
                            nc.tensor.matmul(ps[0:R, 4 + tt, 0:D], gh[:, k, rows], el2[q][:, k, :],
                                             start=False, stop=False)
                            mm = nc.tensor.matmul(ps[0:R, 4 + tt, 0:D], gl[:, k, rows], eh2[q][:, k, :],
                                                  start=False, stop=(k == FM - 1))
                            if k == FM - 1:
                                mm.then_inc(EX["down"], 1)

            with pe.Fori(0, E // 2) as pair:
                for q in range(2):
                    with pe.Fori(0, TILES // E_CHUNK) as c:
                        experts_tensor(2 * pair + q, q, c, E_CHUNK)
                    experts_tensor(2 * pair + q, q, TILES // E_CHUNK, TILES % E_CHUNK)

        @block.scalar
        def _(act):
            act.wait_ge(cleared, 3)
            with act.Fori(0, GROUPS // 2) as i:
                for p in range(2):
                    for k in range(NK):
                        for half in range(2):
                            n = 12 * p + 2 * k + half
                            act.wait_ge(pt_done, 24 * i + n + 1)
                            slots = PT[p][:, k, :].rearrange("p (b s) -> p b s", s=S)[:, :, 1:S]
                            slots = slots.rearrange("p b (g w) -> p w b g", w=GRID)
                            nc.scalar.copy(slots[:, 3 * half:3 * half + 3, :, :],
                                           ps[:, n % 4, 0:3 * GROWS].rearrange("p (w b g) -> p w b g", w=3, b=GI)
                                           ).then_inc(pt_copied, 1)
            act.wait_ge(pos_in, 16 * (IPT + 3))
            act.wait_ge(qz_clear, 1)

            def transposed0(j):
                act.wait_ge(L1["tr"], L1["tr before"] + 2 * j + 2)
                act.wait_ge(v_done, 4 * j)
                nc.scalar.copy(xT[:, :, R:R2], ps[:, 7, 0:3 * R].rearrange("p (c r) -> p c r", c=3)
                               ).then_inc(tr_copied_act, 1)

            def queries0(j):
                act.wait_ge(s_done, 2 * j)
                for g in range(3):
                    act.wait_ge(qk_done, 6 * j + g + 1)
                    for n2 in range(2):
                        for hh in range(2):
                            n = 4 * g + 2 * n2 + hh
                            rows = slice(64 * hh, 64 * hh + 64)
                            nc.scalar.activation(Qz[rows, :, n, :],
                                                 ps[rows, g, n2 * R2:(n2 + 1) * R2].rearrange("p (s r) -> p s r", s=2),
                                                 ACT.Identity, bias=bqk[rows, n // 2:n // 2 + 1]).then_inc(q_copied, 1)

            def exponentials0(j):
                for s in range(2):
                    for b in range(3):
                        act.wait_ge(less_ready, 6 * j + 3 * s + b + 1)
                        part = prob[:, s, b * 4 * R:(b + 1) * 4 * R]
                        nc.scalar.activation(part, part, ACT.Exp, scale=float(HD) ** -0.5).then_inc(exp_ready, 1)

            def attention0_scalar(i, ahead):
                act.wait_ge(pv_done, 4 * i)
                for s in range(2):
                    for b in range(3):
                        act.wait_ge(turned, 6 * i + 3 * s + b + 1)
                        nc.scalar.copy(Pt[:, s, b * 4 * R:(b + 1) * 4 * R], ps[0:R, 3 * s + b, 0:4 * R]
                                       ).then_inc(p_ready, 1)
                    if s == 0 and ahead:
                        transposed0(i + 1)
                if ahead:
                    queries0(i + 1)
                for s in range(2):
                    for b, (c0, c1) in enumerate(((0, 4), (4, 6))):
                        act.wait_ge(ot_done, 4 * i + 2 * s + b + 1)
                        nc.scalar.copy(OT[:, s, c0:c1, :],
                                       ps[:, (6, 0)[s] + b, 0:(c1 - c0) * R].rearrange(
                                           "p (c r) -> p c r", r=R)).then_inc(ot_copied, 1)
                if ahead:
                    exponentials0(i + 1)

            transposed0(0)
            queries0(0)
            exponentials0(0)
            with act.Fori(0, PAIRS - 1) as i:
                attention0_scalar(i, True)
            attention0_scalar(PAIRS - 1, False)
            act.wait_ge(resid_done, TILES)
            act.wait_ge(F["clear"], 1)

            def rows_act(call):
                for s in range(2):
                    act.wait_ge(L2["y"], L2["y before"] + 2 * call + s + 1)
                    act.wait_ge(F["ssq1"], 2 * call)
                    nc.scalar.activation(junk1[:, s, :], yn[:, s, :], ACT.Square, scale=float(D) ** -0.5,
                                         accum_out=ss[0][:, s:s + 1]
                                         ).then_inc(F["ssq1"], 1)

            def rows_round(call):
                act.wait_ge(F["small1"], 2 * call + 2)
                act.wait_ge(F["q1"], call)
                for s in range(2):
                    nc.scalar.activation(t1[:, s, :], xn[:, s, :], ACT.Identity, bias=magic[:, :],
                                         scale=qscale[0][:, s:s + 1]).then_inc(F["t1"], 1)

            def rows_out(call):
                act.wait_ge(F["up"], 2 * call)
                for s in range(2):
                    act.wait_ge(F["tr1"], 2 * call + s + 1)
                    nc.scalar.copy(q1T[:, s, :, 0:R], psb[:, s, 0:2 * (R + 1)].rearrange("p (k r) -> p k r", k=2)[:, :, 0:R]
                                   ).then_inc(F["q1T"], 1)

            def gates(j):
                for s in range(2):
                    act.wait_ge(F["up"], 2 * j + s + 1)
                    act.wait_ge(F["z"], 2 * j)
                    nc.scalar.activation(sg[:, s, :], ps[0:R, 3 + 2 * s, :], ACT.Silu, scale=dscale[0][:, s:s + 1]
                                         ).then_inc(F["sg"], 1)

            def ffn_scalar(i, ahead):
                act.wait_ge(F["ssq2"], 2 * i)
                for s in range(2):
                    act.wait_ge(F["z"], 2 * i + s + 1)
                    nc.scalar.activation(junk2[:, s, :], z[:, s, :], ACT.Square, scale=float(HF) ** -0.5,
                                         accum_out=ss[1][:, s:s + 1]).then_inc(F["ssq2"], 1)
                if ahead:
                    gates(i + 1)
                act.wait_ge(F["small2"], 2 * i + 2)
                act.wait_ge(F["q2"], i)
                for s in range(2):
                    nc.scalar.activation(t2[:, s, :], zn[:, s, :], ACT.Identity, bias=magic[:, :],
                                         scale=qscale[1][:, s:s + 1]).then_inc(F["t2"], 1)
                if ahead:
                    rows_act(i + 2)
                act.wait_ge(F["down"], 2 * i)
                for s in range(2):
                    act.wait_ge(F["tr2"], 2 * i + s + 1)
                    nc.scalar.copy(q2T[:, s, :, 0:R], psb[:, 6 + s, 0:4 * (R + 1)].rearrange("p (k r) -> p k r", k=4)
                                   [:, :, 0:R]).then_inc(F["q2T"], 1)
                if ahead:
                    rows_round(i + 2)
                    rows_out(i + 2)

            rows_act(0)
            rows_round(0)
            rows_out(0)
            rows_act(1)
            gates(0)
            rows_round(1)
            rows_out(1)
            with act.Fori(0, PAIRS - 1) as i:
                ffn_scalar(i, True)
            ffn_scalar(PAIRS - 1, False)

            act.wait_ge(F["resid"], TILES)
            act.wait_ge(A1["clear"], A1["clear before"] + 3)

            def transposed_act(L, A, j):
                act.wait_ge(A["v"], A["v before"] + 2 * j)
                for s in range(2):
                    act.wait_ge(L["tr"], L["tr before"] + 2 * j + s + 1)
                    nc.scalar.copy(xT[:, :, s * R:(s + 1) * R], ps[:, 2 + s, 0:3 * R].rearrange("p (c r) -> p c r", c=3)
                                   ).then_inc(A["tr_act" if s else "tr_dve"], 1)

            def values_act(A, j, bank=6):
                act.wait_ge(A["pv"], A["pv before"] + 2 * j)
                for s in range(2):
                    act.wait_ge(A["v"], A["v before"] + 2 * j + s + 1)
                    nc.scalar.copy(V1[:, s, :, 0:HE], ps[0:R, bank + s, 0:D].rearrange("p (n e) -> p n e", n=NH)
                                   ).then_inc(A["v_out"], 1)

            def outputs_act(A, i):
                act.wait_ge(A["op"], A["op before"] + 2 * i)
                for s in range(2):
                    act.wait_ge(A["ot"], A["ot before"] + 2 * i + s + 1)
                    nc.scalar.copy(OT1[:, s, :, :], ps[:, 6 + s, 0:R2].rearrange("p (c r) -> p c r", c=2)
                                   ).then_inc(A["ot_out"], 1)

            def own_act(j):
                act.wait_ge(A1["rown"], A1["rown before"] + 2 * j)
                for s in range(2):
                    act.wait_ge(A1["s"], A1["s before"] + 6 * j + 3 * s + 3)
                    scores = ps[0:R, 3 * s:3 * s + 3, :].rearrange("p b (n c) -> p (b n) c", n=4)
                    nc.scalar.activation(own[:, s, :].rearrange("p (n q) -> p n q", n=NH), scores[:, :, 0:S],
                                         ACT.Identity, bias=tiny[:, :], scale=image[:, 0:1]).then_inc(A1["own0"], 1)

            def gelus(j):
                for s in range(2):
                    act.wait_ge(A1["own"], A1["own before"] + 4 * j + 2 * s + 2)
                    act.wait_ge(A1["wt"], A1["wt before"] + 2 * j)
                    nc.scalar.activation(gel[:, s, :], own[:, s, :], ACT.Gelu, scale=2.0 ** 0.5 * float(HE) ** -0.5
                                         ).then_inc(A1["gel"], 1)

            def attention1_act(i, ahead):
                if ahead:
                    nc.scalar.activation(spare[:, :], tiny[:, :], ACT.Gelu)
                    transposed_act(L3, A1, i + 1)
                    own_act(i + 1)
                outputs_act(A1, i)
                if ahead:
                    gelus(i + 1)
                    values_act(A1, i + 1, 4)

            act.wait_ge(A1["const_in"], A1["const_in before"] + 144)
            transposed_act(L3, A1, 0)
            own_act(0)
            gelus(0)
            values_act(A1, 0, 4)
            with act.Fori(0, PAIRS - 1) as i:
                attention1_act(i, True)
            attention1_act(PAIRS - 1, False)
            act.wait_ge(A1["resid"], A1["resid before"] + TILES)

            def keys_act(j):
                act.wait_ge(A2["s"], A2["s before"] + 2 * j)
                for g in range(3):
                    act.wait_ge(A2["k"], A2["k before"] + 3 * j + g + 1)
                    nc.scalar.copy(KT1[:, g, :], ps[:, 3 + g, 0:R2]).then_inc(A2["kt"], 1)

            def exponentials(j, s):
                for b in range(3):
                    act.wait_ge(A2["less"], A2["less before"] + 6 * j + 3 * s + b + 1)
                    part = prob[:, s, b * 4 * R:(b + 1) * 4 * R]
                    nc.scalar.activation(part, part, ACT.Exp, scale=float(HE) ** -0.5).then_inc(A2["exp"], 1)

            def attention2_act(i, ahead):
                act.wait_ge(A2["pv"], A2["pv before"] + 2 * i)
                for s in range(2):
                    for b in range(3):
                        act.wait_ge(A2["turned"], A2["turned before"] + 6 * i + 3 * s + b + 1)
                        nc.scalar.copy(Pt1[:, s, b * 4 * R:(b + 1) * 4 * R], ps[0:R, 3 * s + b, 0:4 * R]
                                       ).then_inc(A2["p"], 1)
                if ahead:
                    keys_act(i + 1)
                    exponentials(i + 1, 0)
                outputs_act(A2, i)
                if ahead:
                    values_act(A2, i + 1)
                    exponentials(i + 1, 1)

            keys_act(0)
            values_act(A2, 0)
            for s in range(2):
                exponentials(0, s)
            with act.Fori(0, PAIRS - 1) as i:
                attention2_act(i, True)
            attention2_act(PAIRS - 1, False)
            act.wait_ge(A2["resid"], A2["resid before"] + TILES)
            with act.Fori(0, PAIRS) as i:
                act.wait_ge(L5["tr"], L5["tr before"] + 2 * i + 2)
                act.wait_ge(RT["logits"], 2 * i)
                src = ps[:, 0:2, 0:3 * R].rearrange("p s (c r) -> p s c r", c=3)
                for s in range(2):
                    nc.scalar.copy(xT[:, :, s * R:(s + 1) * R], src[:, s, :, :]).then_inc(RT["tr_act"], 1)
                for s in range(2):
                    nc.scalar.copy(xTm[:, :, bass.ds(i * R2 + s * R, R)], src[:, s, :, :]).then_inc(RT["xm"], 1)
                for s in range(2):
                    act.wait_ge(RT["logits"], 2 * i + s + 1)
                    nc.scalar.copy(logits[:, 0, bass.ds(2 * i + s, 1), :], ps[0:R, 2 + s, 0:E].unsqueeze(1)
                                   ).then_inc(RT["raw"], 1)
            act.wait_ge(RT["k2"], 1)
            nc.scalar.activation(pr[:, 1, :], pr[:, 0, :], ACT.Exp).then_inc(RT["ex"], 1)
            def experts_scalar(e, c, tiles):
                base = 36 * e + 6 * c
                for m in range(FM):
                    act.wait_ge(EX["half"], base + m + 1)
                    if m < 2:
                        act.wait_ge(EX["gl"], base)
                    else:
                        act.wait_ge(EX["gl"], base + m - 1)
                    nc.scalar.activation(graw[:, m % 2, 0:tiles * R], ps[:, m % 4, 0:tiles * R], ACT.Gelu
                                         ).then_inc(EX["gelu"], 1)

            act.wait_ge(A2["resid"], A2["resid before"] + TILES)
            with act.Fori(0, E) as e:
                with act.Fori(0, TILES // E_CHUNK) as c:
                    experts_scalar(e, c, E_CHUNK)
                experts_scalar(e, TILES // E_CHUNK, TILES % E_CHUNK)

        @block.vector
        def _(dve):
            nc.vector.memset(h[:, TILES:TILES_ALL, :], 0.0).then_inc(chain, 1)
            dve.wait_ge(const_in, 16)
            dve.wait_ge(ident_in, 16)
            nc.vector.tensor_copy(identb[:, :], ident[:, :]).then_inc(consts_copied, 1)
            nc.vector.tensor_copy(query_rows[:, :, :], mask_in[:, 0:2 * R].rearrange("p (a r) -> p a r", a=2)
                                  ).then_inc(consts_copied, 1)
            nc.vector.tensor_copy(key_cols[:, :], mask_in[:, 2 * R:6 * R]).then_inc(consts_copied, 1)
            dve.wait_ge(consts_copied, 3)
            dve.wait_ge(pos_in, 16 * (IPT + 3))
            nc.vector.tensor_tensor(posb[:, :], posb[:, :], bo_t[:, :], ALU.add).then_inc(pos_ready, 1)
            dve.wait_ge(pos_ready, 1)
            dve.wait_ge(chain, 1)
            def tokens(i):
                for n in range(2 * GT):
                    dve.wait_ge(tok_done, 12 * i + n + 1)
                    nc.vector.tensor_tensor(h[:, 2 * GT * i + n, :], ps[0:R, 4 + n % 4, 0:D], posb[:, :],
                                            ALU.add).then_inc(tok_h, 1)

            tokens(0)
            dve.wait_ge(cleared, 6)
            dve.wait_ge(tok_h, 2 * GT)
            ln_vector(dve, L1, 0)
            dve.wait_ge(L1["y"], 2)
            split_vector(dve, L1, 0, yn)
            dve.wait_ge(w1_in, 16)
            nc.vector.tensor_copy(wh1[:, :, :], stage1[:, :, :]).then_inc(w1_hi, 1)
            dve.wait_ge(w1_hi, 1)
            nc.vector.tensor_tensor(wl1[:, :, :], stage1[:, :, :], wh1[:, :, :].bitcast(F32),
                                    ALU.subtract).then_inc(w1_ready, 1)
            dve.wait_ge(Q["in"], 32)
            for n, src in enumerate((win_in, wout_in)):
                nc.vector.tensor_reduce(wsum[:, n:n + 1], src[:, :, :], AX.XY, ALU.add, apply_absolute_value=True
                                        ).then_inc(Q["summed"], 1)
            dve.wait_ge(Q["all"], 1)
            for n, size in enumerate((2 * HF * D, HF * D)):
                nc.vector.tensor_scalar(wmean[:, n:n + 1], wall[:, n:n + 1], 1.0 / size, 1e-5, ALU.mult, ALU.max
                                        ).then_inc(Q["step"], 1)
            dve.wait_ge(Q["step"], 2)
            nc.vector.reciprocal(wrec[:, :], wmean[:, :]).then_inc(Q["step"], 1)
            nc.vector.tensor_scalar(w127[:, :], wmean[:, :], 1.0 / 127.0, None, ALU.mult).then_inc(Q["step"], 1)
            dve.wait_ge(Q["step"], 4)
            for n, src in enumerate((win_in, wout_in)):
                nc.vector.tensor_scalar(src[:, :, :], src[:, :, :], wrec[:, n:n + 1], MAGIC, ALU.mult, ALU.add
                                        ).then_inc(Q["step"], 1)
            dve.wait_ge(Q["step"], 6)
            for n, src in enumerate((win_in, wout_in)):
                nc.vector.tensor_scalar(src[:, :, :], src[:, :, :], MAGIC, 1.0, ALU.subtract, ALU.min
                                        ).then_inc(Q["step"], 1)
            dve.wait_ge(Q["step"], 8)
            for src, dst in ((win_in, wq_in), (wout_in, wq_out)):
                nc.vector.tensor_scalar(dst[:, :, :], src[:, :, :], -1.0, None, ALU.max).then_inc(Q["ready"], 1)
            tokens(1)
            nc.vector.memset(mv[0:1, 0, 0:1], 0.0).then_inc(consts_ready, 1)
            dve.wait_ge(consts_ready, 1)
            dve.wait_ge(tok_h, TILES_ALL)
            dve.wait_ge(cleared, 6)

            def transposed0(j):
                dve.wait_ge(L1["tr"], L1["tr before"] + 2 * j + 1)
                dve.wait_ge(v_done, 4 * j)
                nc.vector.tensor_copy(xT[:, :, 0:R], ps[:, 6, 0:3 * R].rearrange("p (c r) -> p c r", c=3)
                                      ).then_inc(tr_copied_dve, 1)

            def keys0(j):
                dve.wait_ge(s_done, 2 * j)
                for g in range(3):
                    dve.wait_ge(qk_done, 6 * j + g + 4)
                    for n2 in range(2):
                        m = 2 * g + n2
                        nc.vector.tensor_scalar(KT[:, m, :], ps[:, 3 + g, n2 * R2:(n2 + 1) * R2], bqk[:, 6 + m:7 + m],
                                                None, ALU.add).then_inc(k_copied, 1)

            def values0(j, s):
                dve.wait_ge(pv_done, 4 * j)
                for b in range(2):
                    dve.wait_ge(v_done, 4 * j + 2 * s + b + 1)
                    nc.vector.tensor_tensor(V[:, s, 6 * b:6 * b + 6, 0:HD],
                                            ps[0:R, 6 + b, 0:384].rearrange("p (n e) -> p n e", n=6),
                                            bv_t[:, 384 * b:384 * b + 384].rearrange("p (n e) -> p n e", n=6),
                                            ALU.add).then_inc(v_copied, 1)

            def maximum0(j, s):
                dve.wait_ge(s_done, 2 * j + s + 1)
                scores = ps[0:R, 3 * s:3 * s + 3, 0:4 * R].rearrange("p b (n r) -> p b n r", n=4)
                nc.vector.tensor_reduce(peak[:, s, :], scores, AX.X, ALU.max).then_inc(peak_ready, 1)
                dve.wait_ge(peak_ready, 2 * j + s + 1)
                dve.wait_ge(turned, 6 * j)
                for b in range(3):
                    nc.vector.tensor_tensor(prob[:, s, b * 4 * R:(b + 1) * 4 * R].rearrange("p (n r) -> p n r", n=4),
                                            scores[:, b, :, :],
                                            peak[:, s, 4 * b:4 * b + 4].unsqueeze(2).to_broadcast([R, 4, R]),
                                            ALU.subtract).then_inc(less_ready, 1)

            def split_weights(i):
                cols = bass.ds(i * WSTEP, WSTEP)
                nc.vector.tensor_copy(wh3[:, :, cols], wst3[:, :, cols]).then_inc(w3_hi, 1)
                dve.wait_ge(w3_hi, i + 1)
                nc.vector.tensor_tensor(wl3[:, :, cols], wst3[:, :, cols], wh3[:, :, cols].bitcast(F32),
                                        ALU.subtract).then_inc(w3_ready, 1)

            def normalise0(i, s):
                heads = ps[0:R, 6:8, 0:6 * (HD + 1)].rearrange("p b (n e) -> p b n e", n=6)
                dve.wait_ge(pv_done, 4 * i + 2 * s + 2)
                nc.vector.reciprocal(rden[:, s, :].rearrange("p (b n) -> p b n", b=2),
                                     heads[:, :, :, HD]).then_inc(rden_ready, 1)
                dve.wait_ge(rden_ready, 2 * i + s + 1)
                dve.wait_ge(ot_done, 4 * i)
                nc.vector.tensor_tensor(O[:, s, :].rearrange("p (b n e) -> p b n e", b=2, n=6),
                                        heads[:, :, :, 0:HD],
                                        rden[:, s, :].rearrange("p (b n) -> p b n", b=2).unsqueeze(3)
                                        .to_broadcast([R, 2, 6, HD]), ALU.mult).then_inc(o_ready, 1)

            def residual0(i, s):
                dve.wait_ge(hb_done, 2 * i + 2)
                dve.wait_ge(op_done, 2 * i + s + 1)
                nc.vector.tensor_tensor(h[:, 2 * i + s, :], ps[0:R, 2 + s, 0:D], h[:, 2 * i + s, :],
                                        ALU.add).then_inc(resid_done, 1)

            def rows0(j):
                dve.wait_ge(L1["y"], L1["y before"] + 2 * j + 2)
                split_vector(dve, L1, j, yn)

            def attention0_vector(i, ahead):
                if ahead:
                    ln_stats(dve, L1, i + 2)
                    transposed0(i + 1)
                    ln_apply(dve, L1, i + 2)
                    rows0(i + 2)
                split_weights(i)
                if ahead:
                    keys0(i + 1)
                normalise0(i, 0)
                if ahead:
                    maximum0(i + 1, 0)
                normalise0(i, 1)
                if ahead:
                    maximum0(i + 1, 1)
                else:
                    ln_vector(dve, L2, 0)
                residual0(i, 0)
                if ahead:
                    values0(i + 1, 0)
                residual0(i, 1)
                if ahead:
                    values0(i + 1, 1)

            transposed0(0)
            ln_vector(dve, L1, 1)
            rows0(1)
            dve.wait_ge(w3_in, 16)
            dve.wait_ge(qz_clear, 2)
            keys0(0)
            for s in range(2):
                maximum0(0, s)
            for s in range(2):
                values0(0, s)
            with dve.Fori(0, PAIRS - 1) as i:
                attention0_vector(i, True)
            attention0_vector(PAIRS - 1, False)
            dve.wait_ge(resid_done, TILES)
            dve.wait_ge(F["gain_in"], 32)
            dve.wait_ge(F["clear"], 2)

            def largest(k, call, rows):
                nc.vector.tensor_reduce(amax[k][:, :], rows, AX.X, ALU.max, apply_absolute_value=True
                                        ).then_inc(F[f"amax{k + 1}"], 1)

            def scales(k, call):
                dve.wait_ge(F[f"rms{k + 1}"], call + 1)
                dve.wait_ge(F[f"amax{k + 1}"], call + 1)
                for s in range(2):
                    nc.vector.tensor_scalar(amaxc[k][:, s:s + 1], amax[k][:, s:s + 1], rms[k][:, s:s + 1], 1e-5,
                                            ALU.mult, ALU.max).then_inc(F[f"amaxc{k + 1}"], 1)
                dve.wait_ge(F[f"amaxc{k + 1}"], 2 * call + 2)
                nc.vector.reciprocal(arec[k][:, :], amaxc[k][:, :]).then_inc(F[f"arec{k + 1}"], 1)
                nc.vector.tensor_scalar(dscale[k][:, :], amaxc[k][:, :], w127[0:R, k:k + 1], None, ALU.mult
                                        ).then_inc(F[f"small{k + 1}"], 1)
                dve.wait_ge(F[f"arec{k + 1}"], call + 1)
                nc.vector.scalar_tensor_tensor(qscale[k][:, :], arec[k][:, :], 127.0, rms[k][:, :], ALU.mult, ALU.mult
                                               ).then_inc(F[f"small{k + 1}"], 1)

            def rows_scaled(call):
                dve.wait_ge(L2["y"], L2["y before"] + 2 * call + 2)
                nc.vector.tensor_tensor(xn[:, :, :], yn[:, :, :], g_in[:, :].unsqueeze(1).to_broadcast([R, 2, D]),
                                        ALU.mult).then_inc(F["xn"], 1)
                dve.wait_ge(F["xn"], call + 1)
                largest(0, call, xn[:, :, :])

            def rows_integer(call):
                dve.wait_ge(F["t1"], 2 * call + 2)
                dve.wait_ge(F["tr1"], 2 * call)
                nc.vector.tensor_scalar(q1[:, :, 0:D], t1[:, :, :], MAGIC, 127.0, ALU.subtract, ALU.min
                                        ).then_inc(F["q1"], 1)

            def gated(j):
                dve.wait_ge(F["ssq2"], 2 * j)
                for s in range(2):
                    dve.wait_ge(F["sg"], 2 * j + s + 1)
                    nc.vector.scalar_tensor_tensor(z[:, s, :], ps[0:R, 2 + 2 * s, :], dscale[0][:, s:s + 1], sg[:, s, :],
                                                   ALU.mult, ALU.mult).then_inc(F["z"], 1)

            def first_rows1():
                ln_vector(dve, L3, 0)
                dve.wait_ge(L3["y"], L3["y before"] + 2)
                split_vector(dve, L3, 0, yn)

            def ffn_vector(i, ahead):
                dve.wait_ge(F["z"], 2 * i + 2)
                nc.vector.tensor_tensor(zn[:, :, :], z[:, :, :], g_out[:, :].unsqueeze(1).to_broadcast([R, 2, HF]),
                                        ALU.mult).then_inc(F["zn"], 1)
                dve.wait_ge(F["zn"], i + 1)
                largest(1, i, zn[:, :, :])
                if ahead:
                    ln_stats(dve, L2, i + 2)
                scales(1, i)
                if ahead:
                    ln_apply(dve, L2, i + 2)
                    gated(i + 1)
                dve.wait_ge(F["t2"], 2 * i + 2)
                dve.wait_ge(F["tr2"], 2 * i)
                nc.vector.tensor_scalar(q2[:, :, :], t2[:, :, :], MAGIC, 127.0, ALU.subtract, ALU.min
                                        ).then_inc(F["q2"], 1)
                if ahead:
                    rows_scaled(i + 2)
                    scales(0, i + 2)
                    rows_integer(i + 2)
                else:
                    first_rows1()
                for s in range(2):
                    dve.wait_ge(F["down"], 2 * i + s + 1)
                    nc.vector.scalar_tensor_tensor(h[:, 2 * i + s, :], ps[0:R, s, 0:D], dscale[1][:, s:s + 1],
                                                   h[:, 2 * i + s, :], ALU.mult, ALU.add).then_inc(F["resid"], 1)

            for n in range(2):
                if n == 1:
                    ln_vector(dve, L2, n)
                rows_scaled(n)
                if n == 1:
                    gated(0)
                scales(0, n)
                rows_integer(n)
            with dve.Fori(0, PAIRS - 1) as i:
                ffn_vector(i, True)
            ffn_vector(PAIRS - 1, False)
            dve.wait_ge(F["resid"], TILES)


            dve.wait_ge(A1["const_in"], A1["const_in before"] + 144)
            dve.wait_ge(A1["clear"], A1["clear before"] + 3)

            def transposed_vector(L, A, j, bank=6):
                dve.wait_ge(L["tr"], L["tr before"] + 2 * j + 1)
                dve.wait_ge(A["v"], A["v before"] + 2 * j)
                nc.vector.tensor_copy(xT[:, :, 0:R], ps[:, bank, 0:3 * R].rearrange("p (c r) -> p c r", c=3)
                                      ).then_inc(A["tr_dve"], 1)

            def queries(A, j, g, table):
                dve.wait_ge(A["q"], A["q before"] + 3 * j + g + 1)
                nc.vector.tensor_tensor(Qz1[:, :, 4 * g:4 * g + 4, :],
                                        ps[:, g, 0:R2].rearrange("p (s r) -> p s r", s=2).unsqueeze(2)
                                        .to_broadcast([128, 2, 4, R]), table, ALU.mult).then_inc(A["qz"], 1)

            def normalise(A, i, least, tiles=(0, 1)):
                heads = [ps[0:R, 6 + s, 0:NH * (HE + 1)].rearrange("p (n e) -> p n e", n=NH) for s in range(2)]
                dve.wait_ge(A["ot"], A["ot before"] + 2 * i)
                for s in tiles:
                    dve.wait_ge(A["pv"], A["pv before"] + 2 * i + s + 1)
                    if least:
                        nc.vector.tensor_scalar(den[:, s, :], heads[s][:, :, HE], least, None, ALU.max
                                                ).then_inc(A["den"], 1)
                        dve.wait_ge(A["den"], A["den before"] + 2 * i + s + 1)
                        nc.vector.reciprocal(rden[:, s, :], den[:, s, :]).then_inc(A["rec"], 1)
                    else:
                        nc.vector.reciprocal(rden[:, s, :], heads[s][:, :, HE]).then_inc(A["rec"], 1)
                    dve.wait_ge(A["rec"], A["rec before"] + 2 * i + s + 1)
                    nc.vector.tensor_tensor(O1[:, s, 0:D].rearrange("p (n e) -> p n e", n=NH), heads[s][:, :, 0:HE],
                                            rden[:, s, :].unsqueeze(2).to_broadcast([R, NH, HE]), ALU.mult
                                            ).then_inc(A["o"], 1)

            def residual(A, i, stream):
                for s in range(2):
                    dve.wait_ge(A["op"], A["op before"] + 2 * i + s + 1)
                    nc.vector.tensor_tensor(stream[:, 2 * i + s, :], ps[0:R, 6 + s, 256:256 + D],
                                            stream[:, 2 * i + s, :], ALU.add).then_inc(A["resid"], 1)

            def queries_keys_vector(j):
                dve.wait_ge(A1["s"], A1["s before"] + 6 * j)
                dve.wait_ge(A1["kt"], A1["kt before"] + 3 * j)
                for g in range(3):
                    queries(A1, j, g, rope_q[:, :, :].unsqueeze(1).to_broadcast([128, 2, 4, R]))
                    dve.wait_ge(A1["k"], A1["k before"] + 3 * j + g + 1)
                    for part, dst in ((0, kc), (1, ks)):
                        nc.vector.tensor_tensor(dst[:, g, :], ps[:, 3 + g, part * R2:(part + 1) * R2],
                                                rope_k[:, part, :], ALU.mult).then_inc(A1["ks"], 1)

            def own_scores(j, s):
                scores = ps[0:R, 3 * s:3 * s + 3, :].rearrange("p b (n c) -> p (b n) c", n=4)
                mine = own[:, s, :].rearrange("p (n q) -> p n q", n=NH)
                for m in range(1, IPT):
                    dve.wait_ge(A1["own0"], A1["own0 before"] + 2 * j + s + 1)
                    if m == 2:
                        dve.wait_ge(A1["own"], A1["own before"] + 4 * j + 2 * s + 1)
                    nc.vector.scalar_tensor_tensor(mine, scores[:, :, m * S:(m + 1) * S], image[:, m:m + 1],
                                                   mine, ALU.mult, ALU.add).then_inc(A1["own"], 1)

            def reciprocals(i, s):
                dve.wait_ge(A1["own"], A1["own before"] + 4 * i + 2 * s + 2)
                nc.vector.reciprocal(rown[:, s, :], own[:, s, :]).then_inc(A1["rown"], 1)

            def weights_vector(i, s):
                dve.wait_ge(A1["rown"], A1["rown before"] + 2 * i + s + 1)
                dve.wait_ge(A1["gel"], A1["gel before"] + 2 * i + s + 1)
                dve.wait_ge(A1["pt"], A1["pt before"] + 2 * i)
                nc.vector.tensor_tensor(wt1[:, s, :], gel[:, s, :], rown[:, s, :], ALU.mult
                                        ).then_inc(A1["wt"], 1)

            def rows_once(j):
                ln_vector(dve, L4, j, dst=x1, count=2 * j)

            def rows_again(j):
                dve.wait_ge(L4["y"], L4["y before"] + 4 * j + 2)
                nc.vector.memset(after_stats[0:1, :], 0.0)
                ln_affine(dve, L4, j, x1, gains[:, 0, :], gains[:, 1, :], count=2 * j + 1)

            def split_rows(j):
                dve.wait_ge(L4["affine"], L4["affine before"] + 2 * j + 2)
                split_vector(dve, L4, j, yn2)

            def attention1_vector(i, ahead):
                weights_vector(i, 0)
                if ahead:
                    ln_stats(dve, L3, i + 2)
                reciprocals(i, 1)
                weights_vector(i, 1)
                if ahead:
                    queries_keys_vector(i + 1)
                    ln_apply(dve, L3, i + 2)
                    dve.wait_ge(L3["y"], L3["y before"] + 2 * i + 6)
                    split_vector(dve, L3, i + 2, yn)
                least = 1e-6 / (2.0 * float(HE) ** 0.5 / 2.0 ** 0.5)
                normalise(A1, i, least, (0,))
                if ahead:
                    own_scores(i + 1, 0)
                normalise(A1, i, least, (1,))
                if ahead:
                    reciprocals(i + 1, 0)
                    own_scores(i + 1, 1)
                else:
                    rows_once(0)
                    rows_again(0)
                    split_rows(0)
                residual(A1, i, h)

            ln_stats(dve, L3, 1)
            ln_apply(dve, L3, 1)
            dve.wait_ge(L3["y"], L3["y before"] + 4)
            split_vector(dve, L3, 1, yn)
            queries_keys_vector(0)
            for s in range(2):
                own_scores(0, s)
            reciprocals(0, 0)
            with dve.Fori(0, PAIRS - 1) as i:
                attention1_vector(i, True)
            attention1_vector(PAIRS - 1, False)
            dve.wait_ge(A1["resid"], A1["resid before"] + TILES)
            def transposed_both(j):
                transposed_vector(L4, A2, j)
                dve.wait_ge(L4["tr"], L4["tr before"] + 2 * j + 2)
                nc.vector.tensor_copy(xT[:, :, R:R2], ps[:, 7, 0:3 * R].rearrange("p (c r) -> p c r", c=3)
                                      ).then_inc(A2["tr_act"], 1)

            def queries_vector(j):
                dve.wait_ge(A2["s"], A2["s before"] + 2 * j)
                for g in range(3):
                    queries(A2, j, g, quarter[:, :].unsqueeze(1).unsqueeze(3).to_broadcast([128, 2, 4, R]))

            def maximum(j, s):
                dve.wait_ge(A2["s"], A2["s before"] + 2 * j + s + 1)
                scores = ps[0:R, 3 * s:3 * s + 3, 0:4 * R].rearrange("p b (n r) -> p b n r", n=4)
                nc.vector.tensor_reduce(peak[:, s, :], scores, AX.X, ALU.max).then_inc(A2["peak"], 1)

            def less_maximum(j, s):
                scores = ps[0:R, 3 * s:3 * s + 3, 0:4 * R].rearrange("p b (n r) -> p b n r", n=4)
                dve.wait_ge(A2["peak"], A2["peak before"] + 2 * j + s + 1)
                dve.wait_ge(A2["turned"], A2["turned before"] + 6 * j)
                for b in range(3):
                    nc.vector.tensor_tensor(prob[:, s, b * 4 * R:(b + 1) * 4 * R].rearrange("p (n r) -> p n r", n=4),
                                            scores[:, b, :, :],
                                            peak[:, s, 4 * b:4 * b + 4].unsqueeze(2).to_broadcast([R, 4, R]),
                                            ALU.subtract).then_inc(A2["less"], 1)

            def attention2_vector(i, ahead):
                if ahead:
                    ln_stats(dve, L4, i + 2, count=2 * i + 4)
                    transposed_both(i + 1)
                    ln_apply(dve, L4, i + 2, dst=x1, count=2 * i + 4)
                    queries_vector(i + 1)
                    rows_again(i + 2)
                    split_rows(i + 2)
                normalise(A2, i, None, (0,))
                if ahead:
                    maximum(i + 1, 0)
                    less_maximum(i + 1, 0)
                normalise(A2, i, None, (1,))
                if ahead:
                    maximum(i + 1, 1)
                if not ahead:
                    ln_affine(dve, L5, 0, x1, gains[:, 2, :], gains[:, 3, :])
                    dve.wait_ge(L5["affine"], L5["affine before"] + 2)
                    split_vector(dve, L5, 0, yn2)
                residual(A2, i, x1)
                if ahead:
                    less_maximum(i + 1, 1)

            transposed_both(0)
            rows_once(1)
            rows_again(1)
            split_rows(1)
            queries_vector(0)
            for s in range(2):
                maximum(0, s)
                less_maximum(0, s)
            with dve.Fori(0, PAIRS - 1) as i:
                attention2_vector(i, True)
            attention2_vector(PAIRS - 1, False)
            dve.wait_ge(A2["resid"], A2["resid before"] + TILES)
            nc.vector.tensor_copy(router_h[:, :, :], router_in[:, :, :]).then_inc(RT["hi"], 1)
            dve.wait_ge(RT["hi"], 1)
            nc.vector.tensor_tensor(router_l[:, :, :], router_in[:, :, :], router_h[:, :, :].bitcast(F32), ALU.subtract
                                    ).then_inc(RT["split"], 1)

            with dve.Fori(0, PAIRS) as i:
                ln_affine(dve, L5, i + 1, x1, gains[:, 2, :], gains[:, 3, :])
                dve.wait_ge(L5["affine"], L5["affine before"] + 2 * i + 4)
                split_vector(dve, L5, i + 1, yn2)
            dve.wait_ge(RT["raw"], TILES)
            step = 0
            wide = [R, TILES, E]
            for n in range(2):
                row = logits[:, n, :, :]
                nc.vector.tensor_reduce(best[:, n, :], row, AX.X, ALU.max).then_inc(RT["pick"], 1)
                dve.wait_ge(RT["pick"], step + 1)
                nc.vector.tensor_tensor(rank[:, :, :], row, best[:, n, :].unsqueeze(2).to_broadcast(wide),
                                        ALU.is_equal).then_inc(RT["pick"], 1)
                dve.wait_ge(RT["pick"], step + 2)
                nc.vector.tensor_tensor(rank[:, :, :], rank[:, :, :], ranks[:, :].unsqueeze(1).to_broadcast(wide),
                                        ALU.mult).then_inc(RT["pick"], 1)
                dve.wait_ge(RT["pick"], step + 3)
                nc.vector.tensor_reduce(best_rank[:, n, :], rank[:, :, :], AX.X, ALU.max).then_inc(RT["pick"], 1)
                dve.wait_ge(RT["pick"], step + 4)
                nc.vector.tensor_tensor(share[:, n, :, :], rank[:, :, :],
                                        best_rank[:, n, :].unsqueeze(2).to_broadcast(wide), ALU.is_equal
                                        ).then_inc(RT["pick"], 1)
                dve.wait_ge(RT["pick"], step + 5)
                if n == 0:
                    nc.vector.scalar_tensor_tensor(logits[:, 1, :, :].rearrange("p t e -> p (t e)"),
                                                   share[:, 0, :, :].rearrange("p t e -> p (t e)"), -3.0e38,
                                                   row.rearrange("p t e -> p (t e)"), ALU.mult, ALU.add
                                                   ).then_inc(RT["pick"], 1)
                    dve.wait_ge(RT["pick"], step + 6)
                step += 6
            nc.vector.tensor_tensor(pr[:, 0, :], best[:, 1, :], best[:, 0, :], ALU.subtract).then_inc(RT["k2"], 1)
            dve.wait_ge(RT["ex"], 1)
            nc.vector.tensor_scalar(pr[:, 2, :], pr[:, 1, :], 1.0, None, ALU.add).then_inc(RT["share"], 1)
            dve.wait_ge(RT["share"], 1)
            nc.vector.reciprocal(pr[:, 3, :], pr[:, 2, :]).then_inc(RT["share"], 1)
            dve.wait_ge(RT["share"], 2)
            nc.vector.tensor_tensor(pr[:, 0, :], pr[:, 1, :], pr[:, 3, :], ALU.mult).then_inc(RT["share"], 1)
            dve.wait_ge(RT["share"], 3)
            for n, p in enumerate((3, 0)):
                nc.vector.tensor_tensor(share[:, n, :, :], share[:, n, :, :], pr[:, p, :].unsqueeze(2).to_broadcast(wide),
                                        ALU.mult).then_inc(RT["share"], 1)
            dve.wait_ge(RT["share"], 5)
            nc.vector.tensor_tensor(we[:, :, :].rearrange("p e t -> p t e"), share[:, 0, :, :], share[:, 1, :, :],
                                    ALU.add).then_inc(RT["share"], 1)
            dve.wait_ge(RT["share"], 6)

            def experts_vector(e, q, c, tiles, part, ahead):
                base = 36 * e + 6 * c
                for m in range(FM):
                    dve.wait_ge(EX["gelu"], base + m + 1)
                    if m == 0:
                        dve.wait_ge(EX["down"], TILES * e + 4 * c)
                    nc.vector.tensor_copy(gh[:, m, 0:tiles * R], graw[:, m % 2, 0:tiles * R]).then_inc(EX["gh"], 1)
                    dve.wait_ge(EX["gh"], base + m + 1)
                    nc.vector.tensor_tensor(gl[:, m, 0:tiles * R], graw[:, m % 2, 0:tiles * R],
                                            gh[:, m, 0:tiles * R].bitcast(F32), ALU.subtract).then_inc(EX["gl"], 1)
                if ahead:
                    part(1 - q)
                dve.wait_ge(EX["acc"], TILES * e)
                for tt in range(tiles):
                    dve.wait_ge(EX["down"], TILES * e + 4 * c + tt + 1)
                    row = h[:, 4 * c + tt, :]
                    nc.vector.scalar_tensor_tensor(row, ps[0:R, 4 + tt, 0:D], we[:, e, bass.ds(4 * c + tt, 1)], row,
                                                   ALU.mult, ALU.add).then_inc(EX["acc"], 1)

            def sixth(e, n):
                def split(q):
                    n1, n2 = 2 * FF // 6, FM * D // 6
                    both = []
                    for src, hi, lo, size in ((est1, eh1[q], el1[q], n1), (est2, eh2[q], el2[q], n2)):
                        cols = bass.ds(n * size, size)
                        both.append((src[:, cols], hi[:, :, :].rearrange("p k n -> p (k n)")[:, cols],
                                     lo[:, :, :].rearrange("p k n -> p (k n)")[:, cols]))
                    dve.wait_ge(EX["in1"], 16 * e + 16)
                    dve.wait_ge(EX["in2"], 16 * e + 16)
                    for src, hi, lo in both:
                        nc.vector.tensor_copy(hi, src).then_inc(EX["hi"], 1)
                    for m, (src, hi, lo) in enumerate(both):
                        dve.wait_ge(EX["hi"], 12 * e + 2 * n + m + 1)
                        nc.vector.tensor_tensor(lo, src, hi.bitcast(F32), ALU.subtract).then_inc(EX["lo"], 1)
                return split

            dve.wait_ge(RT["streams"], PAIRS)

            def expert(e, q, ahead):
                with dve.Fori(0, TILES // E_CHUNK) as c:
                    experts_vector(e, q, c, E_CHUNK, sixth(e + 1, c), ahead)
                last = TILES // E_CHUNK
                experts_vector(e, q, last, TILES % E_CHUNK, sixth(e + 1, last), ahead)

            with dve.Fori(0, E // 2 - 1) as pair:
                expert(2 * pair, 0, True)
                expert(2 * pair + 1, 1, True)
            expert(E - 2, 0, True)
            expert(E - 1, 1, False)


def k192(w):
    return np.ascontiguousarray(np.stack([w[0:K0], np.concatenate([w[K0:D], w[K0:D]])], axis=1))


def constants():
    f = np.float32
    tok = np.arange(R)
    pos, img = tok % S, tok // S
    cols = np.zeros((MK, R), f)
    cols[M_CAUSAL + pos, tok] = 1
    cols[M_IMAGE + img, tok] = 1
    later = np.where(np.arange(S)[:, None] > pos[None, :], BIG, 0).astype(f)
    other = np.where(np.arange(IPT)[:, None] != img[None, :], BIG, 0).astype(f)
    full = np.zeros((2, MK, R), f)
    full[0, M_CAUSAL:M_IMAGE] = later
    full[:, M_IMAGE:] = other
    masks = np.concatenate([full[0], full[1], np.tile(cols, (1, 4))], axis=1)
    freq = (1.0 / 10000.0 ** (np.arange(HE // 2, dtype=f) / f(HE // 2))).astype(f)
    angle = pos[None, :].astype(f) * np.repeat(freq, 2)[:, None]
    cos, sin = np.cos(angle).astype(f), np.sin(angle).astype(f)
    sin[0::2] *= -1
    row = np.arange(128)
    e, half, head = row % HE, row // HE % 2, row // (2 * HE)
    table = np.where(half[:, None] == 0, cos[e], sin[e])
    mine = (head[:, None] == np.arange(4)).astype(f)
    rope_q = table[:, None, :] * mine[:, :, None]
    rope_k = np.stack([np.tile(cos[e], (1, 2)), np.tile(sin[e], (1, 2))], axis=1)
    same = img[:, None] == img[None, :]
    causal = (same & (pos[:, None] <= pos[None, :])).astype(f)
    image = (img[:, None] == np.arange(IPT)).astype(f)
    ranks = np.tile(E - np.arange(E, dtype=f), (R, 1))
    return {"rope_q": rope_q.astype(f), "rope_k": rope_k.astype(f), "causal": causal, "image": image, "quarter": mine,
            "ranks": ranks, "ident": np.eye(128, dtype=f), "masks": masks}


def lay_out(i):
    a = constants()
    a["x"] = np.ascontiguousarray(i["x"].reshape(B, C_IN, GRID, 2, PATCH // 2, GRID, PATCH)
                                  .transpose(0, 2, 1, 3, 5, 4, 6).reshape(B * GRID, C_IN * PW))
    a["wtok"] = np.ascontiguousarray(i["L0_tok_W"].reshape(NK, 128, D).transpose(1, 0, 2))
    near = np.arange(GRID) * 14 // GRID
    pos = i["L0_tok_positions"][0][:, near][:, :, near].reshape(D, GRID * GRID).T
    a["pos"] = np.ascontiguousarray(np.tile(np.concatenate([i["L0_tok_cls_embedding"][0], pos]), (IPT, 1)))
    a["tok_b"] = i["L0_tok_b"].reshape(1, D)
    qkv = [i[f"L0_attn_W_{c}"].transpose(1, 0, 2).reshape(D, NH * HD) for c in "QKV"]
    a["w1"] = k192(np.concatenate(qkv, axis=1))
    a["b_qk"] = np.ascontiguousarray(np.concatenate(
        [i["L0_attn_b_Q"].reshape(6, 128).T, i["L0_attn_b_K"].reshape(6, 128).T], axis=1))
    a["b_v"] = i["L0_attn_b_V"].reshape(1, NH * HD)
    a["b_o"] = i["L0_attn_b_O"].reshape(1, D)
    a["wo1"] = np.ascontiguousarray(i["L0_attn_W_O"].reshape(6, 128, D).transpose(1, 0, 2))
    win = np.zeros((256, 2 * HF), np.float32)
    win[0:D] = i["L0_ffn_w_in"].T
    a["win"] = np.ascontiguousarray(win.reshape(2, 128, 2 * HF).transpose(1, 0, 2))
    a["wout"] = np.ascontiguousarray(i["L0_ffn_w_out"].T.reshape(4, 128, D).transpose(1, 0, 2))
    a["g_in"] = i["L0_ffn_g_in"].reshape(1, D)
    a["g_out"] = i["L0_ffn_g_out"].reshape(1, HF)
    def heads(w, other):
        out = np.zeros((D, NH, 2, HE), np.float32)
        out[:, :, 0] = w.reshape(D, NH, HE)
        if other is not None:
            out[:, :, 1] = other.reshape(D, NH, HE)
        return out.reshape(D, NH * 2 * HE)

    def swapped(w):
        return w.reshape(D, NH, HE // 2, 2)[:, :, :, ::-1].reshape(D, D)

    q, k, v = (i[f"L1_attn_W{c}"].T for c in "qkv")
    q4, k4, v4 = (i["L1_ffn_Wqkv"][:, c * D:(c + 1) * D] for c in range(3))
    both = np.concatenate([heads(q, swapped(q)), heads(k, k), heads(swapped(k), swapped(k)), v,
                           heads(q4, None), heads(k4, None), v4, np.zeros((D, WPAD - WCOLS), np.float32)], axis=1)
    a["w3"] = k192(both)
    w, gap = [], 128
    for m in (i["L1_attn_Wproj"].T, i["L1_ffn_Wproj"]):
        padded = np.zeros((256, D), np.float32)
        padded[0:D] = m
        w.append(padded.reshape(2, 128, D).transpose(1, 0, 2))
    a["proj"] = np.ascontiguousarray(np.stack(w, axis=1))
    a["gains"] = np.stack([i[f"L1_ffn_ln{n}_{x}"] for n in (1, 2) for x in "gb"])[None]
    a["router"] = k192(i["L1_ffn_Wrouter"])
    a["moe1"] = np.stack([k192(m).reshape(128, 2 * FF) for m in i["L1_ffn_W1"]])
    a["moe2"] = np.ascontiguousarray(i["L1_ffn_W2"].reshape(E, FM, 128, D).transpose(0, 2, 1, 3)).reshape(E, 128, FM * D)
    return a


def kernel(**inputs):
    import numpy as _np
    import concourse.bacc as _bacc
    from concourse import mybir as _mybir
    from concourse.bass_utils import run_bass_kernel_spmd as _run

    nc = _bacc.Bacc("TRN2", target_bir_lowering=False, num_devices=1)
    arrays, tensors = {}, {}
    for name, a in lay_out({n: _np.asarray(v) for n, v in inputs.items()}).items():
        a = _np.ascontiguousarray(a)
        arrays[f"in_{name}_dram"] = a
        tensors[name] = nc.dram_tensor(f"in_{name}_dram", a.shape, _mybir.dt.from_np(a.dtype),
                                       kind="ExternalInput").ap()
    tensors["out"] = nc.dram_tensor("out_0_dram", (B, S, D), _mybir.dt.float32, kind="ExternalOutput").ap()
    build_program(nc, tensors)
    r = _run(nc, [arrays], core_ids=[0])
    return r.results[0]["out_0_dram"]
```
